# Optimizing a Trainium2 kernel written in Bass

```python
import numpy as np
import jax
import jax.numpy as jnp

def _softmax(x, axis=-1):
    return jax.nn.softmax(x, axis=axis)

def _gelu(x):
    return jax.nn.gelu(x, approximate=True)

def _silu(x):
    return jax.nn.silu(x)

def _sigmoid(x):
    return jax.nn.sigmoid(x)

def _layernorm(x, axis=-1, eps=1e-05):
    m = jnp.mean(x, axis=axis, keepdims=True)
    v = jnp.var(x, axis=axis, keepdims=True)
    return (x - m) / jnp.sqrt(v + eps)

def _scatter_add(tgt, idx, src, axis=0):
    return tgt.at[idx].add(src)

def _segment_sum(src, seg, n):
    return jax.ops.segment_sum(src, seg, n)
kernel_name = 'mk_decoder_preln_d1_seqx_r4_a1b0ee'

def setup_inputs(seed: int=0):
    np.random.seed(seed)
    _w = jnp.asarray

    def _rec_inputs():
        import jax
        import jax.numpy as jnp
        _rk = jax.random.key(seed)
        x = 7.22e-05 + 1 * jax.random.normal(jax.random.fold_in(_rk, 1), (4, 1024, 256), jnp.float32)
        _lenS = 1024 - jax.random.randint(jax.random.fold_in(_rk, 7), (4,), 0, max(1, 1024 // 4) + 1, jnp.int32)
        _lenS2 = 64 - jax.random.randint(jax.random.fold_in(_rk, 8), (4,), 0, max(1, 64 // 4) + 1, jnp.int32)
        _ctx_1024P = jax.random.normal(jax.random.fold_in(_rk, 11), (4, 16, 256), jnp.float32)
        _ctx_1024c = jax.random.dirichlet(jax.random.fold_in(_rk, 511), 0.3 * jnp.ones((16,), jnp.float32), (4, 64))
        _ctx_1024t = jnp.einsum('bsk,bkd->bsd', _ctx_1024c, _ctx_1024P)
        _ctx_1024t = _ctx_1024t * jax.lax.rsqrt(jnp.mean(jnp.square(_ctx_1024t)) + 1e-12) * 0.953939
        ctx_1024 = -1.39393e-06 + 0.999914 * (_ctx_1024t + 0.3 * jax.random.normal(jax.random.fold_in(_rk, 611), (4, 64, 256), jnp.float32))
        return (x, ctx_1024)
    x, ctx_1024 = _rec_inputs()

    def _L0_attn_setup():
        import jax, jax.numpy as jnp
        import numpy as np
        B, L, D_MODEL = (2, 512, 256)
        D_STATE, D_CONV, EXPAND = (8, 4, 2)
        D_INNER = EXPAND * D_MODEL
        DT_RANK = (D_MODEL + 15) // 16
        key = jax.random.key(seed)
        ks = jax.random.split(key, 8)
        s = 0.02
        x = jax.random.normal(ks[0], (B, L, D_MODEL), dtype=jnp.float32)
        W_in = jax.random.normal(ks[1], (D_MODEL, 2 * D_INNER), dtype=jnp.float32) * s
        dw_kernel = jax.random.normal(ks[2], (D_CONV, D_INNER), dtype=jnp.float32) * s
        pw_kernel = jax.random.normal(ks[3], (D_INNER, D_INNER), dtype=jnp.float32) * s
        conv_bias = jnp.zeros((D_INNER,), dtype=jnp.float32)
        W_x = jax.random.normal(ks[4], (D_INNER, DT_RANK + 2 * D_STATE), dtype=jnp.float32) * s
        W_dt = jax.random.normal(ks[5], (DT_RANK, D_INNER), dtype=jnp.float32) * s
        b_dt = jnp.zeros((D_INNER,), dtype=jnp.float32)
        A_init = np.repeat(np.arange(1, D_STATE + 1, dtype=np.float32), D_INNER).reshape(D_INNER, D_STATE)
        A_log = jnp.asarray(np.log(A_init))
        D = jnp.ones((D_INNER,), dtype=jnp.float32)
        W_out = jax.random.normal(ks[6], (D_INNER, D_MODEL), dtype=jnp.float32) * s
        return {'x': x, 'W_in': W_in, 'dw_kernel': dw_kernel, 'pw_kernel': pw_kernel, 'conv_bias': conv_bias, 'W_x': W_x, 'W_dt': W_dt, 'b_dt': b_dt, 'A_log': A_log, 'D': D, 'W_out': W_out}
    _L0_attn_all = _L0_attn_setup()
    _L0_attn_in = {k: v for k, v in _L0_attn_all.items() if k in ('W_in', 'dw_kernel', 'pw_kernel', 'conv_bias', 'W_x', 'W_dt', 'b_dt', 'A_log', 'D', 'W_out')}
    del _L0_attn_all

    def _L0_xattn_setup():
        import jax, jax.numpy as jnp
        import numpy as np
        HEADS = 16
        DIM_HEAD = 64
        QUERY_DIM = 256
        CONTEXT_DIM = 256
        D_ATTN = HEADS * DIM_HEAD
        SCALE = DIM_HEAD ** (-0.5)
        key = jax.random.key(seed)
        ks = jax.random.split(key, 7)
        B, N, M = (4, 512, 256)
        x = jax.random.normal(ks[0], (B, N, QUERY_DIM), dtype=jnp.float32)
        context = jax.random.normal(ks[1], (B, M, CONTEXT_DIM), dtype=jnp.float32)
        s = 0.02
        Wq = jax.random.normal(ks[2], (QUERY_DIM, D_ATTN), dtype=jnp.float32) * s
        Wk = jax.random.normal(ks[3], (CONTEXT_DIM, D_ATTN), dtype=jnp.float32) * s
        Wv = jax.random.normal(ks[4], (CONTEXT_DIM, D_ATTN), dtype=jnp.float32) * s
        Wo = jax.random.normal(ks[5], (D_ATTN, QUERY_DIM), dtype=jnp.float32) * s
        bo = jax.random.normal(ks[6], (QUERY_DIM,), dtype=jnp.float32) * s
        return {'x': x, 'context': context, 'Wq': Wq, 'Wk': Wk, 'Wv': Wv, 'Wo': Wo, 'bo': bo}
    _L0_xattn_all = _L0_xattn_setup()
    _L0_xattn_in = {k: v for k, v in _L0_xattn_all.items() if k in ('Wq', 'Wk', 'Wv', 'Wo', 'bo')}
    del _L0_xattn_all

    def _L0_ffn_setup():
        import jax, jax.numpy as jnp
        import numpy as np
        B, S, H, F, E = (4, 512, 256, 1024, 8)
        key = jax.random.key(seed)
        ks = jax.random.split(key, 8)
        s = 1.0 / np.sqrt(H)
        sf = 1.0 / np.sqrt(F)
        return {'x': jax.random.normal(ks[0], (B, S, H), jnp.float32), 'wr': jax.random.uniform(ks[1], (H, E), jnp.float32, -s, s), 'br': jax.random.uniform(ks[2], (E,), jnp.float32, -s, s), 'w1': jax.random.uniform(ks[3], (E, H, F), jnp.float32, -s, s), 'b1': jax.random.uniform(ks[4], (E, F), jnp.float32, -s, s), 'w2': jax.random.uniform(ks[5], (E, F, H), jnp.float32, -sf, sf), 'b2': jax.random.uniform(ks[6], (E, H), jnp.float32, -sf, sf)}
    _L0_ffn_all = _L0_ffn_setup()
    _L0_ffn_in = {k: v for k, v in _L0_ffn_all.items() if k in ('wr', 'br', 'w1', 'b1', 'w2', 'b2')}
    del _L0_ffn_all
    return {'x': x, 'ctx_1024': ctx_1024, 'L0_attn_W_in': _L0_attn_in['W_in'], 'L0_attn_dw_kernel': _L0_attn_in['dw_kernel'], 'L0_attn_pw_kernel': _L0_attn_in['pw_kernel'], 'L0_attn_conv_bias': _L0_attn_in['conv_bias'], 'L0_attn_W_x': _L0_attn_in['W_x'], 'L0_attn_W_dt': _L0_attn_in['W_dt'], 'L0_attn_b_dt': _L0_attn_in['b_dt'], 'L0_attn_A_log': _L0_attn_in['A_log'], 'L0_attn_D': _L0_attn_in['D'], 'L0_attn_W_out': _L0_attn_in['W_out'], 'L0_xattn_Wq': _L0_xattn_in['Wq'], 'L0_xattn_Wk': _L0_xattn_in['Wk'], 'L0_xattn_Wv': _L0_xattn_in['Wv'], 'L0_xattn_Wo': _L0_xattn_in['Wo'], 'L0_xattn_bo': _L0_xattn_in['bo'], 'L0_ffn_wr': _L0_ffn_in['wr'], 'L0_ffn_br': _L0_ffn_in['br'], 'L0_ffn_w1': _L0_ffn_in['w1'], 'L0_ffn_b1': _L0_ffn_in['b1'], 'L0_ffn_w2': _L0_ffn_in['w2'], 'L0_ffn_b2': _L0_ffn_in['b2']}

def reference(x, ctx_1024, L0_attn_W_in, L0_attn_dw_kernel, L0_attn_pw_kernel, L0_attn_conv_bias, L0_attn_W_x, L0_attn_W_dt, L0_attn_b_dt, L0_attn_A_log, L0_attn_D, L0_attn_W_out, L0_xattn_Wq, L0_xattn_Wk, L0_xattn_Wv, L0_xattn_Wo, L0_xattn_bo, L0_ffn_wr, L0_ffn_br, L0_ffn_w1, L0_ffn_b1, L0_ffn_w2, L0_ffn_b2):
    import jax
    import jax.numpy as jnp

    def _L0_attn_ref(x, W_in, dw_kernel, pw_kernel, conv_bias, W_x, W_dt, b_dt, A_log, D, W_out):
        import jax, jax.numpy as jnp
        import numpy as np
        B, L, D_MODEL = (2, 512, 256)
        D_STATE, D_CONV, EXPAND = (8, 4, 2)
        D_INNER = EXPAND * D_MODEL
        DT_RANK = (D_MODEL + 15) // 16
        d_inner, d_state = A_log.shape
        dt_rank = W_dt.shape[0]
        d_conv = dw_kernel.shape[0]
        bsz = x.shape[0]
        xz = x @ W_in
        x_in, z = jnp.split(xz, 2, axis=-1)
        xp = jnp.pad(x_in, ((0, 0), (d_conv - 1, 0), (0, 0)))
        xc = jax.lax.conv_general_dilated(xp, dw_kernel[:, None, :], window_strides=(1,), padding='VALID', dimension_numbers=('NWC', 'WIO', 'NWC'), feature_group_count=d_inner)
        xc = jax.nn.silu(xc @ pw_kernel + conv_bias)
        x_dbl = xc @ W_x
        delta = x_dbl[..., :dt_rank]
        Bm = x_dbl[..., dt_rank:dt_rank + d_state]
        C = x_dbl[..., dt_rank + d_state:]
        delta = jax.nn.softplus(delta @ W_dt + b_dt)
        A = -jnp.exp(A_log)
        deltaA = jnp.exp(jnp.einsum('bld,dn->bldn', delta, A))
        deltaB_u = jnp.einsum('bld,bln,bld->bldn', delta, Bm, xc)

        def step(h, inp):
            dA_t, dBu_t, C_t = inp
            h = dA_t * h + dBu_t
            y_t = jnp.einsum('bn,bdn->bd', C_t, h)
            return (h, y_t)
        h0 = jnp.zeros((bsz, d_inner, d_state), dtype=x.dtype)
        elems = (deltaA.transpose(1, 0, 2, 3), deltaB_u.transpose(1, 0, 2, 3), C.transpose(1, 0, 2))
        _, ys = jax.lax.scan(step, h0, elems)
        y = ys.transpose(1, 0, 2)
        y = y + xc * D
        y = y * jax.nn.silu(z)
        return y @ W_out

    def _L0_xattn_ref(x, context, Wq, Wk, Wv, Wo, bo):
        import jax, jax.numpy as jnp
        import numpy as np
        HEADS = 16
        DIM_HEAD = 64
        QUERY_DIM = 256
        CONTEXT_DIM = 256
        D_ATTN = HEADS * DIM_HEAD
        SCALE = DIM_HEAD ** (-0.5)
        B, N, _ = x.shape
        M = context.shape[1]
        Q = (x @ Wq).reshape(B, N, HEADS, DIM_HEAD)
        K = (context @ Wk).reshape(B, M, HEADS, DIM_HEAD)
        V = (context @ Wv).reshape(B, M, HEADS, DIM_HEAD)
        scores = jnp.einsum('bqhd,bmhd->bqhm', Q, K) * SCALE
        attn = jax.nn.softmax(scores, axis=-1)
        out = jnp.einsum('bqhm,bmhd->bqhd', attn, V)
        out = out.reshape(B, N, D_ATTN)
        return out @ Wo + bo

    def _L0_ffn_ref(x, wr, br, w1, b1, w2, b2):
        import jax, jax.numpy as jnp
        import numpy as np
        B, S, H, F, E = (4, 512, 256, 1024, 8)
        scores = jnp.einsum('bsh,he->bse', x, wr) + br
        expert_id = jnp.argmax(scores, axis=-1)
        h = jnp.einsum('bsh,ehf->ebsf', x, w1) + b1[:, None, None, :]
        h = jax.nn.gelu(h, approximate=False)
        y = jnp.einsum('ebsf,efh->ebsh', h, w2) + b2[:, None, None, :]
        one_hot = jax.nn.one_hot(expert_id, E, dtype=x.dtype)
        out = jnp.einsum('ebsh,bse->bsh', y, one_hot)
        return out
    x = x + _L0_attn_ref(_layernorm(x, axis=-1), L0_attn_W_in, L0_attn_dw_kernel, L0_attn_pw_kernel, L0_attn_conv_bias, L0_attn_W_x, L0_attn_W_dt, L0_attn_b_dt, L0_attn_A_log, L0_attn_D, L0_attn_W_out)
    x = x + _L0_xattn_ref(_layernorm(x, axis=-1), ctx_1024, L0_xattn_Wq, L0_xattn_Wk, L0_xattn_Wv, L0_xattn_Wo, L0_xattn_bo)
    x = x + _L0_ffn_ref(_layernorm(x, axis=-1), L0_ffn_wr, L0_ffn_br, L0_ffn_w1, L0_ffn_b1, L0_ffn_w2, L0_ffn_b2)
    return x

_drawn_inputs = setup_inputs


def setup_inputs(seed=0):
    import zlib

    import numpy as np

    out = dict(_drawn_inputs(seed))
    spreads = {'L0_attn_conv_bias': (0.0, 0.465), 'L0_attn_b_dt': (0.0, 0.8), 'L0_attn_D': (1.0, 0.6)}
    factors = {'L0_attn_W_in': 4.188,
     'L0_attn_dw_kernel': 8.0,
     'L0_attn_pw_kernel': 8.0,
     'L0_attn_W_x': 8.0,
     'L0_attn_W_dt': 8.0,
     'L0_attn_A_log': 8.0,
     'L0_attn_W_out': 4.291,
     'L0_xattn_Wq': 40.504,
     'L0_xattn_Wk': 30.384,
     'L0_ffn_b1': 35.928,
     'L0_ffn_b2': 25.264,
     'ctx_1024': 8.0,
     'L0_xattn_Wv': 8.0,
     'L0_xattn_Wo': 8.0,
     'L0_xattn_bo': 8.0,
     'L0_ffn_wr': 8.0,
     'L0_ffn_br': 8.0,
     'L0_ffn_w1': 8.0,
     'L0_ffn_w2': 8.0}
    for name, (base, spread) in spreads.items():
        noise = np.random.default_rng([zlib.crc32(name.encode()), seed]).standard_normal(out[name].shape)
        drawn = base * np.exp(spread * noise) if base else spread * noise
        out[name] = jnp.asarray(drawn.astype(out[name].dtype))
    for name, factor in factors.items():
        out[name] = (out[name] * factor).astype(out[name].dtype)
    return out
```

```python
import concourse.bass as bass
from concourse import mybir
from contextlib import ExitStack

F32 = mybir.dt.float32
I32 = mybir.dt.int32
U32 = mybir.dt.uint32
ALU = mybir.AluOpType
ACT = mybir.ActivationFunctionType
AX = mybir.AxisListType

P = 128
B, S, D = 4, 1024, 256
DI, NS, KC, R = 512, 8, 4, 16
H, DH, M = 16, 64, 64
E, F = 8, 1024
EPS = 1e-5
T = 512
NC = B * S // T
TJ = T // P
KD = D // P
MB = DI // P
HC = H * DH // P
KF = F // P
TT = B * S // P
NT = TT + E - 1
SCALE = DH ** -0.5
RING = 4
GP_ADDS = (2, 3, 4, 6)


def wait(eng, sem, value):
    if isinstance(value, int) and value <= 0:
        return
    eng.wait_ge(sem, value)


def wait_apart(eng, sem, value, passed):
    if isinstance(value, int) and value <= 0:
        return
    eng.wait_ge(sem, value)
    eng.sem_inc(passed, 1)


class Carver:
    def __init__(self, arena):
        self.arena, self.at = arena, 0

    def __call__(self, *shape):
        n = 1
        for s in shape:
            n *= s
        part = self.arena[:, self.at:self.at + n]
        self.at += n
        names = [f"d{i}" for i in range(len(shape))]
        if len(shape) == 1:
            return part
        return part.rearrange(f"p ({' '.join(names)}) -> p {' '.join(names)}",
                              **{k: v for k, v in zip(names[1:], shape[1:])})


ARENA = 34828


def decoder_layer(nc, x, ctx_in, W_in, dwk, pwk, cbias, W_x, W_dt, b_dt, A_log, D_skip, W_out,
                  Wq, Wk, Wv, Wo, bo, wr, br, w1, b1, w2, b2, out):
    x_f = x.rearrange("b s d -> (b s) d")
    x_t = x_f.rearrange("(n p) d -> p n d", p=P)
    out_t = out.rearrange("b s d -> (b s) d").rearrange("(n p) d -> p n d", p=P)

    def dram(name, shape):
        return nc.dram_tensor(name, shape, F32, kind="Internal").ap()

    g_dram = dram("g_dram", (B, P, KD * H * M))
    u_dram = dram("u_dram", (B, P, HC * D))
    bc_dram = dram("bc_dram", (2, 2 * NS, T))
    x2_dram = dram("x2_dram", (P, TT, D))
    xn3_dram = dram("xn3_dram", (P, TT, D))
    xs_dram = dram("xs_dram", (NT * P, D))
    ys_dram = dram("ys_dram", (NT * P, D))

    root = ExitStack()
    with root:
        def sem(name):
            return root.enter_context(nc.semaphore(name))

        def sb_in(stack, name, shape, dt=F32):
            return stack.enter_context(nc.sbuf_tensor(name, shape, dt))

        ident_ready = sem("ident_ready")
        passed = [sem("passed_sync"), sem("passed_gpsimd"), sem("passed_vector")]
        ident = sb_in(root, "ident", [P, P])
        eps_col = sb_in(root, "eps_col", [P, 1])
        scores_all = sb_in(root, "scores_all", [P, TT, E])
        bank = [root.enter_context(nc.psum_tensor(f"bank{i}", [P, 512], F32)) for i in range(4)]
        pair_a = root.enter_context(nc.psum_tensor("pair_a", [P, 1024], F32))
        pair_b = root.enter_context(nc.psum_tensor("pair_b", [P, 1024], F32))

        arena = sb_in(root, "arena", [P, ARENA])
        w1_in, w2_in = sem("w1_in"), sem("w2_in")
        experts = Carver(arena)
        w1_sb, w2_sb = experts(E, KD, F), experts(E, KF, D)

        def load_experts(eng):
            for e in range(E):
                eng.dma_start(w1_sb[:, e], w1[e].rearrange("(k p) f -> p k f", p=P)).then_inc(w1_in, 16)
            for e in range(E):
                eng.dma_start(w2_sb[:, e], w2[e].rearrange("(k p) d -> p k d", p=P)).then_inc(w2_in, 16)

        with ExitStack() as seq:
            weights = Weights(lambda name, shape: sb_in(seq, name, shape), sem("weights_in"))
            setup_part(nc, sem, arena, ident_ready, ident, eps_col, bank, pair_a, ctx_in,
                       Wq, Wk, Wv, Wo, g_dram, u_dram, xs_dram,
                       lambda eng: weights.load(eng, W_in, dwk, pwk, cbias, W_x, W_dt, b_dt, A_log, D_skip,
                                                W_out, bo, wr, br))
            sequence_part(nc, sem, lambda name, shape: sb_in(seq, name, shape), arena, passed, ident, eps_col,
                          scores_all, bank, pair_a, pair_b, x_t, weights, load_experts,
                          g_dram, u_dram, bc_dram, x2_dram, xn3_dram)
        expert_part(nc, sem, sb_in, passed, ident, scores_all, bank, pair_a, pair_b, w1_sb, w2_sb, w1_in, w2_in,
                    b1, b2, x2_dram, xn3_dram, xs_dram, ys_dram, out_t)


class Weights:
    LOADS = 12 + MB

    def __init__(self, sb, arrived):
        self.arrived = arrived
        self.w_in = sb("w_in", [P, KD, 2 * DI])
        self.pw = sb("pw", [P, MB, DI])
        self.w_x = sb("w_x", [P, MB, R + 2 * NS])
        self.w_dt = sb("w_dt", [R, DI])
        self.w_out = sb("w_out", [P, MB, D])
        self.taps = sb("taps", [P, MB, KC])
        self.conv_bias = sb("conv_bias", [P, MB])
        self.dt_bias = sb("dt_bias", [P, MB])
        self.d_skip = sb("d_skip", [P, MB])
        self.a_log = sb("a_log", [P, MB, NS])
        self.bo = sb("bo", [P, D])
        self.wr = sb("wr", [P, KD, E])
        self.br = sb("br", [P, E])

    def load(self, eng, W_in, dwk, pwk, cbias, W_x, W_dt, b_dt, A_log, D_skip, W_out, bo, wr, br):
        for dst, src in (
            (self.w_in, W_in.rearrange("(k p) n -> p k n", p=P)),
            (self.pw, pwk.rearrange("(k p) n -> p k n", p=P)),
            (self.w_x, W_x.rearrange("(k p) n -> p k n", p=P)),
            (self.w_dt, W_dt),
            (self.w_out, W_out.rearrange("(k p) n -> p k n", p=P)),
            (self.conv_bias, cbias.rearrange("(m p) -> p m", p=P)),
            (self.dt_bias, b_dt.rearrange("(m p) -> p m", p=P)),
            (self.d_skip, D_skip.rearrange("(m p) -> p m", p=P)),
            (self.a_log, A_log.rearrange("(m p) n -> p m n", p=P)),
            (self.bo, bo.partition_broadcast(P)),
            (self.wr, wr.rearrange("(k p) n -> p k n", p=P)),
            (self.br, br.partition_broadcast(P)),
        ):
            eng.dma_start(dst[:], src, allow_slow_non_contiguous=True).then_inc(self.arrived, 16)
        for m in range(MB):
            eng.dma_start(self.taps[:, m], dwk[:, m * P:(m + 1) * P].rearrange("k p -> p k"),
                          allow_slow_non_contiguous=True).then_inc(self.arrived, 16)


def setup_part(nc, sem, arena, ident_ready, ident, eps_col, bank, pair_a, ctx_in, Wq, Wk, Wv, Wo,
               g_dram, u_dram, xs_dram, load_weights):
    BM = B * M
    ctx_rows = ctx_in.rearrange("b m d -> (b m) d").rearrange("(k p) d -> p k d", p=P)
    part = Carver(arena)
    ctx_sb, ctxT = part(BM // P, D), part(KD, BM)
    wq_sb, wk_sb, wv_sb, wo_sb = part(KD, H * DH), part(KD, H * DH), part(KD, H * DH), part(HC, D)
    wqT = part(HC, D)
    k_diag, v_diag = part(HC, B, P), part(HC, B, P)
    g_sb, u_sb = part(2, H * M), part(2, 2 * D)
    zeros = part(D)

    ctx_in_s, wk_in, wv_in, wq_in, wo_in = (sem(n) for n in
                                           ("ctx_in", "wk_in", "wv_in", "wq_in", "wo_in"))
    ident_zero, diag_zero, pads_zero = sem("ident_zero"), sem("diag_zero"), sem("pads_zero")
    su_full, su_free = sem("su_full"), sem("su_free")
    g_full, g_evac = sem("g_full"), sem("g_evac")
    u_full, u_evac = sem("u_full"), sem("u_evac")
    g_stored = [sem("g_stored0"), sem("g_stored1")]
    u_stored = [sem("u_stored0"), sem("u_stored1")]
    zeros_stored = sem("zeros_stored")

    WQT0 = KD
    KT0 = WQT0 + HC // 2
    VT0 = KT0 + HC

    with nc.Block() as block:
        @block.sync
        def _(sp):
            sp.dma_start(ctx_sb, ctx_rows).then_inc(ctx_in_s, 16)
            sp.dma_start(wq_sb, Wq.rearrange("(k p) n -> p k n", p=P)).then_inc(wq_in, 16)
            sp.dma_start(wk_sb, Wk.rearrange("(k p) n -> p k n", p=P)).then_inc(wk_in, 16)
            sp.dma_start(wv_sb, Wv.rearrange("(k p) n -> p k n", p=P)).then_inc(wv_in, 16)
            sp.dma_start(wo_sb, Wo.rearrange("(k p) n -> p k n", p=P)).then_inc(wo_in, 16)
            for n in range(B * KD):
                sp.wait_ge(g_evac, n + 1)
                b, k = n // KD, n % KD
                sp.dma_start(g_dram[b][:, k * H * M:(k + 1) * H * M],
                             g_sb[:, n % 2]).then_inc(g_stored[n % 2], 16)
            for n in range(B * HC // 2):
                sp.wait_ge(u_evac, n + 1)
                b, c2 = n // (HC // 2), n % (HC // 2)
                sp.dma_start(u_dram[b][:, c2 * 2 * D:(c2 + 1) * 2 * D],
                             u_sb[:, n % 2]).then_inc(u_stored[n % 2], 16)
            load_weights(sp)
            sp.wait_ge(pads_zero, 1)
            for n in range(NT):
                sp.dma_start(xs_dram[n * P:(n + 1) * P, :], zeros).then_inc(zeros_stored, 16)
            sp.wait_ge(zeros_stored, 16 * NT)
            for p in range(2):
                sp.wait_ge(g_stored[p], 16 * (B * KD // 2))
                sp.wait_ge(u_stored[p], 16 * (B * HC // 4))

        @block.gpsimd
        def _(pool):
            nc.gpsimd.memset(ident[:], 0.0).then_inc(ident_zero, 1)
            pool.wait_ge(ident_zero, 1)
            nc.gpsimd.affine_select(out=ident[:], in_=ident[:], compare_op=ALU.not_equal, fill=1.0,
                                    base=0, pattern=[[-1, P]], channel_multiplier=1).then_inc(ident_ready, 1)

        @block.vector
        def _(dve):
            nc.vector.memset(zeros, 0.0).then_inc(pads_zero, 1)
            nc.vector.memset(eps_col[:], EPS)
            nc.vector.memset(k_diag, 0.0).then_inc(diag_zero, 1)
            nc.vector.memset(v_diag, 0.0).then_inc(diag_zero, 1)
            for n in range(B * KD):
                dve.wait_ge(g_full, n + 1)
                if n >= 2:
                    dve.wait_ge(g_stored[n % 2], 16 * (n // 2))
                nc.vector.tensor_copy(g_sb[:, n % 2], pair_a[:]).then_inc(g_evac, 1)

        @block.scalar
        def _(act):
            for k in range(KD):
                act.wait_ge(su_full, k + 1)
                nc.scalar.activation(ctxT[:, k], bank[k % 2][:, 0:BM], ACT.Copy).then_inc(su_free, 1)
            for i in range(HC // 2):
                act.wait_ge(su_full, WQT0 + i + 1)
                nc.scalar.activation(wqT[:, 2 * i:2 * i + 2].rearrange("p c d -> p (c d)"),
                                     bank[(WQT0 + i) % 2][:], ACT.Copy).then_inc(su_free, 1)
            act.wait_ge(diag_zero, 2)
            for which, (first, diag) in enumerate(((KT0, k_diag), (VT0, v_diag))):
                for c in range(HC):
                    act.wait_ge(su_full, first + c + 1)
                    src = bank[(first + c) % 2]
                    nc.scalar.activation(diag[0:DH, c, :, 0:M],
                                         src[0:DH, 0:BM].rearrange("p (b m) -> p b m", b=B), ACT.Copy)
                    nc.scalar.activation(diag[DH:P, c, :, M:P],
                                         src[DH:P, 0:BM].rearrange("p (b m) -> p b m", b=B),
                                         ACT.Copy).then_inc(su_free, 1)
            for n in range(B * HC // 2):
                act.wait_ge(u_full, n + 1)
                if n >= 2:
                    act.wait_ge(u_stored[n % 2], 16 * (n // 2))
                nc.scalar.activation(u_sb[:, n % 2], bank[2 + n % 2][:], ACT.Copy).then_inc(u_evac, 1)

        @block.tensor
        def _(pe):
            pe.wait_ge(ident_ready, 1)
            pe.wait_ge(ctx_in_s, 16)
            for k in range(KD):
                for t in range(BM // P):
                    last = nc.tensor.transpose(bank[k % 2][:, t * P:(t + 1) * P],
                                               ctx_sb[:, t, k * P:(k + 1) * P], ident[:])
                last.then_inc(su_full, 1)
            pe.wait_ge(wq_in, 16)
            for i in range(HC // 2):
                pe.wait_ge(su_free, WQT0 + i - 1)
                for c in range(2):
                    for k in range(KD):
                        last = nc.tensor.transpose(
                            bank[(WQT0 + i) % 2][:, (c * KD + k) * P:(c * KD + k + 1) * P],
                            wq_sb[:, k, (2 * i + c) * P:(2 * i + c + 1) * P], ident[:])
                last.then_inc(su_full, 1)
            for first, w, arrived in ((KT0, wk_sb, wk_in), (VT0, wv_sb, wv_in)):
                pe.wait_ge(arrived, 16)
                for c in range(HC):
                    pe.wait_ge(su_free, first + c - 1)
                    for k in range(KD):
                        last = nc.tensor.matmul(bank[(first + c) % 2][:, 0:BM], w[:, k, c * P:(c + 1) * P],
                                                ctxT[:, k], start=(k == 0), stop=(k == KD - 1))
                    last.then_inc(su_full, 1)
            pe.wait_ge(su_free, VT0 + HC)
            for n in range(B * KD):
                b, k = n // KD, n % KD
                if n:
                    pe.wait_ge(g_evac, n)
                for c in range(HC):
                    last = nc.tensor.matmul(pair_a[:, c * P:(c + 1) * P], wqT[:, c, k * P:(k + 1) * P],
                                            k_diag[:, c, b], start=True, stop=True)
                last.then_inc(g_full, 1)
            pe.wait_ge(wo_in, 16)
            for n in range(B * HC // 2):
                b, c2 = n // (HC // 2), n % (HC // 2)
                if n >= 2:
                    pe.wait_ge(u_evac, n - 1)
                for i in range(2):
                    c = 2 * c2 + i
                    last = nc.tensor.matmul(bank[2 + n % 2][:, i * D:(i + 1) * D], v_diag[:, c, b],
                                            wo_sb[:, c], start=True, stop=True)
                last.then_inc(u_full, 1)


def sequence_part(nc, sem, sb, arena, passed, ident, eps_col, scores_all, bank, pair_a, pair_b, x_t, weights,
                  load_experts, g_dram, u_dram, bc_dram, x2_dram, xn3_dram):
    W = weights
    a_exp = sb("a_exp", [P, MB, NS])
    a_neg = sb("a_neg", [P, MB, NS])
    g_sb = sb("g_att", [P, KD, H * M])
    u_sb = sb("u_att", [P, HC, D])
    part = Carver(arena)
    xa = part(TJ, D)
    xnT = part(2, KD, T)
    xp = part(MB, KC - 1 + T)
    cv = part(MB, T)
    delta = part(2, MB, T)
    u = part(MB, T)
    xc = part(MB, T)
    zg = part(MB, T)
    y_d = part(MB, T)
    y_g = part(MB, T)
    ring = part(RING, 2, T)
    dA = part(2, MB, T)
    hb = part(2, MB, T)
    xd = sb("xd", [R + 2 * NS, T])
    halo_cols = sb("halo_cols", [P, MB, KC - 1])
    carry = sb("carry", [P, NS, MB])
    xr = sb("xr", [P, 2, TJ, D])
    xn2 = sb("xn2", [P, TJ, D])
    xn2T = sb("xn2T", [P, 2, KD, P])
    probs = sb("probs", [P, 2, H * M])
    probsT = sb("probsT", [P, HC, P])
    xn3 = part(TJ, D)
    xn3T = probsT[:].rearrange("p c t -> p (c t)").rearrange("p (k t) -> p k t", k=KD)
    row_max = sb("row_max", [P, H])
    row_sum = sb("row_sum", [P, H])
    row_inv = sb("row_inv", [P, 2, H])

    class Norm:
        def __init__(self, name):
            self.stats = sb(name + "_stats", [P, TJ, 6])
            self.mv = sb(name + "_mv", [P, TJ, 2])
            self.ln = sb(name + "_ln", [P, TJ])
            self.r0 = sb(name + "_r0", [P, TJ])
            self.tmp = sb(name + "_tmp", [P, 3, TJ])
            self.rstd = sb(name + "_rstd", [P, TJ])
            self.shift = sb(name + "_shift", [P, TJ])
            self.dve = sem(name + "_dve")
            self.act = sem(name + "_act")
            self.done = sem(name + "_done")
    LN_DVE = 2 * TJ + 5
    norm1, norm2, norm3 = Norm("norm1"), Norm("norm2"), Norm("norm3")

    a_steps = sem("a_steps")
    xa_in, xr_in = sem("xa_in"), [sem("xr_in0"), sem("xr_in1")]
    mm_full, mm_free = sem("mm_full"), sem("mm_free")
    tb_full, tb_free = sem("tb_full"), sem("tb_free")
    ao_full, ao_free = sem("ao_full"), sem("ao_free")
    out_full = sem("out_full")
    x1_added = sem("x1_added")
    sc_full, sc_free = sem("sc_full"), sem("sc_free")
    et_full, et_free = sem("et_full"), sem("et_free")
    halo, conv = sem("halo"), sem("conv")
    xc_ready, zg_ready = sem("xc_ready"), sem("zg_ready")
    softplus_act, delta_ready, u_ready = sem("softplus_act"), sem("delta_ready"), sem("u_ready")
    bc_stored, ring_in = sem("bc_stored"), [sem(f"ring_in{s}") for s in range(RING)]
    yd_init = sem("yd_init")
    da_ready, dbu_ready, h_ready, carry_ready = (sem(n) for n in
                                                 ("da_ready", "dbu_ready", "h_ready", "carry_ready"))
    ch_ready, yd_added, yg_added = sem("ch_ready"), sem("yd_added"), sem("yg_added")
    y_sum, y_ready = sem("y_sum"), sem("y_ready")
    g_in, u_in = sem("g_in"), sem("u_in")
    bo_added = sem("bo_added")
    max_ready, exp_ready, sum_ready, inv_ready, probs_ready = (sem(n) for n in (
        "max_ready", "exp_ready", "sum_ready", "inv_ready", "probs_ready"))
    x2_stored, xn3_stored = [sem("x2_stored0"), sem("x2_stored1")], sem("xn3_stored")

    mm, tb, ao = bank[0:2], bank[2], bank[3]
    YG = len(GP_ADDS)
    dve_adds = [n for n in range(1, NS) if n not in GP_ADDS]
    YD = len(dve_adds)
    CONV = MB * KC + 1
    SOFTPLUS = MB + 2

    MM = KD + 4 * MB

    def mm_z(c):
        missing = KD + MB if isinstance(c, int) and c == NC - 1 else 0
        return MM * c + 2 * (KD + 2 * MB) - missing

    def mm_pw(f):
        return MM * f + KD + MB

    def mm_dt(f):
        return mm_pw(f) + MB

    def mm_tr(g):
        return 0 if isinstance(g, int) and g == 0 else MM * g - MB

    def mm_x(g):
        return mm_tr(g) + KD

    TB = TJ + 1 + KD + 1

    def tb_less(a, before_last, last):
        return {NC - 2: before_last, NC - 1: last}.get(a, 0) if isinstance(a, int) else 0

    def tb_bc(f):
        return f if isinstance(f, int) and f < 2 else TB * (f - 2) + 5

    def tb_ln2(a, j):
        if j == 0:
            return 2 if isinstance(a, int) and a == 0 else TB * a - 1 - tb_less(a, 0, 1)
        if j < TJ - 1:
            return TB * a + 2 + j - tb_less(a, 0, 1)
        return TB * a + 3 + j - tb_less(a, 1, 2)

    def tb_ln3(a, i):
        return TB * a + TB + i - tb_less(a, 1, 3)

    def pa_out(c):
        return (1 + TJ) * c

    def pa_scores(a, j):
        return (1 + TJ) * a + 1 + j

    def schedule(eng, step):
        step(-2, -1, True, False, False, False, True)
        step(-1, -1, False, False, False, True, True)
        step(0, 0, True, True, False, True, True)
        with eng.Fori(0, B - 2) as b:
            step(2 * b + 1, b, False, True, True, True, True)
            step(2 * b + 2, b + 1, True, True, True, True, True)
        step(NC - 3, NC // 2 - 2, False, True, True, True, True)
        step(NC - 2, NC // 2 - 1, True, True, True, True, False)
        step(NC - 1, NC // 2 - 1, False, True, True, False, False)
        step(NC, NC // 2, True, False, True, False, False)


    with nc.Block() as block:
        @block.sync
        def _(sp):
            def load_ring(c, n, par):
                wait_apart(sp, ch_ready, NS * c + n - RING + 1, passed[0])
                src = bc_dram[par].rearrange("(g n) t -> g n t", n=NS)[:, n, :]
                sp.dma_start(ring[:, n % RING], src.partition_broadcast(P)).then_inc(ring_in[n % RING], 16)

            def step(c, half, starts, scan, att, conv_part, proj):
                a, f, g, par, other = c - 1, c + 1, c + 2, 0 if starts else 1, 1 if starts else 0
                if proj:
                    if not (isinstance(g, int) and g == 0):
                        wait_apart(sp, mm_full, mm_tr(f) + KD, passed[0])
                    sp.dma_start(xa, x_t[:, bass.ds(TJ * g, TJ), :]).then_inc(xa_in, 16)
                if scan:
                    wait_apart(sp, x2_stored[par], 16 * half + 16, passed[0])
                    wait_apart(sp, norm3.done, TJ * c + TJ, passed[0])
                    sp.dma_start(xr[:, par], x_t[:, bass.ds(TJ * c, TJ), :]).then_inc(xr_in[par], 16)
                    for n in range(RING, NS):
                        load_ring(c, n, par)
                if conv_part:
                    wait_apart(sp, tb_free, tb_bc(f) + 2, passed[0])
                    sp.dma_start(bc_dram[other], xd[R:R + 2 * NS, :]).then_inc(bc_stored, 16)
                    wait_apart(sp, bc_stored, 16 * f + 16, passed[0])
                    for n in range(RING):
                        load_ring(f, n, other)
                if scan and starts:
                    wait_apart(sp, sc_full, TJ * c, passed[0])
                    sp.dma_start(g_sb[:], g_dram[bass.ds(half, 1)].rearrange(
                        "o p (k n) -> (o p) k n", k=KD)).then_inc(g_in, 16)
                    wait_apart(sp, ao_full, TJ * c, passed[0])
                    sp.dma_start(u_sb[:], u_dram[bass.ds(half, 1)].rearrange(
                        "o p (k n) -> (o p) k n", k=HC)).then_inc(u_in, 16)
                if att:
                    wait_apart(sp, ao_free, TJ * a + TJ + 1, passed[0])
                    sp.dma_start(x2_dram[:, bass.ds(TJ * a, TJ), :], xr[:, other]).then_inc(x2_stored[other], 16)
                    wait_apart(sp, norm3.done, TJ * a + 3 * TJ, passed[0])
                    sp.dma_start(xn3_dram[:, bass.ds(TJ * a, TJ), :], xn3).then_inc(xn3_stored, 16)

            schedule(sp, step)
            sp.wait_ge(x2_stored[0], 16 * (NC // 2 + 1))
            sp.wait_ge(x2_stored[1], 16 * (NC // 2 + 1))
            sp.wait_ge(xn3_stored, 16 * (NC + 1))

        @block.gpsimd
        def _(pool):
            pool.sem_inc(mm_free, 2)
            pool.sem_inc(tb_free, 1)
            pool.sem_inc(ao_free, 1)
            pool.sem_inc(sc_free, 1)
            pool.sem_inc(et_free, 1)
            pool.sem_inc(et_full, 2)
            pool.sem_inc(x2_stored[0], 16)
            pool.sem_inc(x2_stored[1], 16)
            pool.sem_inc(xn3_stored, 16)
            pool.sem_inc(norm3.done, 2 * TJ)
            pool.wait_ge(W.arrived, 16 * W.LOADS)

            def normalise(n, base, src, dst):
                wait_apart(pool, n.dve, LN_DVE * base + LN_DVE, passed[1])
                for j in range(TJ):
                    nc.gpsimd.tensor_scalar(dst[:, j], src[:, j], n.rstd[:, j:j + 1], n.shift[:, j:j + 1],
                                            ALU.mult, ALU.add).then_inc(n.done, 1)

            def wait_left(c, n):
                if isinstance(c, int) and c < 0:
                    return
                if n == 0:
                    pool.wait_ge(ch_ready, NS * c + 1)
                elif n in GP_ADDS:
                    pool.wait_ge(yg_added, YG * c + GP_ADDS.index(n) + 1)
                else:
                    pool.wait_ge(yd_added, YD * c + dve_adds.index(n) + 1)

            def step(c, half, starts, scan, att, conv_part, proj):
                a, f, g, par, other = c - 1, c + 1, c + 2, 0 if starts else 1, 1 if starts else 0

                def dbu(c, n):
                    if n >= 2:
                        wait_left(c, n - 2)
                    else:
                        pool.wait_ge(u_ready, c + 1)
                        wait_left(c - 1, NS + n - 2)
                    pool.wait_ge(ring_in[n % RING], 16 * (2 * c + n // RING + 1))
                    nc.gpsimd.tensor_tensor(hb[:, n % 2], u, ring[:, n % RING, 0:1, :].broadcast_to([P, MB, T]),
                                            ALU.mult).then_inc(dbu_ready, 1)

                def add_up(n):
                    pool.wait_ge(ch_ready, NS * c + n + 1)
                    wait(pool, yg_added, YG * c + GP_ADDS.index(n))
                    nc.gpsimd.tensor_tensor(y_g, y_g, hb[:, n % 2], ALU.add).then_inc(yg_added, 1)

                def probabilities(j):
                    if not att:
                        return
                    pool.wait_ge(inv_ready, TJ * a + j + 1)
                    e3 = probs[:, j % 2].rearrange("p (h m) -> p h m", m=M)
                    nc.gpsimd.tensor_tensor(e3, e3, row_inv[:, j % 2, :, None].broadcast_to([P, H, M]),
                                            ALU.mult).then_inc(probs_ready, 1)

                if scan:
                    dbu(c, 2)
                    dbu(c, 3)
                    add_up(2)
                probabilities(0)
                if scan:
                    dbu(c, 4)
                    add_up(3)
                    dbu(c, 5)
                    add_up(4)
                probabilities(1)
                if scan:
                    dbu(c, 6)
                if proj:
                    normalise(norm1, g, xa, xa)
                if scan:
                    dbu(c, 7)
                    add_up(6)
                probabilities(2)
                if conv_part:
                    pool.wait_ge(delta_ready, f + 1)
                    wait(pool, dbu_ready, NS * f)
                    nc.gpsimd.tensor_tensor(u, delta[:, other], xc, ALU.mult).then_inc(u_ready, 1)
                    dbu(f, 0)
                probabilities(3)
                if conv_part:
                    dbu(f, 1)
                if scan:
                    normalise(norm2, c, xr[:, par], xn2)
                    pool.wait_ge(norm2.done, TJ * c + TJ)
                    nc.gpsimd.tensor_tensor(xr[:, par], xr[:, par],
                                            W.bo[:, None, :].broadcast_to([P, TJ, D]),
                                            ALU.add).then_inc(bo_added, 1)
                if att:
                    pool.wait_ge(xn3_stored, 16 * a + 16)
                    normalise(norm3, a, xr[:, other], xn3)

            schedule(pool, step)

        @block.scalar
        def _(act):
            act.wait_ge(W.arrived, 16 * W.LOADS)
            nc.scalar.activation(a_exp[:], W.a_log[:], ACT.Exp).then_inc(a_steps, 1)
            act.wait_ge(a_steps, 1)
            nc.scalar.mul(a_neg[:], a_exp[:], -1.0).then_inc(a_steps, 1)
            act.wait_ge(a_steps, 2)

            def load_tables():
                nc.scalar.preload_act_table_set("natural_log_exp_and_others")

            def rstd_start(n, base):
                act.wait_ge(n.dve, LN_DVE * base + 2 * TJ)
                nc.scalar.activation(n.ln[:], n.mv[:, :, 1], ACT.Ln, bias=eps_col[:, 0:1]).then_inc(n.act, 1)
                act.wait_ge(n.act, 2 * base + 1)
                nc.scalar.activation(n.r0[:], n.ln[:], ACT.Exp, scale=-0.5).then_inc(n.act, 1)

            def step(c, half, starts, scan, att, conv_part, proj):
                a, f, g, par, other = c - 1, c + 1, c + 2, 0 if starts else 1, 1 if starts else 0

                def decay(c, n, parity):
                    wait(act, h_ready, MB * (NS * c + n - 1))
                    for m in range(MB):
                        nc.scalar.activation(dA[:, n % 2, m], delta[:, parity, m], ACT.Exp,
                                             scale=a_neg[:, m, n:n + 1]).then_inc(da_ready, 1)

                def decays(n):
                    if scan:
                        decay(c, n, par)

                def z_out():
                    wait(act, y_ready, c)
                    for m in range(MB):
                        act.wait_ge(mm_full, mm_z(c) + m + 1)
                        nc.scalar.activation(zg[:, m], mm[m % 2][:], ACT.Copy).then_inc(mm_free, 1)

                def ln2_turned(a, j):
                    act.wait_ge(tb_full, tb_ln2(a, j) + 1)
                    nc.scalar.activation(xn2T[:, j % 2].rearrange("p k t -> p (k t)"), tb[:, 0:KD * P],
                                         ACT.Copy).then_inc(tb_free, 1)

                def exponentials(j):
                    if not att:
                        return
                    act.wait_ge(sc_free, pa_scores(a, j) + 2)
                    nc.scalar.activation(probs[:, j % 2], probs[:, j % 2], ACT.Exp, scale=SCALE).then_inc(exp_ready, 1)

                def probs_turned(j):
                    if not att:
                        return
                    act.wait_ge(et_full, TJ * a + j + 3)
                    wait(act, ao_full, TJ * a + j)
                    nc.scalar.activation(probsT[:].rearrange("p c t -> p (c t)"), pair_b[:],
                                         ACT.Copy).then_inc(et_free, 1)

                def ln1_turned():
                    for k in range(KD):
                        act.wait_ge(mm_full, mm_tr(g) + k + 1)
                        nc.scalar.activation(xnT[:, par, k], mm[k % 2][:], ACT.Copy).then_inc(mm_free, 1)

                def x_in_out():
                    wait(act, halo, g)
                    for m in range(MB):
                        act.wait_ge(mm_full, mm_x(g) + m + 1)
                        nc.scalar.activation(xp[:, m, KC - 1:], mm[m % 2][:], ACT.Copy).then_inc(mm_free, 1)

                def pointwise_out(blocks):
                    if 0 in blocks:
                        wait(act, u_ready, f)
                        wait(act, yd_init, MB * f)
                    for m in blocks:
                        act.wait_ge(mm_full, mm_pw(f) + m + 1)
                        nc.scalar.activation(xc[:, m], mm[m % 2][:], ACT.Identity,
                                             bias=W.conv_bias[:, m:m + 1]).then_inc(mm_free, 1)

                def silu_z():
                    act.wait_ge(mm_free, mm_z(c) + MB + 2)
                    nc.scalar.activation(zg, zg, ACT.Silu).then_inc(zg_ready, 1)

                def silu_x():
                    act.wait_ge(mm_free, mm_pw(f) + MB + 2)
                    nc.scalar.activation(xc, xc, ACT.Silu).then_inc(xc_ready, 1)

                def low_rank_out():
                    wait(act, bc_stored, 16 * f)
                    act.wait_ge(tb_full, tb_bc(f) + 1)
                    nc.scalar.activation(xd[:], tb[0:R + 2 * NS, :], ACT.Copy).then_inc(tb_free, 1)

                def softplus():
                    wait(act, da_ready, MB * NS * c)
                    for m in range(MB):
                        act.wait_ge(mm_full, mm_dt(f) + m + 1)
                        src = mm[m % 2]
                        nc.scalar.activation(cv[:, m], src[:], ACT.Abs,
                                             bias=W.dt_bias[:, m:m + 1]).then_inc(softplus_act, 1)
                        nc.scalar.activation(delta[:, other, m], src[:], ACT.Relu,
                                             bias=W.dt_bias[:, m:m + 1]).then_inc(mm_free, 1)
                    act.wait_ge(softplus_act, SOFTPLUS * f + MB)
                    nc.scalar.activation(cv, cv, ACT.Exp, scale=-1.0).then_inc(softplus_act, 1)
                    act.wait_ge(softplus_act, SOFTPLUS * f + MB + 1)
                    nc.scalar.activation(cv, cv, ACT.Ln, bias=1.0).then_inc(softplus_act, 1)

                load_tables()
                if att and not scan:
                    act.wait_ge(out_full, 2 * NC)
                    load_experts(act)
                decays(2)
                if scan:
                    z_out()
                if att:
                    ln2_turned(a, 1)
                exponentials(0)
                decays(3)
                decays(4)
                probs_turned(0)
                if att:
                    ln2_turned(a, 2)
                exponentials(1)
                decays(5)
                if conv_part:
                    pointwise_out((0, 1))
                if scan:
                    silu_z()
                if conv_part:
                    pointwise_out((2, 3))
                    silu_x()
                load_tables()
                probs_turned(1)
                if conv_part:
                    low_rank_out()
                decays(6)
                if proj:
                    rstd_start(norm1, g)
                if att:
                    ln2_turned(a, 3)
                decays(7)
                exponentials(2)
                if conv_part:
                    softplus()
                if proj:
                    ln1_turned()
                exponentials(3)
                if proj:
                    x_in_out()
                probs_turned(2)
                if conv_part:
                    act.wait_ge(delta_ready, f + 1)
                    decay(f, 0, other)
                    decay(f, 1, other)
                probs_turned(3)
                if scan:
                    rstd_start(norm2, c)
                if conv_part:
                    wait(act, out_full, 2 * f)
                    for m in range(MB):
                        nc.scalar.activation(y_d[:, m], xc[:, m], ACT.Copy,
                                             scale=W.d_skip[:, m:m + 1]).then_inc(yd_init, 1)
                if scan:
                    ln2_turned(c, 0)
                if att:
                    rstd_start(norm3, a)
                    for k in range(KD):
                        act.wait_ge(tb_full, tb_ln3(a, k) + 1)
                        nc.scalar.activation(xn3T[:, k], tb[:], ACT.Copy).then_inc(tb_free, 1)

            schedule(act, step)

        @block.vector
        def _(dve):
            dve.wait_ge(W.arrived, 16 * W.LOADS)

            def statistics(n, base, src):
                for j in range(TJ):
                    nc.vector.bn_stats(n.stats[:, j], src[:, j]).then_inc(n.dve, 1)
                wait_apart(dve, n.dve, LN_DVE * base + TJ, passed[2])
                for j in range(TJ):
                    nc.vector.bn_aggr(n.mv[:, j], n.stats[:, j]).then_inc(n.dve, 1)

            def refine(n, base):
                at = LN_DVE * base + 2 * TJ
                dve.wait_ge(n.dve, at)
                dve.wait_ge(n.act, 2 * base + 2)
                nc.vector.scalar_tensor_tensor(out=n.tmp[:, 0], in0=n.mv[:, :, 1], scalar=EPS, in1=n.r0[:],
                                               op0=ALU.add, op1=ALU.mult).then_inc(n.dve, 1)
                dve.wait_ge(n.dve, at + 1)
                nc.vector.tensor_tensor(n.tmp[:, 1], n.tmp[:, 0], n.r0[:], ALU.mult).then_inc(n.dve, 1)
                dve.wait_ge(n.dve, at + 2)
                nc.vector.tensor_scalar(n.tmp[:, 2], n.tmp[:, 1], -0.5, 1.5, ALU.mult, ALU.add).then_inc(n.dve, 1)
                dve.wait_ge(n.dve, at + 3)
                nc.vector.tensor_tensor(n.rstd[:], n.tmp[:, 2], n.r0[:], ALU.mult).then_inc(n.dve, 1)
                dve.wait_ge(n.dve, at + 4)
                nc.vector.scalar_tensor_tensor(out=n.shift[:], in0=n.mv[:, :, 0], scalar=-1.0, in1=n.rstd[:],
                                               op0=ALU.mult, op1=ALU.mult).then_inc(n.dve, 1)

            def step(c, half, starts, scan, att, conv_part, proj):
                a, f, g, par, other = c - 1, c + 1, c + 2, 0 if starts else 1, 1 if starts else 0

                def scan_state(c, n, starts):
                    if n == 0:
                        wait(dve, carry_ready, NS * c)
                    dve.wait_ge(dbu_ready, NS * c + n + 1)
                    for m in range(MB):
                        dve.wait_ge(da_ready, MB * (NS * c + n) + m + 1)
                        nc.vector.tensor_tensor_scan(
                            hb[:, n % 2, m], dA[:, n % 2, m], hb[:, n % 2, m],
                            0.0 if starts else carry[:, n, m:m + 1], ALU.mult, ALU.add).then_inc(h_ready, 1)
                    dve.wait_ge(h_ready, MB * (NS * c + n) + MB)
                    nc.vector.tensor_copy(carry[:, n], hb[:, n % 2, :, T - 1]).then_inc(carry_ready, 1)
                    dst = y_g if n == 0 else hb[:, n % 2]
                    dve.wait_ge(carry_ready, NS * c + n + 1)
                    nc.vector.tensor_tensor(dst, hb[:, n % 2], ring[:, n % RING, 1:2, :].broadcast_to([P, MB, T]),
                                            ALU.mult).then_inc(ch_ready, 1)
                    if n in dve_adds:
                        i = dve_adds.index(n)
                        if i == 0:
                            dve.wait_ge(yd_init, MB * (c + 1))
                        wait(dve, yd_added, YD * c + i)
                        dve.wait_ge(ch_ready, NS * c + n + 1)
                        nc.vector.tensor_tensor(y_d, y_d, hb[:, n % 2], ALU.add).then_inc(yd_added, 1)

                def less_max(j):
                    if not att:
                        return
                    dve.wait_ge(sc_full, TJ * a + j + 1)
                    s3 = pair_a[:].rearrange("p (h m) -> p h m", m=M)
                    nc.vector.tensor_reduce(row_max[:], s3, AX.X, ALU.max).then_inc(max_ready, 1)
                    dve.wait_ge(max_ready, TJ * a + j + 1)
                    dve.wait_ge(et_full, TJ * a + j + 1)
                    nc.vector.tensor_tensor(probs[:, j % 2].rearrange("p (h m) -> p h m", m=M), s3,
                                            row_max[:, :, None].broadcast_to([P, H, M]),
                                            ALU.subtract).then_inc(sc_free, 1)

                def row_sums(j):
                    if not att:
                        return
                    dve.wait_ge(exp_ready, TJ * a + j + 1)
                    nc.vector.tensor_reduce(row_sum[:], probs[:, j % 2].rearrange("p (h m) -> p h m", m=M),
                                            AX.X, ALU.add).then_inc(sum_ready, 1)
                    dve.wait_ge(sum_ready, TJ * a + j + 1)
                    nc.vector.reciprocal(row_inv[:, j % 2], row_sum[:]).then_inc(inv_ready, 1)

                def residual(j):
                    if not att:
                        return
                    if j == 0:
                        dve.wait_ge(bo_added, a + 1)
                    dve.wait_ge(ao_full, TJ * a + j + 1)
                    nc.vector.tensor_tensor(xr[:, other, j], ao[:, 0:D], xr[:, other, j], ALU.add).then_inc(ao_free, 1)

                def convolve(blocks, base):
                    for k in range(KC):
                        for i, m in enumerate(blocks):
                            src = xp[:, m, k:k + T]
                            if k == 0:
                                dve.wait_ge(mm_free, mm_x(f) + m + 3)
                                op = nc.vector.tensor_scalar(cv[:, m], src, W.taps[:, m, 0:1], None, ALU.mult)
                            else:
                                dve.wait_ge(conv, CONV * f + base + len(blocks) * (k - 1) + i + 1)
                                op = nc.vector.scalar_tensor_tensor(
                                    out=cv[:, m], in0=src, scalar=W.taps[:, m, k:k + 1], in1=cv[:, m],
                                    op0=ALU.mult, op1=ALU.add)
                            op.then_inc(conv, 1)

                def state(n):
                    if scan:
                        scan_state(c, n, starts)

                less_max(0)
                if conv_part:
                    wait(dve, halo, f)
                    if starts:
                        nc.vector.tensor_copy(xp[:, :, 0:KC - 1], halo_cols[:]).then_inc(conv, 1)
                    else:
                        nc.vector.memset(xp[:, :, 0:KC - 1], 0.0).then_inc(conv, 1)
                    dve.wait_ge(conv, CONV * f + 1)
                    wait(dve, delta_ready, f)
                    convolve((0, 1), 1)
                state(2)
                row_sums(0)
                if conv_part:
                    convolve((2, 3), 1 + 2 * KC)
                    nc.vector.tensor_copy(halo_cols[:], xp[:, :, T:T + KC - 1]).then_inc(halo, 1)
                state(3)
                less_max(1)
                state(4)
                row_sums(1)
                residual(0)
                if proj:
                    dve.wait_ge(xa_in, 16 * g + 16)
                    wait(dve, norm1.done, TJ * g)
                    statistics(norm1, g, xa)
                state(5)
                less_max(2)
                if proj:
                    refine(norm1, g)
                state(6)
                row_sums(2)
                less_max(3)
                residual(1)
                if conv_part:
                    dve.wait_ge(softplus_act, SOFTPLUS * (f + 1))
                    dve.wait_ge(mm_free, mm_dt(f) + MB + 2)
                    nc.vector.tensor_tensor(delta[:, other], delta[:, other], cv, ALU.add).then_inc(delta_ready, 1)
                state(7)
                row_sums(3)
                if scan:
                    dve.wait_ge(yg_added, YG * (c + 1))
                    dve.wait_ge(yd_added, YD * (c + 1))
                    nc.vector.tensor_tensor(y_d, y_d, y_g, ALU.add).then_inc(y_sum, 1)
                    dve.wait_ge(y_sum, c + 1)
                    dve.wait_ge(zg_ready, c + 1)
                    nc.vector.tensor_tensor(y_d, y_d, zg, ALU.mult).then_inc(y_ready, 1)
                residual(2)
                if conv_part:
                    scan_state(f, 0, not starts)
                if scan:
                    dve.wait_ge(xr_in[par], 16 * half + 16)
                    for i in range(2):
                        two = xr[:, par, 2 * i:2 * i + 2]
                        dve.wait_ge(out_full, 2 * c + i + 1)
                        op = nc.vector.tensor_tensor(two, pair_a[:, 512 * i:512 * (i + 1)].rearrange(
                            "p (j d) -> p j d", d=D), two, ALU.add)
                        op.then_inc(sc_free if i else x1_added, 1)
                    dve.wait_ge(x1_added, c + 1)
                    dve.wait_ge(sc_free, pa_out(c) + 2)
                    statistics(norm2, c, xr[:, par])
                    refine(norm2, c)
                residual(3)
                if att:
                    dve.wait_ge(ao_free, TJ * a + TJ + 1)
                    statistics(norm3, a, xr[:, other])
                    refine(norm3, a)
                if conv_part:
                    scan_state(f, 1, not starts)
                if att:
                    dve.wait_ge(tb_full, tb_ln3(a, KD) + 1)
                    nc.vector.tensor_tensor(scores_all[:, bass.ds(TJ * a, TJ), :],
                                            tb[:, 0:TJ * E].rearrange("p (j e) -> p j e", e=E),
                                            W.br[:, None, :].broadcast_to([P, TJ, E]),
                                            ALU.add).then_inc(tb_free, 1)

            schedule(dve, step)

        @block.tensor
        def _(pe):
            pe.wait_ge(W.arrived, 16 * W.LOADS)

            def step(c, half, starts, scan, att, conv_part, proj):
                a, f, g, par, other = c - 1, c + 1, c + 2, 0 if starts else 1, 1 if starts else 0

                def mm_take(first, m):
                    pe.wait_ge(mm_free, first + m + 1)
                    return mm[m % 2]

                def ln2_turn(a, j):
                    pe.wait_ge(norm2.done, TJ * a + TJ)
                    pe.wait_ge(tb_free, tb_ln2(a, j) + 1)
                    for k in range(KD):
                        last = nc.tensor.transpose(tb[:, k * P:(k + 1) * P], xn2[:, j, k * P:(k + 1) * P], ident[:])
                    last.then_inc(tb_full, 1)

                def scores(a, j):
                    pe.wait_ge(tb_free, tb_ln2(a, j) + 2)
                    pe.wait_ge(sc_free, pa_scores(a, j) + 1)
                    for half_n in range(2):
                        for k in range(KD):
                            last = nc.tensor.matmul(pair_a[:, half_n * 512:(half_n + 1) * 512],
                                                    xn2T[:, j % 2, k], g_sb[:, k, half_n * 512:(half_n + 1) * 512],
                                                    start=(k == 0), stop=(k == KD - 1))
                    last.then_inc(sc_full, 1)

                def turn_probs(j):
                    if not att:
                        return
                    pe.wait_ge(probs_ready, TJ * a + j + 1)
                    pe.wait_ge(et_free, TJ * a + j + 1)
                    for hc in range(HC):
                        last = nc.tensor.transpose(pair_b[:, hc * P:(hc + 1) * P],
                                                   probs[:, j % 2, hc * P:(hc + 1) * P], ident[:])
                    last.then_inc(et_full, 1)

                def attend(j):
                    if not att:
                        return
                    pe.wait_ge(et_free, TJ * a + j + 2)
                    pe.wait_ge(ao_free, TJ * a + j + 1)
                    for hc in range(HC):
                        last = nc.tensor.matmul(ao[:, 0:D], probsT[:, hc], u_sb[:, hc],
                                                start=(hc == 0), stop=(hc == HC - 1))
                    last.then_inc(ao_full, 1)

                if scan:
                    for m in range(MB):
                        dst = mm_take(mm_z(c), m)
                        for k in range(KD):
                            last = nc.tensor.matmul(dst[:], W.w_in[:, k, DI + m * P:DI + (m + 1) * P],
                                                    xnT[:, par, k], start=(k == 0), stop=(k == KD - 1))
                        last.then_inc(mm_full, 1)
                if att:
                    ln2_turn(a, 1)
                    scores(a, 1)
                    if not starts:
                        pe.wait_ge(u_in, 16 * half + 16)
                turn_probs(0)
                if att:
                    ln2_turn(a, 2)
                attend(0)
                if conv_part:
                    pe.wait_ge(conv, CONV * (f + 1))
                    for m in range(MB):
                        dst = mm_take(mm_pw(f), m)
                        for k in range(MB):
                            last = nc.tensor.matmul(dst[:], W.pw[:, k, m * P:(m + 1) * P], cv[:, k],
                                                    start=(k == 0), stop=(k == MB - 1))
                        last.then_inc(mm_full, 1)
                if att:
                    scores(a, 2)
                turn_probs(1)
                if conv_part:
                    pe.wait_ge(xc_ready, f + 1)
                    pe.wait_ge(tb_free, tb_bc(f) + 1)
                    for k in range(MB):
                        last = nc.tensor.matmul(tb[0:R + 2 * NS, :], W.w_x[:, k], xc[:, k],
                                                start=(k == 0), stop=(k == MB - 1))
                    last.then_inc(tb_full, 1)
                attend(1)
                if att:
                    ln2_turn(a, 3)
                if conv_part:
                    pe.wait_ge(tb_free, tb_bc(f) + 2)
                    for m in range(MB):
                        nc.tensor.matmul(mm_take(mm_dt(f), m)[:], W.w_dt[:, m * P:(m + 1) * P], xd[0:R, :],
                                         start=True, stop=True).then_inc(mm_full, 1)
                if att:
                    scores(a, 3)
                if proj:
                    pe.wait_ge(norm1.done, TJ * g + TJ)
                    for k in range(KD):
                        dst = mm_take(mm_tr(g), k)
                        for j in range(TJ):
                            last = nc.tensor.transpose(dst[:, j * P:(j + 1) * P], xa[:, j, k * P:(k + 1) * P],
                                                       ident[:])
                        last.then_inc(mm_full, 1)
                    pe.wait_ge(mm_free, mm_tr(g) + KD + 2)
                    for m in range(MB):
                        dst = mm_take(mm_x(g), m)
                        for k in range(KD):
                            last = nc.tensor.matmul(dst[:], W.w_in[:, k, m * P:(m + 1) * P], xnT[:, par, k],
                                                    start=(k == 0), stop=(k == KD - 1))
                        last.then_inc(mm_full, 1)
                turn_probs(2)
                attend(2)
                turn_probs(3)
                if scan:
                    pe.wait_ge(y_ready, c + 1)
                    pe.wait_ge(sc_free, pa_out(c) + 1)
                    for j in range(TJ):
                        for k in range(MB):
                            last = nc.tensor.matmul(pair_a[:, j * D:(j + 1) * D], y_d[:, k, j * P:(j + 1) * P],
                                                    W.w_out[:, k], start=(k == 0), stop=(k == MB - 1))
                        if j % 2:
                            last.then_inc(out_full, 1)
                attend(3)
                if scan:
                    ln2_turn(c, 0)
                    if starts:
                        pe.wait_ge(g_in, 16 * half + 16)
                    scores(c, 0)
                if att:
                    pe.wait_ge(norm3.done, TJ * a + 3 * TJ)
                    for k in range(KD):
                        pe.wait_ge(tb_free, tb_ln3(a, k) + 1)
                        for j in range(TJ):
                            last = nc.tensor.transpose(tb[:, j * P:(j + 1) * P], xn3[:, j, k * P:(k + 1) * P],
                                                       ident[:])
                        last.then_inc(tb_full, 1)
                    pe.wait_ge(tb_free, tb_ln3(a, KD) + 1)
                    for j in range(TJ):
                        for k in range(KD):
                            last = nc.tensor.matmul(tb[:, j * E:(j + 1) * E], xn3T[:, k, j * P:(j + 1) * P],
                                                    W.wr[:, k], start=(k == 0), stop=(k == KD - 1))
                    last.then_inc(tb_full, 1)

            schedule(pe, step)


def expert_part(nc, sem, sb_in, passed, ident, scores_all, bank, pair_a, pair_b, w1_sb, w2_sb, w1_in, w2_in,
                b1, b2, x2_dram, xn3_dram, xs_dram, ys_dram, out_t):
    with ExitStack() as st:
        def sb(name, shape, dt=F32):
            return sb_in(st, name, shape, dt)

        slot = sb("slot", [P, TT], U32)
        tile_expert = sb("tile_expert", [P, NT], I32)
        b1_sb = sb("b1_sb", [P, E, KF])
        b2_sb = sb("b2_sb", [P, E, D])

        bias_in = sem("bias_in")
        xn3_in = sem("xn3_in")
        consts, const_steps, route = sem("route_consts"), sem("const_steps"), sem("route_steps")
        counts_ready, scattered = sem("counts_ready"), sem("scattered")

        with ExitStack() as rt:
            def rb(name, shape, dt=F32):
                return sb_in(rt, name, shape, dt)

            rows = rb("rows", [P, TT, D])
            e_less = rb("e_less", [P, TT, E])
            tri = rb("tri", [P, P])
            ones = rb("ones", [P, P])
            k128 = rb("k128", [P, E, TT])
            tile_no = rb("tile_no", [P, NT, E])
            best = rb("best", [P, TT])
            is_best = rb("is_best", [P, TT, E])
            pick = rb("pick", [P, TT, E])
            first = rb("first", [P, TT])
            onehot = rb("onehot", [P, TT, E])
            within = rb("within", [P, TT, E])
            total = rb("total", [P, E, TT])
            upto = rb("upto", [P, E, TT])
            more = rb("more", [P, E, TT])
            tiles = rb("tiles", [P, E])
            tiles_end = rb("tiles_end", [P, E])
            base = rb("base", [P, E])
            offs = rb("offs", [P, TT, E])
            slot_f = rb("slot_f", [P, TT])
            past = rb("past", [P, NT, E])
            expert_f = rb("expert_f", [P, NT])
            expert_c = rb("expert_c", [P, NT])

            ROUTE_SLOTS = 18 + E

            with nc.Block() as block:
                @block.sync
                def _(sp):
                    sp.dma_start(rows[:], xn3_dram).then_inc(xn3_in, 16)
                    sp.dma_start(b1_sb[:], b1.rearrange("e (k p) -> p e k", p=P),
                                 allow_slow_non_contiguous=True).then_inc(bias_in, 16)
                    sp.dma_start(b2_sb[:], b2.partition_broadcast(P)).then_inc(bias_in, 16)
                    sp.wait_ge(bias_in, 32)

                @block.gpsimd
                def _(pool):
                    kw = dict(allow_small_or_imprecise_dtypes=True)
                    nc.gpsimd.iota(e_less[:], [[0, TT], [1, E]], base=-E, channel_multiplier=0, **kw).then_inc(consts, 1)
                    nc.gpsimd.iota(k128[:], [[0, E], [P, TT]], base=0, channel_multiplier=0, **kw).then_inc(consts, 1)
                    nc.gpsimd.iota(tile_no[:], [[1, NT], [0, E]], base=0, channel_multiplier=0, **kw).then_inc(consts, 1)
                    nc.gpsimd.memset(ones[:], 1.0).then_inc(consts, 1)
                    nc.gpsimd.memset(tri[:], 1.0).then_inc(const_steps, 1)
                    pool.wait_ge(const_steps, 1)
                    nc.gpsimd.affine_select(out=tri[:], in_=tri[:], compare_op=ALU.is_gt, fill=0.0, base=0,
                                            pattern=[[1, P]], channel_multiplier=-1).then_inc(consts, 1)
                    pool.wait_ge(route, ROUTE_SLOTS)
                    pool.wait_ge(xn3_in, 16)
                    for n in range(TT):
                        nc.gpsimd.indirect_dma_start(
                            xs_dram, bass.IndirectOffsetOnAxis(ap=slot[:, n:n + 1], axis=0),
                            rows[:, n], None).then_inc(scattered, 16)
                    pool.wait_ge(scattered, 16 * TT)

                @block.vector
                def _(dve):
                    count = [0]

                    def then(op):
                        op.then_inc(route, 1)
                        count[0] += 1
                        dve.wait_ge(route, count[0])

                    V = nc.vector
                    dve.wait_ge(consts, 5)
                    then(V.tensor_reduce(best[:], scores_all[:], AX.X, ALU.max))
                    then(V.tensor_tensor(is_best[:], scores_all[:], best[:, :, None].broadcast_to([P, TT, E]), ALU.is_ge))
                    then(V.tensor_tensor(pick[:], is_best[:], e_less[:], ALU.mult))
                    then(V.tensor_reduce(first[:], pick[:], AX.X, ALU.min))
                    then(V.tensor_tensor(onehot[:], e_less[:], first[:, :, None].broadcast_to([P, TT, E]), ALU.is_equal))
                    dve.wait_ge(counts_ready, 2)
                    then(V.tensor_copy(within[:], bank[0][:, 0:TT * E].rearrange("p (t e) -> p t e", e=E)))
                    then(V.tensor_copy(total[:].rearrange("p e t -> p t e"),
                                       bank[1][:, 0:TT * E].rearrange("p (t e) -> p t e", e=E)))
                    for e in range(E):
                        then(V.tensor_tensor_scan(upto[:, e], ones[:, 0:TT], total[:, e], 0.0, ALU.mult, ALU.add))
                    then(V.tensor_tensor(more[:], upto[:, :, TT - 1:TT].broadcast_to([P, E, TT]), k128[:], ALU.is_gt))
                    then(V.tensor_reduce(tiles[:], more[:], AX.X, ALU.add))
                    then(V.tensor_tensor_scan(tiles_end[:], ones[:, 0:E], tiles[:], 0.0, ALU.mult, ALU.add))
                    then(V.tensor_tensor(base[:], tiles_end[:], tiles[:], ALU.subtract))
                    then(V.tensor_scalar(base[:], base[:], float(P), None, ALU.mult))
                    then(V.tensor_tensor(upto[:], upto[:], total[:], ALU.subtract))
                    then(V.tensor_tensor(offs[:], upto[:].rearrange("p e t -> p t e"), within[:], ALU.add))
                    then(V.tensor_tensor(offs[:], offs[:], base[:, None, :].broadcast_to([P, TT, E]), ALU.add))
                    then(V.tensor_tensor(offs[:], offs[:], onehot[:], ALU.mult))
                    then(V.tensor_reduce(slot_f[:], offs[:], AX.X, ALU.add))
                    then(V.tensor_copy(slot[:], slot_f[:]))
                    then(V.tensor_tensor(past[:], tile_no[:], tiles_end[:, None, :].broadcast_to([P, NT, E]), ALU.is_ge))
                    then(V.tensor_reduce(expert_f[:], past[:], AX.X, ALU.add))
                    then(V.tensor_scalar(expert_c[:], expert_f[:], float(E - 1), None, ALU.min))
                    then(V.tensor_copy(tile_expert[:], expert_c[:]))

                @block.tensor
                def _(pe):
                    pe.wait_ge(route, 5)
                    oh = onehot[:].rearrange("p t e -> p (t e)")
                    nc.tensor.matmul(bank[0][:, 0:TT * E], tri[:], oh, start=True, stop=True).then_inc(counts_ready, 1)
                    nc.tensor.matmul(bank[1][:, 0:TT * E], ones[:], oh, start=True, stop=True).then_inc(counts_ready, 1)

        with ExitStack() as ft:
            def fb(name, shape, dt=F32):
                return sb_in(ft, name, shape, dt)

            xs = fb("xs", [P, 2, D])
            xsT = fb("xsT", [P, 2, KD, P])
            hid = fb("hid", [P, 2, F])
            hidT = fb("hidT", [P, 2, KF, P])
            ys = fb("ys", [P, 2, D])

            xs_in = [sem("xs_in0"), sem("xs_in1")]
            x_turned, xsT_ready = sem("x_turned"), sem("xsT_ready")
            up_full, up_free = sem("up_full"), sem("up_free")
            hid_turned, act_done = sem("hid_turned"), sem("act_done")
            down_full, down_free = sem("down_full"), sem("down_free")
            ys_stored = [sem("ys_stored0"), sem("ys_stored1")]
            x_bank, y_bank = bank[0], bank[1]

            def tiles_loop(eng, step):
                with eng.Fori(0, (NT - 3) // 2) as k:
                    step(2 * k, k, 0, True)
                    step(2 * k + 1, k, 1, True)
                k = (NT - 3) // 2
                step(NT - 3, k, 0, True)
                step(NT - 2, k, 1, False)

            with nc.Block() as block:
                @block.sync
                def _(sp):
                    def load(i, p):
                        sp.dma_start(xs[:, p], xs_dram[bass.ds(i * P, P), :]).then_inc(xs_in[p], 16)

                    def store(i, p):
                        wait_apart(sp, down_free, i + 1, passed[0])
                        sp.dma_start(ys_dram[bass.ds(i * P, P), :], ys[:, p]).then_inc(ys_stored[p], 16)

                    load(0, 0)
                    load(1, 1)
                    sp.wait_ge(x_turned, 1)
                    load(2, 0)

                    def step(i, k, p, more):
                        if more and not (isinstance(i, int) and i == NT - 3):
                            sp.wait_ge(x_turned, i + 2)
                            load(i + 3, 1 - p)
                        store(i, p)

                    tiles_loop(sp, step)
                    store(NT - 1, 0)
                    sp.wait_ge(ys_stored[0], 16 * (NT // 2 + 1))
                    sp.wait_ge(ys_stored[1], 16 * (NT // 2))

                @block.tensor
                def _(pe):
                    pe.wait_ge(w1_in, 16 * E)
                    pe.wait_ge(w2_in, 16 * E)

                    def turn_x(i, k, p):
                        pe.wait_ge(xs_in[p], 16 * k + 16)
                        wait(pe, xsT_ready, i)
                        for c in range(KD):
                            last = nc.tensor.transpose(x_bank[:, c * P:(c + 1) * P], xs[:, p, c * P:(c + 1) * P], ident[:])
                        last.then_inc(x_turned, 1)

                    def up(i, p):
                        e = pe.value_load(tile_expert[0:1, bass.ds(i, 1)], min_val=0, max_val=E - 1)
                        pe.wait_ge(xsT_ready, i + 1)
                        wait(pe, up_free, i)
                        for half in range(F // 512):
                            for c in range(KD):
                                last = nc.tensor.matmul(
                                    pair_a[:, half * 512:(half + 1) * 512], xsT[:, p, c],
                                    w1_sb[:, bass.ds(e, 1), c, half * 512:(half + 1) * 512].rearrange("p o f -> p (o f)"),
                                    start=(c == 0), stop=(c == KD - 1))
                        last.then_inc(up_full, 1)

                    def turn_hidden(i, p):
                        pe.wait_ge(up_free, i + 1)
                        wait(pe, act_done, KF * i)
                        for c in range(KF):
                            last = nc.tensor.transpose(pair_b[:, c * P:(c + 1) * P], hid[:, p, c * P:(c + 1) * P], ident[:])
                        last.then_inc(hid_turned, 1)

                    def down(i, p):
                        e = pe.value_load(tile_expert[0:1, bass.ds(i, 1)], min_val=0, max_val=E - 1)
                        pe.wait_ge(act_done, KF * i + KF)
                        wait(pe, down_free, i)
                        for c in range(KF):
                            last = nc.tensor.matmul(y_bank[:, 0:D], hidT[:, p, c],
                                                    w2_sb[:, bass.ds(e, 1), c, :].rearrange("p o d -> p (o d)"),
                                                    start=(c == 0), stop=(c == KF - 1))
                        last.then_inc(down_full, 1)

                    turn_x(0, 0, 0)
                    turn_x(1, 0, 1)
                    up(0, 0)
                    turn_hidden(0, 0)

                    def step(i, k, p, more):
                        up(i + 1, 1 - p)
                        if more:
                            turn_x(i + 2, k + 1, p)
                        down(i, p)
                        turn_hidden(i + 1, 1 - p)

                    tiles_loop(pe, step)
                    down(NT - 1, 0)

                @block.vector
                def _(dve):
                    def x_out(i, p):
                        dve.wait_ge(x_turned, i + 1)
                        if not (isinstance(i, int) and i < 2):
                            dve.wait_ge(up_full, i - 1)
                        nc.vector.tensor_copy(xsT[:, p].rearrange("p c t -> p (c t)"),
                                              x_bank[:, 0:KD * P]).then_inc(xsT_ready, 1)

                    def hid_out(i, p):
                        dve.wait_ge(up_full, i + 1)
                        nc.vector.tensor_copy(hid[:, p], pair_a[:]).then_inc(up_free, 1)

                    def y_out(i, k, p):
                        e = dve.value_load(tile_expert[0:1, bass.ds(i, 1)], min_val=0, max_val=E - 1)
                        dve.wait_ge(down_full, i + 1)
                        dve.wait_ge(ys_stored[p], 16 * k + 16)
                        nc.vector.tensor_tensor(ys[:, p], y_bank[:, 0:D],
                                                b2_sb[:, bass.ds(e, 1), :].rearrange("p o d -> p (o d)"),
                                                ALU.add).then_inc(down_free, 1)

                    x_out(0, 0)
                    x_out(1, 1)
                    hid_out(0, 0)

                    def step(i, k, p, more):
                        hid_out(i + 1, 1 - p)
                        if more:
                            x_out(i + 2, p)
                        y_out(i, k, p)

                    tiles_loop(dve, step)
                    y_out(NT - 1, (NT - 1) // 2, 0)

                @block.scalar
                def _(act):
                    def gelu(i, p):
                        e = act.value_load(tile_expert[0:1, bass.ds(i, 1)], min_val=0, max_val=E - 1)
                        act.wait_ge(hid_turned, i + 1)
                        for c in range(KF):
                            nc.scalar.activation(hidT[:, p, c], pair_b[:, c * P:(c + 1) * P], ACT.Gelu,
                                                 bias=b1_sb[:, bass.ds(e, 1), c]).then_inc(act_done, 1)

                    gelu(0, 0)

                    def step(i, k, p, more):
                        gelu(i + 1, 1 - p)

                    tiles_loop(act, step)

                @block.gpsimd
                def _(pool):
                    pool.sem_inc(ys_stored[0], 16)
                    pool.sem_inc(ys_stored[1], 16)

        with ExitStack() as ot:
            res = sb_in(ot, "res", [P, TT, D])
            got = sb_in(ot, "got", [P, TT // 4, D])
            got2 = sb_in(ot, "got2", [P, TT // 4, D])
            res_in, res_done, out_stored = sem("res_in"), sem("res_done"), sem("out_stored")
            gathered = [sem(f"gathered{n}") for n in range(4)]
            GT = TT // 4
            halves = (got, got2)
            with nc.Block() as block:
                @block.sync
                def _(sp):
                    sp.dma_start(res[:], x2_dram).then_inc(res_in, 16)
                    for n in range(4):
                        sp.wait_ge(res_done, n + 1)
                        sp.dma_start(out_t[:, n * GT:(n + 1) * GT, :], res[:, n * GT:(n + 1) * GT, :]).then_inc(out_stored, 16)
                    sp.wait_ge(out_stored, 64)

                @block.gpsimd
                def _(pool):
                    for n in range(4):
                        if n >= 2:
                            pool.wait_ge(res_done, n - 1)
                        for t in range(GT):
                            nc.gpsimd.indirect_dma_start(
                                halves[n % 2][:, t], None, ys_dram,
                                bass.IndirectOffsetOnAxis(ap=slot[:, n * GT + t:n * GT + t + 1], axis=0),
                            ).then_inc(gathered[n], 16)

                @block.vector
                def _(dve):
                    dve.wait_ge(res_in, 16)
                    for n in range(4):
                        dve.wait_ge(gathered[n], 16 * GT)
                        nc.vector.tensor_tensor(res[:, n * GT:(n + 1) * GT, :], res[:, n * GT:(n + 1) * GT, :],
                                                halves[n % 2][:], ALU.add).then_inc(res_done, 1)


_INS = ["x", "ctx_1024", "L0_attn_W_in", "L0_attn_dw_kernel", "L0_attn_pw_kernel", "L0_attn_conv_bias",
        "L0_attn_W_x", "L0_attn_W_dt", "L0_attn_b_dt", "L0_attn_A_log", "L0_attn_D", "L0_attn_W_out",
        "L0_xattn_Wq", "L0_xattn_Wk", "L0_xattn_Wv", "L0_xattn_Wo", "L0_xattn_bo",
        "L0_ffn_wr", "L0_ffn_br", "L0_ffn_w1", "L0_ffn_b1", "L0_ffn_w2", "L0_ffn_b2"]


def kernel(**inputs):
    import numpy as _np
    import concourse.bacc as _bacc
    from concourse import mybir as _mybir
    from concourse.bass_utils import run_bass_kernel_spmd as _run

    nc = _bacc.Bacc("TRN2", target_bir_lowering=False, num_devices=1)
    arrays, args = {}, []
    for name in _INS:
        a = _np.ascontiguousarray(inputs[name])
        arrays[f"in_{name}"] = a
        args.append(nc.dram_tensor(f"in_{name}", a.shape, _mybir.dt.from_np(a.dtype), kind="ExternalInput").ap())
    out = nc.dram_tensor("out_0", (B, S, D), _mybir.dt.float32, kind="ExternalOutput").ap()
    decoder_layer(nc, *args, out)
    r = _run(nc, [arrays], core_ids=[0])
    return r.results[0]["out_0"]
```

```python
import concourse.bass as bass
from concourse import mybir
from contextlib import ExitStack

F32 = mybir.dt.float32
I32 = mybir.dt.int32
U32 = mybir.dt.uint32
BF16 = mybir.dt.bfloat16
ALU = mybir.AluOpType
ACT = mybir.ActivationFunctionType
AX = mybir.AxisListType

P = 128
B, S, D = 4, 1024, 256
DI, NS, KC, R = 512, 8, 4, 16
H, DH, M = 16, 64, 64
E, F = 8, 1024
EPS = 1e-5
T = 512
NC = B * S // T
TJ = T // P
KD = D // P
MB = DI // P
HC = H * DH // P
KF = F // P
TT = B * S // P
NT = TT + E - 1
SCALE = DH ** -0.5
RING = 4
GP_ADDS = (1, 2, 3, 4, 6)


def wait(eng, sem, value):
    if isinstance(value, int) and value <= 0:
        return
    eng.wait_ge(sem, value)


def wait_apart(eng, sem, value, passed):
    if isinstance(value, int) and value <= 0:
        return
    eng.wait_ge(sem, value)
    eng.sem_inc(passed, 1)


class Carver:
    def __init__(self, arena):
        self.arena, self.at = arena, 0

    def __call__(self, *shape):
        n = 1
        for s in shape:
            n *= s
        part = self.arena[:, self.at:self.at + n]
        self.at += n
        names = [f"d{i}" for i in range(len(shape))]
        if len(shape) == 1:
            return part
        return part.rearrange(f"p ({' '.join(names)}) -> p {' '.join(names)}",
                              **{k: v for k, v in zip(names[1:], shape[1:])})


ARENA = 34828


def decoder_layer(nc, x, ctx_in, W_in, dwk, pwk, cbias, W_x, W_dt, b_dt, A_log, D_skip, W_out,
                  Wq, Wk, Wv, Wo, bo, wr, br, w1, b1, w2, b2, out):
    x_f = x.rearrange("b s d -> (b s) d")
    x_t = x_f.rearrange("(n p) d -> p n d", p=P)
    out_rows = out.rearrange("b s d -> (b s) d")

    def dram(name, shape):
        return nc.dram_tensor(name, shape, F32, kind="Internal").ap()

    g_dram = dram("g_dram", (B, P, KD * H * M))
    u_dram = dram("u_dram", (B, P, HC * D))
    bc_dram = dram("bc_dram", (2, 2 * NS, T))
    x2_dram = dram("x2_dram", (P, TT, D))
    xn3_dram = dram("xn3_dram", (P, TT, D))

    root = ExitStack()
    with root:
        def sem(name):
            return root.enter_context(nc.semaphore(name))

        def sb_in(stack, name, shape, dt=F32):
            return stack.enter_context(nc.sbuf_tensor(name, shape, dt))

        ident_ready = sem("ident_ready")
        passed = [sem("passed_sync"), sem("passed_gpsimd"), sem("passed_vector")]
        ident = sb_in(root, "ident", [P, P])
        eps_col = sb_in(root, "eps_col", [P, 1])
        scores_all = sb_in(root, "scores_all", [P, TT, E])
        bank = [root.enter_context(nc.psum_tensor(f"bank{i}", [P, 512], F32)) for i in range(4)]
        pair_a = root.enter_context(nc.psum_tensor("pair_a", [P, 1024], F32))
        pair_b = root.enter_context(nc.psum_tensor("pair_b", [P, 1024], F32))

        arena = sb_in(root, "arena", [P, ARENA])
        w1_in, w2_in = sem("w1_in"), sem("w2_in")
        experts = Carver(arena)
        w1_sb, w2_sb = experts(E, KD, F), experts(E, KF, D)

        def load_experts(eng):
            for e in range(E):
                eng.dma_start(w1_sb[:, e], w1[e].rearrange("(k p) f -> p k f", p=P)).then_inc(w1_in, 16)
            for e in range(E):
                eng.dma_start(w2_sb[:, e], w2[e].rearrange("(k p) d -> p k d", p=P)).then_inc(w2_in, 16)

        with ExitStack() as seq:
            weights = Weights(lambda name, shape: sb_in(seq, name, shape), sem("weights_in"))
            setup_part(nc, sem, arena, ident_ready, ident, eps_col, bank, pair_a, ctx_in,
                       Wq, Wk, Wv, Wo, g_dram, u_dram,
                       lambda eng: weights.load(eng, W_in, dwk, pwk, cbias, W_x, W_dt, b_dt, A_log, D_skip,
                                                W_out, bo, wr, br))
            sequence_part(nc, sem, lambda name, shape: sb_in(seq, name, shape), arena, passed, ident, eps_col,
                          scores_all, bank, pair_a, pair_b, x_t, weights, load_experts,
                          g_dram, u_dram, bc_dram, x2_dram, xn3_dram)
        expert_part(nc, sem, sb_in, passed, ident, scores_all, bank, pair_a, pair_b, w1_sb, w2_sb, w1_in, w2_in,
                    b1, b2, x2_dram, xn3_dram, out_rows)


class Weights:
    LOADS = 12 + MB

    def __init__(self, sb, arrived):
        self.arrived = arrived
        self.w_in = sb("w_in", [P, KD, 2 * DI])
        self.pw = sb("pw", [P, MB, DI])
        self.w_x = sb("w_x", [P, MB, R + 2 * NS])
        self.w_dt = sb("w_dt", [R, DI])
        self.w_out = sb("w_out", [P, MB, D])
        self.taps = sb("taps", [P, MB, KC])
        self.conv_bias = sb("conv_bias", [P, MB])
        self.dt_bias = sb("dt_bias", [P, MB])
        self.d_skip = sb("d_skip", [P, MB])
        self.a_log = sb("a_log", [P, MB, NS])
        self.bo = sb("bo", [P, D])
        self.wr = sb("wr", [P, KD, E])
        self.br = sb("br", [P, E])

    def load(self, eng, W_in, dwk, pwk, cbias, W_x, W_dt, b_dt, A_log, D_skip, W_out, bo, wr, br):
        for dst, src in (
            (self.w_in, W_in.rearrange("(k p) n -> p k n", p=P)),
            (self.pw, pwk.rearrange("(k p) n -> p k n", p=P)),
            (self.w_x, W_x.rearrange("(k p) n -> p k n", p=P)),
            (self.w_dt, W_dt),
            (self.w_out, W_out.rearrange("(k p) n -> p k n", p=P)),
            (self.conv_bias, cbias.rearrange("(m p) -> p m", p=P)),
            (self.dt_bias, b_dt.rearrange("(m p) -> p m", p=P)),
            (self.d_skip, D_skip.rearrange("(m p) -> p m", p=P)),
            (self.a_log, A_log.rearrange("(m p) n -> p m n", p=P)),
            (self.bo, bo.partition_broadcast(P)),
            (self.wr, wr.rearrange("(k p) n -> p k n", p=P)),
            (self.br, br.partition_broadcast(P)),
        ):
            eng.dma_start(dst[:], src, allow_slow_non_contiguous=True).then_inc(self.arrived, 16)
        for m in range(MB):
            eng.dma_start(self.taps[:, m], dwk[:, m * P:(m + 1) * P].rearrange("k p -> p k"),
                          allow_slow_non_contiguous=True).then_inc(self.arrived, 16)


def setup_part(nc, sem, arena, ident_ready, ident, eps_col, bank, pair_a, ctx_in, Wq, Wk, Wv, Wo,
               g_dram, u_dram, load_weights):
    BM = B * M
    ctx_rows = ctx_in.rearrange("b m d -> (b m) d").rearrange("(k p) d -> p k d", p=P)
    part = Carver(arena)
    ctx_sb, ctxT = part(BM // P, D), part(KD, BM)
    wq_sb, wk_sb, wv_sb, wo_sb = part(KD, H * DH), part(KD, H * DH), part(KD, H * DH), part(HC, D)
    wqT = part(HC, D)
    k_diag, v_diag = part(HC, B, P), part(HC, B, P)
    g_sb, u_sb = part(2, H * M), part(2, 2 * D)

    ctx_in_s, wk_in, wv_in, wq_in, wo_in = (sem(n) for n in
                                           ("ctx_in", "wk_in", "wv_in", "wq_in", "wo_in"))
    ident_zero, diag_zero = sem("ident_zero"), sem("diag_zero")
    su_full, su_free = sem("su_full"), sem("su_free")
    g_full, g_evac = sem("g_full"), sem("g_evac")
    u_full, u_evac = sem("u_full"), sem("u_evac")
    g_stored = [sem("g_stored0"), sem("g_stored1")]
    u_stored = [sem("u_stored0"), sem("u_stored1")]

    WQT0 = KD
    KT0 = WQT0 + HC // 2
    VT0 = KT0 + HC

    with nc.Block() as block:
        @block.sync
        def _(sp):
            sp.dma_start(ctx_sb, ctx_rows).then_inc(ctx_in_s, 16)
            sp.dma_start(wq_sb, Wq.rearrange("(k p) n -> p k n", p=P)).then_inc(wq_in, 16)
            sp.dma_start(wk_sb, Wk.rearrange("(k p) n -> p k n", p=P)).then_inc(wk_in, 16)
            sp.dma_start(wv_sb, Wv.rearrange("(k p) n -> p k n", p=P)).then_inc(wv_in, 16)
            sp.dma_start(wo_sb, Wo.rearrange("(k p) n -> p k n", p=P)).then_inc(wo_in, 16)
            load_weights(sp)
            for n in range(B * KD):
                sp.wait_ge(g_evac, n + 1)
                b, k = n // KD, n % KD
                sp.dma_start(g_dram[b][:, k * H * M:(k + 1) * H * M],
                             g_sb[:, n % 2]).then_inc(g_stored[n % 2], 16)
            for n in range(B * HC // 2):
                sp.wait_ge(u_evac, n + 1)
                b, c2 = n // (HC // 2), n % (HC // 2)
                sp.dma_start(u_dram[b][:, c2 * 2 * D:(c2 + 1) * 2 * D],
                             u_sb[:, n % 2]).then_inc(u_stored[n % 2], 16)
            for p in range(2):
                sp.wait_ge(g_stored[p], 16 * (B * KD // 2))
                sp.wait_ge(u_stored[p], 16 * (B * HC // 4))

        @block.gpsimd
        def _(pool):
            nc.gpsimd.memset(ident[:], 0.0).then_inc(ident_zero, 1)
            pool.wait_ge(ident_zero, 1)
            nc.gpsimd.affine_select(out=ident[:], in_=ident[:], compare_op=ALU.not_equal, fill=1.0,
                                    base=0, pattern=[[-1, P]], channel_multiplier=1).then_inc(ident_ready, 1)

        @block.vector
        def _(dve):
            nc.vector.memset(eps_col[:], EPS)
            nc.vector.memset(k_diag, 0.0).then_inc(diag_zero, 1)
            nc.vector.memset(v_diag, 0.0).then_inc(diag_zero, 1)
            for n in range(B * KD):
                dve.wait_ge(g_full, n + 1)
                if n >= 2:
                    dve.wait_ge(g_stored[n % 2], 16 * (n // 2))
                nc.vector.tensor_copy(g_sb[:, n % 2], pair_a[:]).then_inc(g_evac, 1)

        @block.scalar
        def _(act):
            for k in range(KD):
                act.wait_ge(su_full, k + 1)
                nc.scalar.activation(ctxT[:, k], bank[k % 2][:, 0:BM], ACT.Copy).then_inc(su_free, 1)
            for i in range(HC // 2):
                act.wait_ge(su_full, WQT0 + i + 1)
                nc.scalar.activation(wqT[:, 2 * i:2 * i + 2].rearrange("p c d -> p (c d)"),
                                     bank[(WQT0 + i) % 2][:], ACT.Copy).then_inc(su_free, 1)
            act.wait_ge(diag_zero, 2)
            for which, (first, diag) in enumerate(((KT0, k_diag), (VT0, v_diag))):
                for c in range(HC):
                    act.wait_ge(su_full, first + c + 1)
                    src = bank[(first + c) % 2]
                    nc.scalar.activation(diag[0:DH, c, :, 0:M],
                                         src[0:DH, 0:BM].rearrange("p (b m) -> p b m", b=B), ACT.Copy)
                    nc.scalar.activation(diag[DH:P, c, :, M:P],
                                         src[DH:P, 0:BM].rearrange("p (b m) -> p b m", b=B),
                                         ACT.Copy).then_inc(su_free, 1)
            for n in range(B * HC // 2):
                act.wait_ge(u_full, n + 1)
                if n >= 2:
                    act.wait_ge(u_stored[n % 2], 16 * (n // 2))
                nc.scalar.activation(u_sb[:, n % 2], bank[2 + n % 2][:], ACT.Copy).then_inc(u_evac, 1)

        @block.tensor
        def _(pe):
            pe.wait_ge(ident_ready, 1)
            pe.wait_ge(ctx_in_s, 16)
            for k in range(KD):
                for t in range(BM // P):
                    last = nc.tensor.transpose(bank[k % 2][:, t * P:(t + 1) * P],
                                               ctx_sb[:, t, k * P:(k + 1) * P], ident[:])
                last.then_inc(su_full, 1)
            pe.wait_ge(wq_in, 16)
            for i in range(HC // 2):
                pe.wait_ge(su_free, WQT0 + i - 1)
                for c in range(2):
                    for k in range(KD):
                        last = nc.tensor.transpose(
                            bank[(WQT0 + i) % 2][:, (c * KD + k) * P:(c * KD + k + 1) * P],
                            wq_sb[:, k, (2 * i + c) * P:(2 * i + c + 1) * P], ident[:])
                last.then_inc(su_full, 1)
            for first, w, arrived in ((KT0, wk_sb, wk_in), (VT0, wv_sb, wv_in)):
                pe.wait_ge(arrived, 16)
                for c in range(HC):
                    pe.wait_ge(su_free, first + c - 1)
                    for k in range(KD):
                        last = nc.tensor.matmul(bank[(first + c) % 2][:, 0:BM], w[:, k, c * P:(c + 1) * P],
                                                ctxT[:, k], start=(k == 0), stop=(k == KD - 1))
                    last.then_inc(su_full, 1)
            pe.wait_ge(su_free, VT0 + HC)
            for n in range(B * KD):
                b, k = n // KD, n % KD
                if n:
                    pe.wait_ge(g_evac, n)
                for c in range(HC):
                    last = nc.tensor.matmul(pair_a[:, c * P:(c + 1) * P], wqT[:, c, k * P:(k + 1) * P],
                                            k_diag[:, c, b], start=True, stop=True)
                last.then_inc(g_full, 1)
            pe.wait_ge(wo_in, 16)
            for n in range(B * HC // 2):
                b, c2 = n // (HC // 2), n % (HC // 2)
                if n >= 2:
                    pe.wait_ge(u_evac, n - 1)
                for i in range(2):
                    c = 2 * c2 + i
                    last = nc.tensor.matmul(bank[2 + n % 2][:, i * D:(i + 1) * D], v_diag[:, c, b],
                                            wo_sb[:, c], start=True, stop=True)
                last.then_inc(u_full, 1)


def sequence_part(nc, sem, sb, arena, passed, ident, eps_col, scores_all, bank, pair_a, pair_b, x_t, weights,
                  load_experts, g_dram, u_dram, bc_dram, x2_dram, xn3_dram):
    W = weights
    a_exp = sb("a_exp", [P, MB, NS])
    a_neg = sb("a_neg", [P, MB, NS])
    g_sb = sb("g_att", [P, KD, H * M])
    u_sb = sb("u_att", [P, HC, D])
    part = Carver(arena)
    xa = part(TJ, D)
    xnT = part(2, KD, T)
    xp = part(MB, KC - 1 + T)
    cv = part(MB, T)
    delta = part(2, MB, T)
    u = part(MB, T)
    xc = part(MB, T)
    zg = part(MB, T)
    y_d = part(MB, T)
    y_g = part(MB, T)
    ring = part(RING, 2, T)
    dA = part(2, MB, T)
    hb = part(2, MB, T)
    xd = sb("xd", [R + 2 * NS, T])
    halo_cols = sb("halo_cols", [P, MB, KC - 1])
    carry = sb("carry", [P, NS, MB])
    xr = sb("xr", [P, 2, TJ, D])
    xn2 = sb("xn2", [P, TJ, D])
    xn2T = sb("xn2T", [P, 2, KD, P])
    probs = sb("probs", [P, 2, H * M])
    probsT = sb("probsT", [P, HC, P])
    xn3 = part(TJ, D)
    xn3T = probsT[:].rearrange("p c t -> p (c t)").rearrange("p (k t) -> p k t", k=KD)
    row_max = sb("row_max", [P, H])
    row_sum = sb("row_sum", [P, H])
    row_inv = sb("row_inv", [P, 2, H])

    class Norm:
        def __init__(self, name):
            self.stats = sb(name + "_stats", [P, TJ, 6])
            self.mv = sb(name + "_mv", [P, TJ, 2])
            self.ln = sb(name + "_ln", [P, TJ])
            self.r0 = sb(name + "_r0", [P, TJ])
            self.tmp = sb(name + "_tmp", [P, 3, TJ])
            self.rstd = sb(name + "_rstd", [P, TJ])
            self.shift = sb(name + "_shift", [P, TJ])
            self.dve = sem(name + "_dve")
            self.act = sem(name + "_act")
            self.done = sem(name + "_done")
    LN_DVE = 2 * TJ + 5
    norm1, norm2, norm3 = Norm("norm1"), Norm("norm2"), Norm("norm3")

    a_steps = sem("a_steps")
    xa_in, xr_in = sem("xa_in"), [sem("xr_in0"), sem("xr_in1")]
    mm_full, mm_free = sem("mm_full"), sem("mm_free")
    tb_full, tb_free = sem("tb_full"), sem("tb_free")
    ao_full, ao_free = sem("ao_full"), sem("ao_free")
    out_full = sem("out_full")
    x1_added = sem("x1_added")
    sc_full, sc_free = sem("sc_full"), sem("sc_free")
    et_full, et_free = sem("et_full"), sem("et_free")
    halo, conv = sem("halo"), sem("conv")
    xc_ready, zg_ready = sem("xc_ready"), sem("zg_ready")
    softplus_act, delta_ready, u_ready = sem("softplus_act"), sem("delta_ready"), sem("u_ready")
    bc_stored, ring_in = sem("bc_stored"), [sem(f"ring_in{s}") for s in range(RING)]
    yd_init = sem("yd_init")
    da_ready, dbu_ready, h_ready, carry_ready = (sem(n) for n in
                                                 ("da_ready", "dbu_ready", "h_ready", "carry_ready"))
    ch_ready, yd_added, yg_added = sem("ch_ready"), sem("yd_added"), sem("yg_added")
    y_sum, y_ready = sem("y_sum"), sem("y_ready")
    g_in, u_in = sem("g_in"), sem("u_in")
    bo_added = sem("bo_added")
    max_ready, exp_ready, sum_ready, inv_ready, probs_ready = (sem(n) for n in (
        "max_ready", "exp_ready", "sum_ready", "inv_ready", "probs_ready"))
    x2_stored, xn3_stored = [sem("x2_stored0"), sem("x2_stored1")], sem("xn3_stored")

    mm, tb, ao = bank[0:2], bank[2], bank[3]
    YG = len(GP_ADDS)
    dve_adds = [n for n in range(1, NS) if n not in GP_ADDS]
    YD = len(dve_adds)
    CONV = MB * KC + 1
    SOFTPLUS = MB + 2

    MM = KD + 4 * MB

    def mm_z(c):
        missing = KD + MB if isinstance(c, int) and c == NC - 1 else 0
        return MM * c + 2 * (KD + 2 * MB) - missing

    def mm_pw(f):
        return MM * f + KD + MB

    def mm_dt(f):
        return mm_pw(f) + MB

    def mm_tr(g):
        return 0 if isinstance(g, int) and g == 0 else MM * g - MB

    def mm_x(g):
        return mm_tr(g) + KD

    TB = TJ + 1 + KD + 1

    def tb_less(a, before_last, last):
        return {NC - 2: before_last, NC - 1: last}.get(a, 0) if isinstance(a, int) else 0

    def tb_bc(f):
        return f if isinstance(f, int) and f < 2 else TB * (f - 2) + 2 + TJ

    def tb_ln2(a, j):
        return TB * a + 2 + j - tb_less(a, 0, 1)

    def tb_ln3(a, i):
        return TB * a + 3 + TJ + i - tb_less(a, 1, 2)

    def pa_out(c):
        return (1 + TJ) * c

    def pa_scores(a, j):
        return (1 + TJ) * a + 1 + j

    def schedule(eng, step):
        step(-2, -1, True, False, False, False, True)
        step(-1, -1, False, False, False, True, True)
        step(0, 0, True, True, False, True, True)
        with eng.Fori(0, B - 2) as b:
            step(2 * b + 1, b, False, True, True, True, True)
            step(2 * b + 2, b + 1, True, True, True, True, True)
        step(NC - 3, NC // 2 - 2, False, True, True, True, True)
        step(NC - 2, NC // 2 - 1, True, True, True, True, False)
        step(NC - 1, NC // 2 - 1, False, True, True, False, False)
        step(NC, NC // 2, True, False, True, False, False)


    with nc.Block() as block:
        @block.sync
        def _(sp):
            def load_ring(c, n, par):
                wait_apart(sp, ch_ready, NS * c + n - RING + 1, passed[0])
                src = bc_dram[par].rearrange("(g n) t -> g n t", n=NS)[:, n, :]
                sp.dma_start(ring[:, n % RING], src.partition_broadcast(P)).then_inc(ring_in[n % RING], 16)

            def step(c, half, starts, scan, att, conv_part, proj):
                a, f, g, par, other = c - 1, c + 1, c + 2, 0 if starts else 1, 1 if starts else 0
                if proj:
                    if not (isinstance(g, int) and g == 0):
                        wait_apart(sp, mm_full, mm_tr(f) + KD, passed[0])
                    sp.dma_start(xa, x_t[:, bass.ds(TJ * g, TJ), :]).then_inc(xa_in, 16)
                if scan:
                    wait_apart(sp, x2_stored[par], 16 * half + 16, passed[0])
                    wait_apart(sp, norm3.done, TJ * c + TJ, passed[0])
                    sp.dma_start(xr[:, par], x_t[:, bass.ds(TJ * c, TJ), :]).then_inc(xr_in[par], 16)
                    for n in range(RING, NS):
                        load_ring(c, n, par)
                if conv_part:
                    wait_apart(sp, tb_free, tb_bc(f) + 2, passed[0])
                    sp.dma_start(bc_dram[other], xd[R:R + 2 * NS, :]).then_inc(bc_stored, 16)
                    wait_apart(sp, bc_stored, 16 * f + 16, passed[0])
                    for n in range(RING):
                        load_ring(f, n, other)
                if scan and starts:
                    wait_apart(sp, sc_full, TJ * c, passed[0])
                    sp.dma_start(g_sb[:], g_dram[bass.ds(half, 1)].rearrange(
                        "o p (k n) -> (o p) k n", k=KD)).then_inc(g_in, 16)
                    wait_apart(sp, ao_full, TJ * c, passed[0])
                    sp.dma_start(u_sb[:], u_dram[bass.ds(half, 1)].rearrange(
                        "o p (k n) -> (o p) k n", k=HC)).then_inc(u_in, 16)
                if att:
                    wait_apart(sp, ao_free, TJ * a + TJ + 1, passed[0])
                    sp.dma_start(x2_dram[:, bass.ds(TJ * a, TJ), :], xr[:, other]).then_inc(x2_stored[other], 16)
                    wait_apart(sp, norm3.done, TJ * a + 3 * TJ, passed[0])
                    sp.dma_start(xn3_dram[:, bass.ds(TJ * a, TJ), :], xn3).then_inc(xn3_stored, 16)

            schedule(sp, step)
            sp.wait_ge(x2_stored[0], 16 * (NC // 2 + 1))
            sp.wait_ge(x2_stored[1], 16 * (NC // 2 + 1))
            sp.wait_ge(xn3_stored, 16 * (NC + 1))

        @block.gpsimd
        def _(pool):
            pool.sem_inc(mm_free, 2)
            pool.sem_inc(tb_free, 1)
            pool.sem_inc(ao_free, 1)
            pool.sem_inc(sc_free, 1)
            pool.sem_inc(et_free, 1)
            pool.sem_inc(et_full, 2)
            pool.sem_inc(x2_stored[0], 16)
            pool.sem_inc(x2_stored[1], 16)
            pool.sem_inc(xn3_stored, 16)
            pool.sem_inc(norm3.done, 2 * TJ)
            pool.wait_ge(W.arrived, 16 * W.LOADS)

            def wait_left(c, n):
                if isinstance(c, int) and c < 0:
                    return
                if n == 0:
                    pool.wait_ge(ch_ready, NS * c + 1)
                elif n in GP_ADDS:
                    pool.wait_ge(yg_added, YG * c + GP_ADDS.index(n) + 1)
                else:
                    pool.wait_ge(yd_added, YD * c + dve_adds.index(n) + 1)

            def step(c, half, starts, scan, att, conv_part, proj):
                a, f, g, par, other = c - 1, c + 1, c + 2, 0 if starts else 1, 1 if starts else 0

                def dbu(c, n):
                    if n >= 2:
                        wait_left(c, n - 2)
                    else:
                        pool.wait_ge(u_ready, c + 1)
                        wait_left(c - 1, NS + n - 2)
                    pool.wait_ge(ring_in[n % RING], 16 * (2 * c + n // RING + 1))
                    nc.gpsimd.tensor_tensor(hb[:, n % 2], u, ring[:, n % RING, 0:1, :].broadcast_to([P, MB, T]),
                                            ALU.mult).then_inc(dbu_ready, 1)

                def add_up(n):
                    pool.wait_ge(ch_ready, NS * c + n + 1)
                    wait(pool, yg_added, YG * c + GP_ADDS.index(n))
                    nc.gpsimd.tensor_tensor(y_g, y_g, hb[:, n % 2], ALU.add).then_inc(yg_added, 1)

                def probabilities(j):
                    if not att:
                        return
                    pool.wait_ge(inv_ready, TJ * a + j + 1)
                    e3 = probs[:, j % 2].rearrange("p (h m) -> p h m", m=M)
                    nc.gpsimd.tensor_tensor(e3, e3, row_inv[:, j % 2, :, None].broadcast_to([P, H, M]),
                                            ALU.mult).then_inc(probs_ready, 1)

                if scan:
                    add_up(1)
                    dbu(c, 3)
                probabilities(0)
                if scan:
                    add_up(2)
                    dbu(c, 4)
                probabilities(1)
                if scan:
                    add_up(3)
                    dbu(c, 5)
                    add_up(4)
                    dbu(c, 6)
                if proj:
                    wait_apart(pool, norm1.dve, LN_DVE * g + LN_DVE, passed[1])
                    for j in range(TJ):
                        nc.gpsimd.tensor_scalar(xa[:, j], xa[:, j], norm1.rstd[:, j:j + 1],
                                                norm1.shift[:, j:j + 1], ALU.mult, ALU.add).then_inc(norm1.done, 1)
                if scan:
                    dbu(c, 7)
                probabilities(2)
                if scan:
                    add_up(6)
                probabilities(3)
                if conv_part:
                    pool.wait_ge(delta_ready, f + 1)
                    wait(pool, dbu_ready, NS * f)
                    nc.gpsimd.tensor_tensor(u, delta[:, other], xc, ALU.mult).then_inc(u_ready, 1)
                    dbu(f, 0)
                    dbu(f, 1)
                    dbu(f, 2)
                if scan:
                    pool.wait_ge(norm2.done, TJ * c + TJ)
                    nc.gpsimd.tensor_tensor(xr[:, par], xr[:, par],
                                            W.bo[:, None, :].broadcast_to([P, TJ, D]),
                                            ALU.add).then_inc(bo_added, 1)

            schedule(pool, step)

        @block.scalar
        def _(act):
            act.wait_ge(W.arrived, 16 * W.LOADS)
            nc.scalar.activation(a_exp[:], W.a_log[:], ACT.Exp).then_inc(a_steps, 1)
            act.wait_ge(a_steps, 1)
            nc.scalar.mul(a_neg[:], a_exp[:], -1.0).then_inc(a_steps, 1)
            act.wait_ge(a_steps, 2)

            def load_tables():
                nc.scalar.preload_act_table_set("natural_log_exp_and_others")

            def rstd_start(n, base):
                act.wait_ge(n.dve, LN_DVE * base + 2 * TJ)
                nc.scalar.activation(n.ln[:], n.mv[:, :, 1], ACT.Ln, bias=eps_col[:, 0:1]).then_inc(n.act, 1)
                act.wait_ge(n.act, 2 * base + 1)
                nc.scalar.activation(n.r0[:], n.ln[:], ACT.Exp, scale=-0.5).then_inc(n.act, 1)

            def normalise(n, base, src, dst):
                act.wait_ge(n.dve, LN_DVE * base + LN_DVE)
                for j in range(TJ):
                    nc.scalar.activation(dst[:, j], src[:, j], ACT.Identity, scale=n.rstd[:, j:j + 1],
                                         bias=n.shift[:, j:j + 1]).then_inc(n.done, 1)

            def step(c, half, starts, scan, att, conv_part, proj):
                a, f, g, par, other = c - 1, c + 1, c + 2, 0 if starts else 1, 1 if starts else 0

                def decay(c, n, parity):
                    wait(act, h_ready, MB * (NS * c + n - 1))
                    for m in range(MB):
                        nc.scalar.activation(dA[:, n % 2, m], delta[:, parity, m], ACT.Exp,
                                             scale=a_neg[:, m, n:n + 1]).then_inc(da_ready, 1)

                def decays(n):
                    if scan:
                        decay(c, n, par)

                def z_out():
                    wait(act, y_ready, f)
                    for m in range(MB):
                        act.wait_ge(mm_full, mm_z(f) + m + 1)
                        nc.scalar.activation(zg[:, m], mm[m % 2][:], ACT.Copy).then_inc(mm_free, 1)

                def ln2_turned(a, j):
                    act.wait_ge(tb_full, tb_ln2(a, j) + 1)
                    nc.scalar.activation(xn2T[:, j % 2].rearrange("p k t -> p (k t)"), tb[:, 0:KD * P],
                                         ACT.Copy).then_inc(tb_free, 1)

                def exponentials(j):
                    if not att:
                        return
                    act.wait_ge(sc_free, pa_scores(a, j) + 2)
                    nc.scalar.activation(probs[:, j % 2], probs[:, j % 2], ACT.Exp, scale=SCALE).then_inc(exp_ready, 1)

                def probs_turned(j):
                    if not att:
                        return
                    act.wait_ge(et_full, TJ * a + j + 3)
                    wait(act, ao_full, TJ * a + j)
                    nc.scalar.activation(probsT[:].rearrange("p c t -> p (c t)"), pair_b[:],
                                         ACT.Copy).then_inc(et_free, 1)

                def ln1_turned():
                    for k in range(KD):
                        act.wait_ge(mm_full, mm_tr(g) + k + 1)
                        nc.scalar.activation(xnT[:, par, k], mm[k % 2][:], ACT.Copy).then_inc(mm_free, 1)

                def x_in_out(blocks):
                    if 0 in blocks:
                        wait(act, halo, g)
                    for m in blocks:
                        act.wait_ge(mm_full, mm_x(g) + m + 1)
                        nc.scalar.activation(xp[:, m, KC - 1:], mm[m % 2][:], ACT.Copy).then_inc(mm_free, 1)

                def pointwise_out(blocks):
                    if 0 in blocks:
                        wait(act, u_ready, f)
                        wait(act, yd_init, MB * f)
                    for m in blocks:
                        act.wait_ge(mm_full, mm_pw(f) + m + 1)
                        nc.scalar.activation(xc[:, m], mm[m % 2][:], ACT.Identity,
                                             bias=W.conv_bias[:, m:m + 1]).then_inc(mm_free, 1)

                def silu_z():
                    act.wait_ge(mm_free, mm_z(c) + MB + 2)
                    nc.scalar.activation(zg, zg, ACT.Silu).then_inc(zg_ready, 1)

                def silu_x():
                    act.wait_ge(mm_free, mm_pw(f) + MB + 2)
                    nc.scalar.activation(xc, xc, ACT.Silu).then_inc(xc_ready, 1)

                def low_rank_out():
                    wait(act, bc_stored, 16 * f)
                    act.wait_ge(tb_full, tb_bc(f) + 1)
                    nc.scalar.activation(xd[:], tb[0:R + 2 * NS, :], ACT.Copy).then_inc(tb_free, 1)

                def softplus_in():
                    wait(act, da_ready, MB * NS * c)
                    for m in range(MB):
                        act.wait_ge(mm_full, mm_dt(f) + m + 1)
                        src = mm[m % 2]
                        nc.scalar.activation(cv[:, m], src[:], ACT.Abs,
                                             bias=W.dt_bias[:, m:m + 1]).then_inc(softplus_act, 1)
                        nc.scalar.activation(delta[:, other, m], src[:], ACT.Relu,
                                             bias=W.dt_bias[:, m:m + 1]).then_inc(mm_free, 1)

                def softplus_out():
                    act.wait_ge(softplus_act, SOFTPLUS * f + MB)
                    nc.scalar.activation(cv, cv, ACT.Exp, scale=-1.0).then_inc(softplus_act, 1)
                    act.wait_ge(softplus_act, SOFTPLUS * f + MB + 1)
                    nc.scalar.activation(cv, cv, ACT.Ln, bias=1.0).then_inc(softplus_act, 1)

                load_tables()
                if att and not scan:
                    act.wait_ge(out_full, 2 * NC)
                    load_experts(act)
                decays(2)
                exponentials(0)
                if att:
                    ln2_turned(a, 1)
                decays(3)
                probs_turned(0)
                if att:
                    ln2_turned(a, 2)
                decays(4)
                exponentials(1)
                if conv_part:
                    pointwise_out((0,))
                decays(5)
                if conv_part:
                    pointwise_out((1,))
                if proj:
                    rstd_start(norm1, g)
                if scan:
                    silu_z()
                probs_turned(1)
                if att:
                    ln2_turned(a, 3)
                if conv_part:
                    pointwise_out((2, 3))
                    silu_x()
                load_tables()
                decays(6)
                exponentials(2)
                if conv_part:
                    low_rank_out()
                decays(7)
                if conv_part:
                    softplus_in()
                if proj:
                    ln1_turned()
                exponentials(3)
                if conv_part:
                    softplus_out()
                if proj:
                    x_in_out((0, 1))
                probs_turned(2)
                probs_turned(3)
                if proj:
                    x_in_out((2, 3))
                if conv_part:
                    act.wait_ge(delta_ready, f + 1)
                    decay(f, 0, other)
                    decay(f, 1, other)
                if att:
                    rstd_start(norm3, a)
                    act.wait_ge(xn3_stored, 16 * a + 16)
                    normalise(norm3, a, xr[:, other], xn3)
                if conv_part:
                    wait(act, out_full, 2 * f)
                    for m in range(MB):
                        nc.scalar.activation(y_d[:, m], xc[:, m], ACT.Copy,
                                             scale=W.d_skip[:, m:m + 1]).then_inc(yd_init, 1)
                if att:
                    for k in range(KD):
                        act.wait_ge(tb_full, tb_ln3(a, k) + 1)
                        nc.scalar.activation(xn3T[:, k], tb[:], ACT.Copy).then_inc(tb_free, 1)
                if scan:
                    rstd_start(norm2, c)
                    normalise(norm2, c, xr[:, par], xn2)
                    ln2_turned(c, 0)
                if conv_part:
                    z_out()

            schedule(act, step)

        @block.vector
        def _(dve):
            dve.wait_ge(W.arrived, 16 * W.LOADS)

            def statistics(n, base, src):
                for j in range(TJ):
                    nc.vector.bn_stats(n.stats[:, j], src[:, j]).then_inc(n.dve, 1)
                wait_apart(dve, n.dve, LN_DVE * base + TJ, passed[2])
                for j in range(TJ):
                    nc.vector.bn_aggr(n.mv[:, j], n.stats[:, j]).then_inc(n.dve, 1)

            def refine(n, base):
                at = LN_DVE * base + 2 * TJ
                dve.wait_ge(n.dve, at)
                dve.wait_ge(n.act, 2 * base + 2)
                nc.vector.scalar_tensor_tensor(out=n.tmp[:, 0], in0=n.mv[:, :, 1], scalar=EPS, in1=n.r0[:],
                                               op0=ALU.add, op1=ALU.mult).then_inc(n.dve, 1)
                dve.wait_ge(n.dve, at + 1)
                nc.vector.tensor_tensor(n.tmp[:, 1], n.tmp[:, 0], n.r0[:], ALU.mult).then_inc(n.dve, 1)
                dve.wait_ge(n.dve, at + 2)
                nc.vector.tensor_scalar(n.tmp[:, 2], n.tmp[:, 1], -0.5, 1.5, ALU.mult, ALU.add).then_inc(n.dve, 1)
                dve.wait_ge(n.dve, at + 3)
                nc.vector.tensor_tensor(n.rstd[:], n.tmp[:, 2], n.r0[:], ALU.mult).then_inc(n.dve, 1)
                dve.wait_ge(n.dve, at + 4)
                nc.vector.scalar_tensor_tensor(out=n.shift[:], in0=n.mv[:, :, 0], scalar=-1.0, in1=n.rstd[:],
                                               op0=ALU.mult, op1=ALU.mult).then_inc(n.dve, 1)

            def step(c, half, starts, scan, att, conv_part, proj):
                a, f, g, par, other = c - 1, c + 1, c + 2, 0 if starts else 1, 1 if starts else 0

                def scan_state(c, n, starts):
                    if n == 0:
                        wait(dve, carry_ready, NS * c)
                    dve.wait_ge(dbu_ready, NS * c + n + 1)
                    for m in range(MB):
                        dve.wait_ge(da_ready, MB * (NS * c + n) + m + 1)
                        nc.vector.tensor_tensor_scan(
                            hb[:, n % 2, m], dA[:, n % 2, m], hb[:, n % 2, m],
                            0.0 if starts else carry[:, n, m:m + 1], ALU.mult, ALU.add).then_inc(h_ready, 1)
                    dve.wait_ge(h_ready, MB * (NS * c + n) + MB)
                    nc.vector.tensor_copy(carry[:, n], hb[:, n % 2, :, T - 1]).then_inc(carry_ready, 1)
                    dst = y_g if n == 0 else hb[:, n % 2]
                    dve.wait_ge(carry_ready, NS * c + n + 1)
                    nc.vector.tensor_tensor(dst, hb[:, n % 2], ring[:, n % RING, 1:2, :].broadcast_to([P, MB, T]),
                                            ALU.mult).then_inc(ch_ready, 1)
                    if n in dve_adds:
                        i = dve_adds.index(n)
                        if i == 0:
                            dve.wait_ge(yd_init, MB * (c + 1))
                        wait(dve, yd_added, YD * c + i)
                        dve.wait_ge(ch_ready, NS * c + n + 1)
                        nc.vector.tensor_tensor(y_d, y_d, hb[:, n % 2], ALU.add).then_inc(yd_added, 1)

                def less_max(j):
                    if not att:
                        return
                    dve.wait_ge(sc_full, TJ * a + j + 1)
                    s3 = pair_a[:].rearrange("p (h m) -> p h m", m=M)
                    nc.vector.tensor_reduce(row_max[:], s3, AX.X, ALU.max).then_inc(max_ready, 1)
                    dve.wait_ge(max_ready, TJ * a + j + 1)
                    dve.wait_ge(et_full, TJ * a + j + 1)
                    nc.vector.tensor_tensor(probs[:, j % 2].rearrange("p (h m) -> p h m", m=M), s3,
                                            row_max[:, :, None].broadcast_to([P, H, M]),
                                            ALU.subtract).then_inc(sc_free, 1)

                def row_sums(j):
                    if not att:
                        return
                    dve.wait_ge(exp_ready, TJ * a + j + 1)
                    nc.vector.tensor_reduce(row_sum[:], probs[:, j % 2].rearrange("p (h m) -> p h m", m=M),
                                            AX.X, ALU.add).then_inc(sum_ready, 1)
                    dve.wait_ge(sum_ready, TJ * a + j + 1)
                    nc.vector.reciprocal(row_inv[:, j % 2], row_sum[:]).then_inc(inv_ready, 1)

                def residual(j):
                    if not att:
                        return
                    if j == 0:
                        dve.wait_ge(bo_added, a + 1)
                    dve.wait_ge(ao_full, TJ * a + j + 1)
                    nc.vector.tensor_tensor(xr[:, other, j], ao[:, 0:D], xr[:, other, j], ALU.add).then_inc(ao_free, 1)

                def convolve(blocks, base):
                    for k in range(KC):
                        for i, m in enumerate(blocks):
                            src = xp[:, m, k:k + T]
                            if k == 0:
                                dve.wait_ge(mm_free, mm_x(f) + m + 3)
                                op = nc.vector.tensor_scalar(cv[:, m], src, W.taps[:, m, 0:1], None, ALU.mult)
                            else:
                                dve.wait_ge(conv, CONV * f + base + len(blocks) * (k - 1) + i + 1)
                                op = nc.vector.scalar_tensor_tensor(
                                    out=cv[:, m], in0=src, scalar=W.taps[:, m, k:k + 1], in1=cv[:, m],
                                    op0=ALU.mult, op1=ALU.add)
                            op.then_inc(conv, 1)

                def state(n):
                    if scan:
                        scan_state(c, n, starts)

                less_max(0)
                if conv_part:
                    wait(dve, halo, f)
                    if starts:
                        nc.vector.tensor_copy(xp[:, :, 0:KC - 1], halo_cols[:]).then_inc(conv, 1)
                    else:
                        nc.vector.memset(xp[:, :, 0:KC - 1], 0.0).then_inc(conv, 1)
                    dve.wait_ge(conv, CONV * f + 1)
                    wait(dve, delta_ready, f)
                    convolve((0, 1), 1)
                row_sums(0)
                state(2)
                if conv_part:
                    convolve((2, 3), 1 + 2 * KC)
                    nc.vector.tensor_copy(halo_cols[:], xp[:, :, T:T + KC - 1]).then_inc(halo, 1)
                less_max(1)
                state(3)
                row_sums(1)
                residual(0)
                if proj:
                    dve.wait_ge(xa_in, 16 * g + 16)
                    wait(dve, norm1.done, TJ * g)
                    statistics(norm1, g, xa)
                state(4)
                less_max(2)
                if proj:
                    refine(norm1, g)
                state(5)
                row_sums(2)
                less_max(3)
                state(6)
                row_sums(3)
                residual(1)
                state(7)
                if conv_part:
                    dve.wait_ge(softplus_act, SOFTPLUS * (f + 1))
                    dve.wait_ge(mm_free, mm_dt(f) + MB + 2)
                    nc.vector.tensor_tensor(delta[:, other], delta[:, other], cv, ALU.add).then_inc(delta_ready, 1)
                residual(2)
                if scan:
                    dve.wait_ge(yg_added, YG * (c + 1))
                    dve.wait_ge(yd_added, YD * (c + 1))
                    nc.vector.tensor_tensor(y_d, y_d, y_g, ALU.add).then_inc(y_sum, 1)
                    dve.wait_ge(y_sum, c + 1)
                    dve.wait_ge(zg_ready, c + 1)
                    nc.vector.tensor_tensor(y_d, y_d, zg, ALU.mult).then_inc(y_ready, 1)
                residual(3)
                if att:
                    dve.wait_ge(ao_free, TJ * a + TJ + 1)
                    statistics(norm3, a, xr[:, other])
                    refine(norm3, a)
                if conv_part:
                    scan_state(f, 0, not starts)
                if scan:
                    dve.wait_ge(xr_in[par], 16 * half + 16)
                    for i in range(2):
                        two = xr[:, par, 2 * i:2 * i + 2]
                        dve.wait_ge(out_full, 2 * c + i + 1)
                        op = nc.vector.tensor_tensor(two, pair_a[:, 512 * i:512 * (i + 1)].rearrange(
                            "p (j d) -> p j d", d=D), two, ALU.add)
                        op.then_inc(sc_free if i else x1_added, 1)
                    dve.wait_ge(x1_added, c + 1)
                    dve.wait_ge(sc_free, pa_out(c) + 2)
                    statistics(norm2, c, xr[:, par])
                    refine(norm2, c)
                if att:
                    dve.wait_ge(tb_full, tb_ln3(a, KD) + 1)
                    nc.vector.tensor_tensor(scores_all[:, bass.ds(TJ * a, TJ), :],
                                            tb[:, 0:TJ * E].rearrange("p (j e) -> p j e", e=E),
                                            W.br[:, None, :].broadcast_to([P, TJ, E]),
                                            ALU.add).then_inc(tb_free, 1)
                if conv_part:
                    scan_state(f, 1, not starts)

            schedule(dve, step)

        @block.tensor
        def _(pe):
            pe.wait_ge(W.arrived, 16 * W.LOADS)

            def step(c, half, starts, scan, att, conv_part, proj):
                a, f, g, par, other = c - 1, c + 1, c + 2, 0 if starts else 1, 1 if starts else 0

                def mm_take(first, m):
                    pe.wait_ge(mm_free, first + m + 1)
                    return mm[m % 2]

                def ln2_turn(a, j):
                    pe.wait_ge(norm2.done, TJ * a + j + 1)
                    pe.wait_ge(tb_free, tb_ln2(a, j) + 1)
                    for k in range(KD):
                        last = nc.tensor.transpose(tb[:, k * P:(k + 1) * P], xn2[:, j, k * P:(k + 1) * P], ident[:])
                    last.then_inc(tb_full, 1)

                def scores(a, j):
                    pe.wait_ge(tb_free, tb_ln2(a, j) + 2)
                    pe.wait_ge(sc_free, pa_scores(a, j) + 1)
                    for half_n in range(2):
                        for k in range(KD):
                            last = nc.tensor.matmul(pair_a[:, half_n * 512:(half_n + 1) * 512],
                                                    xn2T[:, j % 2, k], g_sb[:, k, half_n * 512:(half_n + 1) * 512],
                                                    start=(k == 0), stop=(k == KD - 1))
                    last.then_inc(sc_full, 1)

                def x_in(blocks):
                    if 0 in blocks:
                        pe.wait_ge(mm_free, mm_tr(g) + KD + 2)
                    for m in blocks:
                        dst = mm_take(mm_x(g), m)
                        for k in range(KD):
                            last = nc.tensor.matmul(dst[:], W.w_in[:, k, m * P:(m + 1) * P], xnT[:, par, k],
                                                    start=(k == 0), stop=(k == KD - 1))
                        last.then_inc(mm_full, 1)

                def z_in(blocks):
                    for m in blocks:
                        dst = mm_take(mm_z(f), m)
                        for k in range(KD):
                            last = nc.tensor.matmul(dst[:], W.w_in[:, k, DI + m * P:DI + (m + 1) * P],
                                                    xnT[:, other, k], start=(k == 0), stop=(k == KD - 1))
                        last.then_inc(mm_full, 1)

                def turn_probs(j):
                    if not att:
                        return
                    pe.wait_ge(probs_ready, TJ * a + j + 1)
                    pe.wait_ge(et_free, TJ * a + j + 1)
                    for hc in range(HC):
                        last = nc.tensor.transpose(pair_b[:, hc * P:(hc + 1) * P],
                                                   probs[:, j % 2, hc * P:(hc + 1) * P], ident[:])
                    last.then_inc(et_full, 1)

                def attend(j):
                    if not att:
                        return
                    pe.wait_ge(et_free, TJ * a + j + 2)
                    pe.wait_ge(ao_free, TJ * a + j + 1)
                    for hc in range(HC):
                        last = nc.tensor.matmul(ao[:, 0:D], probsT[:, hc], u_sb[:, hc],
                                                start=(hc == 0), stop=(hc == HC - 1))
                    last.then_inc(ao_full, 1)

                if att:
                    ln2_turn(a, 1)
                    scores(a, 1)
                    if not starts:
                        pe.wait_ge(u_in, 16 * half + 16)
                turn_probs(0)
                if att:
                    ln2_turn(a, 2)
                attend(0)
                if conv_part:
                    pe.wait_ge(conv, CONV * (f + 1))
                for m in range(MB):
                    if att and m == 2:
                        scores(a, 2)
                        turn_probs(1)
                        ln2_turn(a, 3)
                    if conv_part:
                        dst = mm_take(mm_pw(f), m)
                        for k in range(MB):
                            last = nc.tensor.matmul(dst[:], W.pw[:, k, m * P:(m + 1) * P], cv[:, k],
                                                    start=(k == 0), stop=(k == MB - 1))
                        last.then_inc(mm_full, 1)
                attend(1)
                if conv_part:
                    pe.wait_ge(xc_ready, f + 1)
                    pe.wait_ge(tb_free, tb_bc(f) + 1)
                    for k in range(MB):
                        last = nc.tensor.matmul(tb[0:R + 2 * NS, :], W.w_x[:, k], xc[:, k],
                                                start=(k == 0), stop=(k == MB - 1))
                    last.then_inc(tb_full, 1)
                if att:
                    scores(a, 3)
                if conv_part:
                    pe.wait_ge(tb_free, tb_bc(f) + 2)
                    for m in range(MB):
                        nc.tensor.matmul(mm_take(mm_dt(f), m)[:], W.w_dt[:, m * P:(m + 1) * P], xd[0:R, :],
                                         start=True, stop=True).then_inc(mm_full, 1)
                if proj:
                    pe.wait_ge(norm1.done, TJ * g + TJ)
                    for k in range(KD):
                        dst = mm_take(mm_tr(g), k)
                        for j in range(TJ):
                            last = nc.tensor.transpose(dst[:, j * P:(j + 1) * P], xa[:, j, k * P:(k + 1) * P],
                                                       ident[:])
                        last.then_inc(mm_full, 1)
                    x_in((0, 1))
                turn_probs(2)
                attend(2)
                turn_probs(3)
                if proj:
                    x_in((2, 3))
                attend(3)
                if scan:
                    pe.wait_ge(y_ready, c + 1)
                    pe.wait_ge(sc_free, pa_out(c) + 1)
                    for j in range(TJ):
                        for k in range(MB):
                            last = nc.tensor.matmul(pair_a[:, j * D:(j + 1) * D], y_d[:, k, j * P:(j + 1) * P],
                                                    W.w_out[:, k], start=(k == 0), stop=(k == MB - 1))
                        if j % 2:
                            last.then_inc(out_full, 1)
                if conv_part:
                    z_in((0, 1))
                if att:
                    pe.wait_ge(norm3.done, TJ * a + 3 * TJ)
                    for k in range(KD):
                        pe.wait_ge(tb_free, tb_ln3(a, k) + 1)
                        for j in range(TJ):
                            last = nc.tensor.transpose(tb[:, j * P:(j + 1) * P], xn3[:, j, k * P:(k + 1) * P],
                                                       ident[:])
                        last.then_inc(tb_full, 1)
                    pe.wait_ge(tb_free, tb_ln3(a, KD) + 1)
                    for j in range(TJ):
                        for k in range(KD):
                            last = nc.tensor.matmul(tb[:, j * E:(j + 1) * E], xn3T[:, k, j * P:(j + 1) * P],
                                                    W.wr[:, k], start=(k == 0), stop=(k == KD - 1))
                    last.then_inc(tb_full, 1)
                if scan:
                    ln2_turn(c, 0)
                    if starts:
                        pe.wait_ge(g_in, 16 * half + 16)
                    scores(c, 0)
                if conv_part:
                    z_in((2, 3))

            schedule(pe, step)


def expert_part(nc, sem, sb_in, passed, ident, scores_all, bank, pair_a, pair_b, w1_sb, w2_sb, w1_in, w2_in,
                b1, b2, x2_dram, xn3_dram, out_rows):
    x2_rows = x2_dram.rearrange("p t d -> (p t) d")
    xn3_rows = xn3_dram.rearrange("p t d -> (p t) d")
    with ExitStack() as st:
        def sb(name, shape, dt=F32):
            return sb_in(st, name, shape, dt)

        tile_expert = sb("tile_expert", [P, NT], I32)
        get_row = sb("get_row", [P, NT], U32)
        put_row = sb("put_row", [P, NT], U32)
        b1_sb = sb("b1_sb", [P, E, KF])
        b2_sb = sb("b2_sb", [P, E, D])
        bias_in = sem("bias_in")
        consts, const_steps, route = sem("route_consts"), sem("const_steps"), sem("route_steps")
        counts_ready, cols_ready, rows_ready = sem("counts_ready"), sem("cols_ready"), sem("rows_ready")

        with ExitStack() as rt:
            def rb(name, shape, dt=F32):
                return sb_in(rt, name, shape, dt)

            e_less = rb("e_less", [P, TT, E])
            tri = rb("tri", [P, P])
            ones = rb("ones", [P, P])
            k128 = rb("k128", [P, E, TT])
            tile_no = rb("tile_no", [P, NT, E])
            edges = rb("edges", [P, NT + 1])
            col_no = rb("col_no", [P, P])
            part_no = rb("part_no", [P, 1])
            tt_no = rb("tt_no", [P, TT])
            best = rb("best", [P, TT])
            is_best = rb("is_best", [P, TT, E])
            pick = rb("pick", [P, TT, E])
            first = rb("first", [P, TT])
            onehot = rb("onehot", [P, TT, E])
            within = rb("within", [P, TT, E])
            total = rb("total", [P, E, TT])
            upto = rb("upto", [P, E, TT])
            more = rb("more", [P, E, TT])
            tiles = rb("tiles", [P, E])
            tiles_end = rb("tiles_end", [P, E])
            base = rb("base", [P, E])
            offs = rb("offs", [P, TT, E])
            slot = rb("slot", [P, TT])
            past = rb("past", [P, NT, E])
            expert_f = rb("expert_f", [P, NT])
            expert_c = rb("expert_c", [P, NT])
            reached = rb("reached", [P, TT, NT + 1])
            tiles_to = rb("tiles_to", [P, TT])
            start = rb("start", [P, TT])
            place = rb("place", [P, TT])
            at_place = rb("at_place", [P, TT, P], BF16)
            at_tile = rb("at_tile", [P, TT, 3, NT], BF16)
            found = rb("found", [P, 3, NT])
            get_f = rb("get_f", [P, NT])
            put_f = rb("put_f", [P, NT])
            skip_f = rb("skip_f", [P, NT])

            STEPS_TILE = 19 + E

            with nc.Block() as block:
                @block.sync
                def _(sp):
                    sp.dma_start(b1_sb[:], b1.rearrange("e (k p) -> p e k", p=P),
                                 allow_slow_non_contiguous=True).then_inc(bias_in, 16)
                    sp.dma_start(b2_sb[:], b2.partition_broadcast(P)).then_inc(bias_in, 16)
                    sp.wait_ge(bias_in, 32)

                @block.gpsimd
                def _(pool):
                    kw = dict(allow_small_or_imprecise_dtypes=True)
                    nc.gpsimd.iota(e_less[:], [[0, TT], [1, E]], base=-E, channel_multiplier=0, **kw).then_inc(consts, 1)
                    nc.gpsimd.memset(ones[:], 1.0).then_inc(consts, 1)
                    nc.gpsimd.memset(tri[:], 1.0).then_inc(const_steps, 1)
                    pool.wait_ge(const_steps, 1)
                    nc.gpsimd.affine_select(out=tri[:], in_=tri[:], compare_op=ALU.is_gt, fill=0.0, base=0,
                                            pattern=[[1, P]], channel_multiplier=-1).then_inc(consts, 1)
                    nc.gpsimd.iota(k128[:], [[0, E], [P, TT]], base=0, channel_multiplier=0, **kw).then_inc(consts, 1)
                    nc.gpsimd.iota(tile_no[:], [[1, NT], [0, E]], base=0, channel_multiplier=0, **kw).then_inc(consts, 1)
                    nc.gpsimd.iota(edges[:], [[P, NT + 1]], base=0, channel_multiplier=0, **kw).then_inc(consts, 1)
                    nc.gpsimd.iota(col_no[:], [[1, P]], base=0, channel_multiplier=0, **kw).then_inc(consts, 1)
                    nc.gpsimd.iota(part_no[:], [[0, 1]], base=0, channel_multiplier=1, **kw).then_inc(consts, 1)
                    nc.gpsimd.iota(tt_no[:], [[1, TT]], base=0, channel_multiplier=0, **kw).then_inc(consts, 1)
                    pool.wait_ge(consts, 9)
                    pool.wait_ge(route, STEPS_TILE)
                    nc.gpsimd.tensor_tensor(at_tile[:, :, 1], at_tile[:, :, 0],
                                            part_no[:, :, None].broadcast_to([P, TT, NT]), ALU.mult).then_inc(cols_ready, 1)
                    nc.gpsimd.tensor_tensor(at_tile[:, :, 2], at_tile[:, :, 0],
                                            tt_no[:, :, None].broadcast_to([P, TT, NT]), ALU.mult).then_inc(cols_ready, 1)

                @block.vector
                def _(dve):
                    count = [0]

                    def then(op):
                        op.then_inc(route, 1)
                        count[0] += 1
                        dve.wait_ge(route, count[0])

                    V = nc.vector
                    dve.wait_ge(consts, 9)
                    then(V.tensor_reduce(best[:], scores_all[:], AX.X, ALU.max))
                    then(V.tensor_tensor(is_best[:], scores_all[:], best[:, :, None].broadcast_to([P, TT, E]), ALU.is_ge))
                    then(V.tensor_tensor(pick[:], is_best[:], e_less[:], ALU.mult))
                    then(V.tensor_reduce(first[:], pick[:], AX.X, ALU.min))
                    then(V.tensor_tensor(onehot[:], e_less[:], first[:, :, None].broadcast_to([P, TT, E]), ALU.is_equal))
                    dve.wait_ge(counts_ready, 2)
                    then(V.tensor_copy(within[:], bank[0][:, 0:TT * E].rearrange("p (t e) -> p t e", e=E)))
                    then(V.tensor_copy(total[:].rearrange("p e t -> p t e"),
                                       bank[1][:, 0:TT * E].rearrange("p (t e) -> p t e", e=E)))
                    for e in range(E):
                        then(V.tensor_tensor_scan(upto[:, e], ones[:, 0:TT], total[:, e], 0.0, ALU.mult, ALU.add))
                    then(V.tensor_tensor(more[:], upto[:, :, TT - 1:TT].broadcast_to([P, E, TT]), k128[:], ALU.is_gt))
                    then(V.tensor_reduce(tiles[:], more[:], AX.X, ALU.add))
                    then(V.tensor_tensor_scan(tiles_end[:], ones[:, 0:E], tiles[:], 0.0, ALU.mult, ALU.add))
                    then(V.tensor_tensor(base[:], tiles_end[:], tiles[:], ALU.subtract))
                    then(V.tensor_scalar(base[:], base[:], float(P), None, ALU.mult))
                    then(V.tensor_tensor(upto[:], upto[:], total[:], ALU.subtract))
                    then(V.tensor_tensor(offs[:], upto[:].rearrange("p e t -> p t e"), within[:], ALU.add))
                    then(V.tensor_tensor(offs[:], offs[:], base[:, None, :].broadcast_to([P, TT, E]), ALU.add))
                    then(V.tensor_tensor(offs[:], offs[:], onehot[:], ALU.mult))
                    then(V.tensor_reduce(slot[:], offs[:], AX.X, ALU.add))
                    then(V.tensor_tensor(reached[:], slot[:, :, None].broadcast_to([P, TT, NT + 1]),
                                         edges[:, None, :].broadcast_to([P, TT, NT + 1]), ALU.is_ge))
                    then(V.tensor_tensor(at_tile[:, :, 0], reached[:, :, 0:NT], reached[:, :, 1:NT + 1], ALU.subtract))
                    then(V.tensor_reduce(tiles_to[:], reached[:], AX.X, ALU.add))
                    then(V.tensor_scalar(start[:], tiles_to[:], -float(P), float(P), ALU.mult, ALU.add))
                    then(V.tensor_tensor(place[:], slot[:], start[:], ALU.add))
                    for t in range(0, TT, TT // 4):
                        q = slice(t, t + TT // 4)
                        V.tensor_tensor(at_place[:, q], place[:, q, None].broadcast_to([P, TT // 4, P]),
                                        col_no[:, None, :].broadcast_to([P, TT // 4, P]),
                                        ALU.is_equal).then_inc(rows_ready, 1)
                    then(V.tensor_tensor(past[:], tile_no[:], tiles_end[:, None, :].broadcast_to([P, NT, E]), ALU.is_ge))
                    then(V.tensor_reduce(expert_f[:], past[:], AX.X, ALU.add))
                    then(V.tensor_scalar(expert_c[:], expert_f[:], float(E - 1), None, ALU.min))
                    then(V.tensor_copy(tile_expert[:], expert_c[:]))
                    dve.wait_ge(counts_ready, 3)
                    then(V.tensor_copy(found[:], bank[0][:, 0:3 * NT].rearrange("p (k n) -> p k n", k=3)))
                    then(V.scalar_tensor_tensor(out=get_f[:], in0=found[:, 1], scalar=float(TT), in1=found[:, 2],
                                                op0=ALU.mult, op1=ALU.add))
                    then(V.tensor_copy(get_row[:], get_f[:]))
                    then(V.scalar_tensor_tensor(out=put_f[:], in0=found[:, 2], scalar=float(P), in1=found[:, 1],
                                                op0=ALU.mult, op1=ALU.add))
                    then(V.tensor_scalar(skip_f[:], found[:, 0], -float(2 * TT * P), float(2 * TT * P), ALU.mult, ALU.add))
                    then(V.tensor_tensor(put_f[:], put_f[:], skip_f[:], ALU.add))
                    then(V.tensor_copy(put_row[:], put_f[:]))

                @block.tensor
                def _(pe):
                    pe.wait_ge(route, 5)
                    oh = onehot[:].rearrange("p t e -> p (t e)")
                    nc.tensor.matmul(bank[0][:, 0:TT * E], tri[:], oh, start=True, stop=True).then_inc(counts_ready, 1)
                    nc.tensor.matmul(bank[1][:, 0:TT * E], ones[:], oh, start=True, stop=True).then_inc(counts_ready, 1)
                    pe.wait_ge(cols_ready, 2)
                    for t in range(TT):
                        if t % (TT // 4) == 0:
                            pe.wait_ge(rows_ready, t // (TT // 4) + 1)
                        last = nc.tensor.matmul(bank[0][:, 0:3 * NT], at_place[:, t],
                                                at_tile[:, t].rearrange("p k n -> p (k n)"),
                                                start=(t == 0), stop=(t == TT - 1))
                    last.then_inc(counts_ready, 1)

        with ExitStack() as ft:
            def fb(name, shape, dt=F32):
                return sb_in(ft, name, shape, dt)

            xs = fb("xs", [P, 2, D])
            xsT = fb("xsT", [P, 2, KD, P])
            hid = fb("hid", [P, 2, F])
            hidT = fb("hidT", [P, 2, KF, P])
            x2s = fb("x2s", [P, 2, D])
            ys = fb("ys", [P, 2, D])
            x_now, x2_now, put_now = (fb(n, [P, 2, 1], U32) for n in ("x_now", "x2_now", "put_now"))

            xs_in = [sem("xs_in0"), sem("xs_in1")]
            x2s_in = [sem("x2s_in0"), sem("x2s_in1")]
            x_turned, xsT_ready = sem("x_turned"), sem("xsT_ready")
            up_full, up_free = sem("up_full"), sem("up_free")
            hid_turned, act_done = sem("hid_turned"), sem("act_done")
            down_full, down_free, y_done = sem("down_full"), sem("down_free"), sem("y_done")
            x_copied, x2_copied, put_copied = sem("x_copied"), sem("x2_copied"), sem("put_copied")
            out_stored = [sem("out_stored0"), sem("out_stored1")]
            x_bank, y_bank = bank[0], bank[1]

            def tiles_loop(eng, step):
                step(0, 0, 0, True)
                step(1, 0, 1, True)
                with eng.Fori(1, (NT - 3) // 2) as k:
                    step(2 * k, k, 0, True)
                    step(2 * k + 1, k, 1, True)
                k = (NT - 3) // 2
                step(NT - 3, k, 0, True)
                step(NT - 2, k, 1, False)

            with nc.Block() as block:
                @block.gpsimd
                def _(pool):
                    pool.sem_inc(y_done, 1)

                    def indices(table, i, now, p, copied, count):
                        nc.gpsimd.tensor_copy(now[:, p], table[:, bass.ds(i, 1)]).then_inc(copied, 1)
                        wait_apart(pool, copied, count, passed[1])

                    def get_x(i, p):
                        indices(get_row, i, x_now, p, x_copied, i + 1)
                        nc.gpsimd.indirect_dma_start(
                            xs[:, p], None, xn3_rows,
                            bass.IndirectOffsetOnAxis(ap=x_now[:, p], axis=0)).then_inc(xs_in[p], 16)

                    def get_x2(i, p):
                        indices(get_row, i, x2_now, p, x2_copied, i + 1)
                        nc.gpsimd.indirect_dma_start(
                            x2s[:, p], None, x2_rows,
                            bass.IndirectOffsetOnAxis(ap=x2_now[:, p], axis=0)).then_inc(x2s_in[p], 16)

                    def put(i, k, p):
                        wait_apart(pool, out_stored[p], 16 * k, passed[1])
                        indices(put_row, i, put_now, p, put_copied, i + 1)
                        wait_apart(pool, y_done, i + 2, passed[1])
                        nc.gpsimd.indirect_dma_start(
                            out_rows, bass.IndirectOffsetOnAxis(ap=put_now[:, p], axis=0),
                            ys[:, p], None, bounds_check=B * S - 1, oob_is_err=False).then_inc(out_stored[p], 16)

                    get_x(0, 0)
                    get_x(1, 1)
                    get_x2(0, 0)
                    pool.wait_ge(x_turned, 1)
                    get_x(2, 0)

                    def step(i, k, p, more):
                        if more and not (isinstance(i, int) and i == NT - 3):
                            wait_apart(pool, x_turned, i + 2, passed[1])
                            get_x(i + 3, 1 - p)
                        wait_apart(pool, y_done, i + 1, passed[1])
                        get_x2(i + 1, 1 - p)
                        put(i, k, p)

                    tiles_loop(pool, step)
                    put(NT - 1, (NT - 1) // 2, 0)
                    pool.wait_ge(out_stored[0], 16 * (NT // 2 + 1))
                    pool.wait_ge(out_stored[1], 16 * (NT // 2))

                @block.tensor
                def _(pe):
                    def turn_x(i, k, p):
                        pe.wait_ge(xs_in[p], 16 * k + 16)
                        wait(pe, xsT_ready, i)
                        for c in range(KD):
                            last = nc.tensor.transpose(x_bank[:, c * P:(c + 1) * P], xs[:, p, c * P:(c + 1) * P], ident[:])
                        last.then_inc(x_turned, 1)

                    def up(i, p):
                        e = pe.value_load(tile_expert[0:1, bass.ds(i, 1)], min_val=0, max_val=E - 1)
                        pe.wait_ge(xsT_ready, i + 1)
                        wait(pe, up_free, i)
                        for half in range(F // 512):
                            for c in range(KD):
                                last = nc.tensor.matmul(
                                    pair_a[:, half * 512:(half + 1) * 512], xsT[:, p, c],
                                    w1_sb[:, bass.ds(e, 1), c, half * 512:(half + 1) * 512].rearrange("p o f -> p (o f)"),
                                    start=(c == 0), stop=(c == KD - 1))
                        last.then_inc(up_full, 1)

                    def turn_hidden(i, p):
                        pe.wait_ge(up_free, i + 1)
                        wait(pe, act_done, KF * i)
                        for c in range(KF):
                            last = nc.tensor.transpose(pair_b[:, c * P:(c + 1) * P], hid[:, p, c * P:(c + 1) * P], ident[:])
                        last.then_inc(hid_turned, 1)

                    def down(i, p):
                        e = pe.value_load(tile_expert[0:1, bass.ds(i, 1)], min_val=0, max_val=E - 1)
                        pe.wait_ge(act_done, KF * i + KF)
                        wait(pe, down_free, i)
                        for c in range(KF):
                            last = nc.tensor.matmul(y_bank[:, 0:D], hidT[:, p, c],
                                                    w2_sb[:, bass.ds(e, 1), c, :].rearrange("p o d -> p (o d)"),
                                                    start=(c == 0), stop=(c == KF - 1))
                        last.then_inc(down_full, 1)

                    turn_x(0, 0, 0)
                    turn_x(1, 0, 1)
                    pe.wait_ge(w1_in, 16 * E)
                    up(0, 0)
                    turn_hidden(0, 0)
                    pe.wait_ge(w2_in, 16 * E)

                    def step(i, k, p, more):
                        up(i + 1, 1 - p)
                        if more:
                            turn_x(i + 2, k + 1, p)
                        down(i, p)
                        turn_hidden(i + 1, 1 - p)

                    tiles_loop(pe, step)
                    down(NT - 1, 0)

                @block.vector
                def _(dve):
                    dve.wait_ge(bias_in, 32)

                    def x_out(i, p):
                        dve.wait_ge(x_turned, i + 1)
                        if not (isinstance(i, int) and i < 2):
                            dve.wait_ge(up_full, i - 1)
                        nc.vector.tensor_copy(xsT[:, p].rearrange("p c t -> p (c t)"),
                                              x_bank[:, 0:KD * P]).then_inc(xsT_ready, 1)

                    def hid_out(i, p):
                        dve.wait_ge(up_full, i + 1)
                        nc.vector.tensor_copy(hid[:, p], pair_a[:]).then_inc(up_free, 1)

                    def y_out(i, k, p):
                        e = dve.value_load(tile_expert[0:1, bass.ds(i, 1)], min_val=0, max_val=E - 1)
                        dve.wait_ge(down_full, i + 1)
                        wait(dve, out_stored[p], 16 * k)
                        nc.vector.tensor_tensor(ys[:, p], y_bank[:, 0:D],
                                                b2_sb[:, bass.ds(e, 1), :].rearrange("p o d -> p (o d)"),
                                                ALU.add).then_inc(down_free, 1)
                        dve.wait_ge(down_free, i + 1)
                        dve.wait_ge(x2s_in[p], 16 * k + 16)
                        nc.vector.tensor_tensor(ys[:, p], ys[:, p], x2s[:, p], ALU.add).then_inc(y_done, 1)

                    x_out(0, 0)
                    x_out(1, 1)
                    hid_out(0, 0)

                    def step(i, k, p, more):
                        hid_out(i + 1, 1 - p)
                        if more:
                            x_out(i + 2, p)
                        y_out(i, k, p)

                    tiles_loop(dve, step)
                    y_out(NT - 1, (NT - 1) // 2, 0)

                @block.scalar
                def _(act):
                    act.wait_ge(bias_in, 32)

                    def gelu(i, p):
                        e = act.value_load(tile_expert[0:1, bass.ds(i, 1)], min_val=0, max_val=E - 1)
                        act.wait_ge(hid_turned, i + 1)
                        for c in range(KF):
                            nc.scalar.activation(hidT[:, p, c], pair_b[:, c * P:(c + 1) * P], ACT.Gelu,
                                                 bias=b1_sb[:, bass.ds(e, 1), c]).then_inc(act_done, 1)

                    gelu(0, 0)

                    def step(i, k, p, more):
                        gelu(i + 1, 1 - p)

                    tiles_loop(act, step)


_INS = ["x", "ctx_1024", "L0_attn_W_in", "L0_attn_dw_kernel", "L0_attn_pw_kernel", "L0_attn_conv_bias",
        "L0_attn_W_x", "L0_attn_W_dt", "L0_attn_b_dt", "L0_attn_A_log", "L0_attn_D", "L0_attn_W_out",
        "L0_xattn_Wq", "L0_xattn_Wk", "L0_xattn_Wv", "L0_xattn_Wo", "L0_xattn_bo",
        "L0_ffn_wr", "L0_ffn_br", "L0_ffn_w1", "L0_ffn_b1", "L0_ffn_w2", "L0_ffn_b2"]


def kernel(**inputs):
    import numpy as _np
    import concourse.bacc as _bacc
    from concourse import mybir as _mybir
    from concourse.bass_utils import run_bass_kernel_spmd as _run

    nc = _bacc.Bacc("TRN2", target_bir_lowering=False, num_devices=1)
    arrays, args = {}, []
    for name in _INS:
        a = _np.ascontiguousarray(inputs[name])
        arrays[f"in_{name}"] = a
        args.append(nc.dram_tensor(f"in_{name}", a.shape, _mybir.dt.from_np(a.dtype), kind="ExternalInput").ap())
    out = nc.dram_tensor("out_0", (B, S, D), _mybir.dt.float32, kind="ExternalOutput").ap()
    decoder_layer(nc, *args, out)
    r = _run(nc, [arrays], core_ids=[0])
    return r.results[0]["out_0"]
```

```python
import concourse.bass as bass
from concourse import mybir
from contextlib import ExitStack

F32 = mybir.dt.float32
I32 = mybir.dt.int32
U32 = mybir.dt.uint32
BF16 = mybir.dt.bfloat16
ALU = mybir.AluOpType
ACT = mybir.ActivationFunctionType
AX = mybir.AxisListType

P = 128
B, S, D = 4, 1024, 256
DI, NS, KC, R = 512, 8, 4, 16
H, DH, M = 16, 64, 64
E, F = 8, 1024
EPS = 1e-5
T = 512
NC = B * S // T
TJ = T // P
KD = D // P
MB = DI // P
HC = H * DH // P
KF = F // P
TT = B * S // P
NT = TT + E - 1
SCALE = DH ** -0.5
RING = 4
GP_ADDS = (1, 2, 3, 4, 6)


def wait(eng, sem, value):
    if isinstance(value, int) and value <= 0:
        return
    eng.wait_ge(sem, value)


def wait_apart(eng, sem, value, passed):
    if isinstance(value, int) and value <= 0:
        return
    eng.wait_ge(sem, value)
    eng.sem_inc(passed, 1)


class Carver:
    def __init__(self, arena):
        self.arena, self.at = arena, 0

    def __call__(self, *shape):
        n = 1
        for s in shape:
            n *= s
        part = self.arena[:, self.at:self.at + n]
        self.at += n
        names = [f"d{i}" for i in range(len(shape))]
        if len(shape) == 1:
            return part
        return part.rearrange(f"p ({' '.join(names)}) -> p {' '.join(names)}",
                              **{k: v for k, v in zip(names[1:], shape[1:])})


ARENA = 34828


def decoder_layer(nc, x, ctx_in, W_in, dwk, pwk, cbias, W_x, W_dt, b_dt, A_log, D_skip, W_out,
                  Wq, Wk, Wv, Wo, bo, wr, br, w1, b1, w2, b2, out):
    x_f = x.rearrange("b s d -> (b s) d")
    x_t = x_f.rearrange("(n p) d -> p n d", p=P)
    out_rows = out.rearrange("b s d -> (b s) d")

    def dram(name, shape):
        return nc.dram_tensor(name, shape, F32, kind="Internal").ap()

    g_dram = dram("g_dram", (B, P, KD * H * M))
    u_dram = dram("u_dram", (B, P, HC * D))
    bc_dram = dram("bc_dram", (2, 2 * NS, T))
    x2_dram = dram("x2_dram", (P, TT, D))
    xn3_dram = dram("xn3_dram", (P, TT, D))

    root = ExitStack()
    with root:
        def sem(name):
            return root.enter_context(nc.semaphore(name))

        def sb_in(stack, name, shape, dt=F32):
            return stack.enter_context(nc.sbuf_tensor(name, shape, dt))

        passed = [sem("passed_sync"), sem("passed_gpsimd"), sem("passed_vector")]
        ident = sb_in(root, "ident", [P, P])
        eps_col = sb_in(root, "eps_col", [P, 1])
        scores_all = sb_in(root, "scores_all", [P, TT, E])
        bank = [root.enter_context(nc.psum_tensor(f"bank{i}", [P, 512], F32)) for i in range(4)]
        pair_a = root.enter_context(nc.psum_tensor("pair_a", [P, 1024], F32))
        pair_b = root.enter_context(nc.psum_tensor("pair_b", [P, 1024], F32))

        arena = sb_in(root, "arena", [P, ARENA])
        w1_in, w2_in = sem("w1_in"), sem("w2_in")
        experts = Carver(arena)
        w1_sb, w2_sb = experts(E, KD, F), experts(E, KF, D)

        def load_experts(eng):
            for e in range(E):
                eng.dma_start(w1_sb[:, e], w1[e].rearrange("(k p) f -> p k f", p=P)).then_inc(w1_in, 16)
            for e in range(E):
                eng.dma_start(w2_sb[:, e], w2[e].rearrange("(k p) d -> p k d", p=P)).then_inc(w2_in, 16)

        with ExitStack() as seq:
            weights = Weights(lambda name, shape: sb_in(seq, name, shape), sem("weights_in"),
                              sem("w_in_arrived"))
            sequence_part(nc, sem, lambda name, shape: sb_in(seq, name, shape), arena, passed, ident, eps_col,
                          scores_all, bank, pair_a, pair_b, x_t, weights,
                          lambda eng: weights.load(eng, W_in, dwk, pwk, cbias, W_x, W_dt, b_dt, A_log, D_skip,
                                                   W_out, bo, wr, br),
                          load_experts, ctx_in, Wq, Wk, Wv, Wo, g_dram, u_dram, bc_dram, x2_dram, xn3_dram)
        expert_part(nc, sem, sb_in, passed, ident, scores_all, bank, pair_a, pair_b, w1_sb, w2_sb, w1_in, w2_in,
                    b1, b2, x2_dram, xn3_dram, out_rows)


class Weights:
    LOADS = 11 + MB

    def __init__(self, sb, arrived, first_arrived):
        self.arrived, self.first_arrived = arrived, first_arrived
        self.w_in = sb("w_in", [P, KD, 2 * DI])
        self.pw = sb("pw", [P, MB, DI])
        self.w_x = sb("w_x", [P, MB, R + 2 * NS])
        self.w_dt = sb("w_dt", [R, DI])
        self.w_out = sb("w_out", [P, MB, D])
        self.taps = sb("taps", [P, MB, KC])
        self.conv_bias = sb("conv_bias", [P, MB])
        self.dt_bias = sb("dt_bias", [P, MB])
        self.d_skip = sb("d_skip", [P, MB])
        self.a_log = sb("a_log", [P, MB, NS])
        self.bo = sb("bo", [P, D])
        self.wr = sb("wr", [P, KD, E])
        self.br = sb("br", [P, E])

    def load(self, eng, W_in, dwk, pwk, cbias, W_x, W_dt, b_dt, A_log, D_skip, W_out, bo, wr, br):
        eng.dma_start(self.w_in[:], W_in.rearrange("(k p) n -> p k n", p=P)).then_inc(self.first_arrived, 16)
        for dst, src in (
            (self.pw, pwk.rearrange("(k p) n -> p k n", p=P)),
            (self.w_x, W_x.rearrange("(k p) n -> p k n", p=P)),
            (self.w_dt, W_dt),
            (self.w_out, W_out.rearrange("(k p) n -> p k n", p=P)),
            (self.conv_bias, cbias.rearrange("(m p) -> p m", p=P)),
            (self.dt_bias, b_dt.rearrange("(m p) -> p m", p=P)),
            (self.d_skip, D_skip.rearrange("(m p) -> p m", p=P)),
            (self.a_log, A_log.rearrange("(m p) n -> p m n", p=P)),
            (self.bo, bo.partition_broadcast(P)),
            (self.wr, wr.rearrange("(k p) n -> p k n", p=P)),
            (self.br, br.partition_broadcast(P)),
        ):
            eng.dma_start(dst[:], src, allow_slow_non_contiguous=True).then_inc(self.arrived, 16)
        for m in range(MB):
            eng.dma_start(self.taps[:, m], dwk[:, m * P:(m + 1) * P].rearrange("k p -> p k"),
                          allow_slow_non_contiguous=True).then_inc(self.arrived, 16)


def sequence_part(nc, sem, sb, arena, passed, ident, eps_col, scores_all, bank, pair_a, pair_b, x_t, weights,
                  load_weights, load_experts, ctx_in, Wq, Wk, Wv, Wo, g_dram, u_dram, bc_dram, x2_dram, xn3_dram):
    W = weights
    a_exp = sb("a_exp", [P, MB, NS])
    a_neg = sb("a_neg", [P, MB, NS])
    g_sb = sb("g_att", [P, KD, H * M])
    u_sb = sb("u_att", [P, HC, D])
    part = Carver(arena)
    xa = part(TJ, D)
    xnT = part(2, KD, T)
    xp = part(MB, KC - 1 + T)
    cv = part(MB, T)
    delta = part(2, MB, T)
    u = part(MB, T)
    xc = part(MB, T)
    zg = part(MB, T)
    y_d = part(MB, T)
    y_g = part(MB, T)
    ring = part(RING, 2, T)
    dA = part(2, MB, T)
    hb = part(2, MB, T)
    xd = sb("xd", [R + 2 * NS, T])
    halo_cols = sb("halo_cols", [P, MB, KC - 1])
    carry = sb("carry", [P, NS, MB])
    xr = sb("xr", [P, 2, TJ, D])
    xn2 = sb("xn2", [P, TJ, D])
    xn2T = sb("xn2T", [P, 2, KD, P])
    probs = sb("probs", [P, 2, H * M])
    probsT = sb("probsT", [P, HC, P])
    xn3 = part(TJ, D)
    xn3T = probsT[:].rearrange("p c t -> p (c t)").rearrange("p (k t) -> p k t", k=KD)
    row_max = sb("row_max", [P, H])
    row_sum = sb("row_sum", [P, H])
    row_inv = sb("row_inv", [P, 2, H])

    BM = B * M
    flat = lambda t, names: t[:].rearrange(f"p {names} -> p ({names})")
    pair_w = flat(g_sb, "k n").rearrange("p (s w n) -> p s w n", s=2, w=4)
    diag = flat(u_sb, "c d").rearrange("p (s w b n) -> p s w b n", s=2, w=2, b=B)
    wqT = xn2T[:].rearrange("p s k t -> p s (k t)")
    g_out = probs
    u_out = (probsT[:].rearrange("p c t -> p (c t)"), xn2[:].rearrange("p j d -> p (j d)"))
    kv_bank = (bank[3][:, 0:BM], pair_b[:, 512:512 + BM])
    ctx_sb = xr[:, 1, 0:BM // P]
    ctxT = xr[:, 1, BM // P:BM // P + KD]

    class Norm:
        def __init__(self, name):
            self.stats = sb(name + "_stats", [P, TJ, 6])
            self.mv = sb(name + "_mv", [P, TJ, 2])
            self.ln = sb(name + "_ln", [P, TJ])
            self.r0 = sb(name + "_r0", [P, TJ])
            self.tmp = sb(name + "_tmp", [P, 3, TJ])
            self.rstd = sb(name + "_rstd", [P, TJ])
            self.shift = sb(name + "_shift", [P, TJ])
            self.dve = sem(name + "_dve")
            self.act = sem(name + "_act")
            self.done = sem(name + "_done")
    LN_DVE = 2 * TJ + 5
    norm1, norm2, norm3 = Norm("norm1"), Norm("norm2"), Norm("norm3")

    a_steps = sem("a_steps")
    ident_zero, ident_ready, eps_ready, diag_zero = (sem(n) for n in (
        "ident_zero", "ident_ready", "eps_ready", "diag_zero"))
    ctx_arrived, pair_w_in = sem("ctx_arrived"), [sem("pair_w_in0"), sem("pair_w_in1")]
    gu_full, gu_free = sem("gu_full"), sem("gu_free")
    g_stored, u_stored = ([sem(f"{n}_stored{s}") for s in range(2)] for n in "gu")
    xa_in, xr_in = sem("xa_in"), [sem("xr_in0"), sem("xr_in1")]
    mm_full, mm_free = sem("mm_full"), sem("mm_free")
    tb_full, tb_free = sem("tb_full"), sem("tb_free")
    ao_full, ao_free = sem("ao_full"), sem("ao_free")
    out_full = sem("out_full")
    x1_added = sem("x1_added")
    sc_full, sc_free = sem("sc_full"), sem("sc_free")
    et_full, et_free = sem("et_full"), sem("et_free")
    halo, conv = sem("halo"), sem("conv")
    xc_ready, zg_ready = sem("xc_ready"), sem("zg_ready")
    softplus_act, delta_ready, u_ready = sem("softplus_act"), sem("delta_ready"), sem("u_ready")
    bc_stored, ring_in = sem("bc_stored"), [sem(f"ring_in{s}") for s in range(RING)]
    yd_init = sem("yd_init")
    da_ready, dbu_ready, h_ready, carry_ready = (sem(n) for n in
                                                 ("da_ready", "dbu_ready", "h_ready", "carry_ready"))
    ch_ready, yd_added, yg_added = sem("ch_ready"), sem("yd_added"), sem("yg_added")
    y_sum, y_ready = sem("y_sum"), sem("y_ready")
    g_in, u_in = sem("g_in"), sem("u_in")
    bo_added = sem("bo_added")
    max_ready, exp_ready, sum_ready, inv_ready, probs_ready = (sem(n) for n in (
        "max_ready", "exp_ready", "sum_ready", "inv_ready", "probs_ready"))
    x2_stored, xn3_stored = [sem("x2_stored0"), sem("x2_stored1")], sem("xn3_stored")

    mm, tb, ao = bank[0:2], bank[2], bank[3]
    YG = len(GP_ADDS)
    dve_adds = [n for n in range(1, NS) if n not in GP_ADDS]
    YD = len(dve_adds)
    CONV = MB * KC + 1
    SOFTPLUS = MB + 2

    MM = KD + 4 * MB

    def mm_z(c):
        missing = KD + MB if isinstance(c, int) and c == NC - 1 else 0
        return MM * c + 2 * (KD + 2 * MB) - missing

    def mm_pw(f):
        return MM * f + KD + MB

    def mm_dt(f):
        return mm_pw(f) + MB

    def mm_tr(g):
        return 0 if isinstance(g, int) and g == 0 else MM * g - MB

    def mm_x(g):
        return mm_tr(g) + KD

    TB = TJ + 1 + KD + 1

    def tb_less(a, before_last, last):
        return {NC - 2: before_last, NC - 1: last}.get(a, 0) if isinstance(a, int) else 0

    def tb_bc(f):
        return f if isinstance(f, int) and f < 2 else TB * (f - 2) + 2 + TJ

    def tb_ln2(a, j):
        return TB * a + 2 + j - tb_less(a, 0, 1)

    def tb_ln3(a, i):
        return TB * a + 3 + TJ + i - tb_less(a, 1, 2)

    def pa_out(c):
        return (1 + TJ) * c

    def pa_scores(a, j):
        return (1 + TJ) * a + 1 + j

    def schedule(eng, step):
        step(-2, -1, True, False, False, False, True)
        step(-1, -1, False, False, False, True, True)
        step(0, 0, True, True, False, True, True)
        with eng.Fori(0, B - 2) as b:
            step(2 * b + 1, b, False, True, True, True, True)
            step(2 * b + 2, b + 1, True, True, True, True, True)
        step(NC - 3, NC // 2 - 2, False, True, True, True, True)
        step(NC - 2, NC // 2 - 1, True, True, True, True, False)
        step(NC - 1, NC // 2 - 1, False, True, True, False, False)
        step(NC, NC // 2, True, False, True, False, False)

    def gu_use(pair, what=0):
        return KD + 5 * pair + what

    def at(c, iteration):
        return isinstance(c, int) and c == iteration


    def load_pair(eng, pair):
        s = pair % 2
        for w, src in enumerate((Wq, Wk, Wv)):
            eng.dma_start(pair_w[:, s, w].rearrange("p (k n) -> p k n", k=KD),
                          src[:, pair * P:(pair + 1) * P].rearrange("(k p) n -> p k n", p=P)
                          ).then_inc(pair_w_in[s], 16)
        eng.dma_start(pair_w[:, s, 3], Wo[pair * P:(pair + 1) * P, :]).then_inc(pair_w_in[s], 16)

    with nc.Block() as block:
        @block.sync
        def _(sp):
            def store_pair(pair):
                s = pair % 2
                sp.wait_ge(gu_free, gu_use(pair, 3) + 1)
                for k in range(KD):
                    sp.dma_start(g_dram.rearrange("b p (k n) -> p b k n", k=KD)[:, :, k, pair * P:(pair + 1) * P],
                                 g_out[:, s].rearrange("p (b k n) -> p b k n", b=B, k=KD)[:, :, k]
                                 ).then_inc(g_stored[s], 16)
                sp.wait_ge(gu_free, gu_use(pair, 4) + 1)
                sp.dma_start(u_dram.rearrange("b p (c d) -> p b c d", c=HC)[:, :, pair],
                             u_out[s].rearrange("p (b d) -> p b d", b=B)).then_inc(u_stored[s], 16)
                if pair + 2 < HC:
                    load_pair(sp, pair + 2)

            def load_ring(c, n, par):
                wait_apart(sp, ch_ready, NS * c + n - RING + 1, passed[0])
                src = bc_dram[par].rearrange("(g n) t -> g n t", n=NS)[:, n, :]
                sp.dma_start(ring[:, n % RING], src.partition_broadcast(P)).then_inc(ring_in[n % RING], 16)

            def step(c, half, starts, scan, att, conv_part, proj):
                a, f, g, par, other = c - 1, c + 1, c + 2, 0 if starts else 1, 1 if starts else 0
                if proj:
                    if not (isinstance(g, int) and g == 0):
                        wait_apart(sp, mm_full, mm_tr(f) + KD, passed[0])
                    sp.dma_start(xa, x_t[:, bass.ds(TJ * g, TJ), :]).then_inc(xa_in, 16)
                if scan:
                    wait_apart(sp, x2_stored[par], 16 * half + 16, passed[0])
                    wait_apart(sp, norm3.done, TJ * c + TJ, passed[0])
                    sp.dma_start(xr[:, par], x_t[:, bass.ds(TJ * c, TJ), :]).then_inc(xr_in[par], 16)
                    for n in range(RING, NS):
                        load_ring(c, n, par)
                        if at(c, 0) and n % 2 == 0:
                            store_pair(2 if n == RING else 3)
                if at(c, -1):
                    store_pair(0)
                if conv_part:
                    wait_apart(sp, tb_free, tb_bc(f) + 2, passed[0])
                    sp.dma_start(bc_dram[other], xd[R:R + 2 * NS, :]).then_inc(bc_stored, 16)
                    wait_apart(sp, bc_stored, 16 * f + 16, passed[0])
                    for n in range(RING):
                        load_ring(f, n, other)
                if at(c, -1):
                    store_pair(1)
                if at(c, 0):
                    for pair in range(4, HC):
                        store_pair(pair)
                if scan and starts:
                    if at(c, 0):
                        for s in range(2):
                            sp.wait_ge(g_stored[s], 16 * KD * (HC // 2))
                            sp.wait_ge(u_stored[s], 16 * (HC // 2))
                    wait_apart(sp, sc_full, TJ * c, passed[0])
                    sp.dma_start(g_sb[:], g_dram[bass.ds(half, 1)].rearrange(
                        "o p (k n) -> (o p) k n", k=KD)).then_inc(g_in, 16)
                    wait_apart(sp, ao_full, TJ * c, passed[0])
                    sp.dma_start(u_sb[:], u_dram[bass.ds(half, 1)].rearrange(
                        "o p (k n) -> (o p) k n", k=HC)).then_inc(u_in, 16)
                if att:
                    wait_apart(sp, ao_free, TJ * a + TJ + 1, passed[0])
                    sp.dma_start(x2_dram[:, bass.ds(TJ * a, TJ), :], xr[:, other]).then_inc(x2_stored[other], 16)
                    wait_apart(sp, norm3.done, TJ * a + 3 * TJ, passed[0])
                    sp.dma_start(xn3_dram[:, bass.ds(TJ * a, TJ), :], xn3).then_inc(xn3_stored, 16)

            sp.dma_start(ctx_sb, ctx_in.rearrange("b m d -> (b m) d").rearrange("(k p) d -> p k d", p=P)
                         ).then_inc(ctx_arrived, 16)
            schedule(sp, step)
            sp.wait_ge(x2_stored[0], 16 * (NC // 2 + 1))
            sp.wait_ge(x2_stored[1], 16 * (NC // 2 + 1))
            sp.wait_ge(xn3_stored, 16 * (NC + 1))

        @block.gpsimd
        def _(pool):
            pool.sem_inc(mm_free, 2)
            pool.sem_inc(tb_free, 1)
            pool.sem_inc(ao_free, 1)
            pool.sem_inc(sc_free, 1)
            pool.sem_inc(et_free, 1)
            pool.sem_inc(et_full, 2)
            pool.sem_inc(x2_stored[0], 16)
            pool.sem_inc(x2_stored[1], 16)
            pool.sem_inc(xn3_stored, 16)
            pool.sem_inc(norm3.done, 2 * TJ)
            nc.gpsimd.memset(ident[:], 0.0).then_inc(ident_zero, 1)
            pool.wait_ge(ident_zero, 1)
            nc.gpsimd.affine_select(out=ident[:], in_=ident[:], compare_op=ALU.not_equal, fill=1.0,
                                    base=0, pattern=[[-1, P]], channel_multiplier=1).then_inc(ident_ready, 1)

            def wait_left(c, n):
                if isinstance(c, int) and c < 0:
                    return
                if n == 0:
                    pool.wait_ge(ch_ready, NS * c + 1)
                elif n in GP_ADDS:
                    pool.wait_ge(yg_added, YG * c + GP_ADDS.index(n) + 1)
                else:
                    pool.wait_ge(yd_added, YD * c + dve_adds.index(n) + 1)

            def step(c, half, starts, scan, att, conv_part, proj):
                a, f, g, par, other = c - 1, c + 1, c + 2, 0 if starts else 1, 1 if starts else 0

                def dbu(c, n):
                    if n >= 2:
                        wait_left(c, n - 2)
                    else:
                        pool.wait_ge(u_ready, c + 1)
                        wait_left(c - 1, NS + n - 2)
                    pool.wait_ge(ring_in[n % RING], 16 * (2 * c + n // RING + 1))
                    nc.gpsimd.tensor_tensor(hb[:, n % 2], u, ring[:, n % RING, 0:1, :].broadcast_to([P, MB, T]),
                                            ALU.mult).then_inc(dbu_ready, 1)

                def add_up(n):
                    pool.wait_ge(ch_ready, NS * c + n + 1)
                    wait(pool, yg_added, YG * c + GP_ADDS.index(n))
                    nc.gpsimd.tensor_tensor(y_g, y_g, hb[:, n % 2], ALU.add).then_inc(yg_added, 1)

                def probabilities(j):
                    if not att:
                        return
                    pool.wait_ge(inv_ready, TJ * a + j + 1)
                    e3 = probs[:, j % 2].rearrange("p (h m) -> p h m", m=M)
                    nc.gpsimd.tensor_tensor(e3, e3, row_inv[:, j % 2, :, None].broadcast_to([P, H, M]),
                                            ALU.mult).then_inc(probs_ready, 1)

                if scan:
                    add_up(1)
                    dbu(c, 3)
                probabilities(0)
                if scan:
                    add_up(2)
                    dbu(c, 4)
                probabilities(1)
                if scan:
                    add_up(3)
                    dbu(c, 5)
                    add_up(4)
                    dbu(c, 6)
                if proj:
                    wait_apart(pool, norm1.dve, LN_DVE * g + LN_DVE, passed[1])
                    for j in range(TJ):
                        nc.gpsimd.tensor_scalar(xa[:, j], xa[:, j], norm1.rstd[:, j:j + 1],
                                                norm1.shift[:, j:j + 1], ALU.mult, ALU.add).then_inc(norm1.done, 1)
                if scan:
                    dbu(c, 7)
                probabilities(2)
                if scan:
                    add_up(6)
                probabilities(3)
                if conv_part:
                    pool.wait_ge(delta_ready, f + 1)
                    wait(pool, dbu_ready, NS * f)
                    nc.gpsimd.tensor_tensor(u, delta[:, other], xc, ALU.mult).then_inc(u_ready, 1)
                    dbu(f, 0)
                    dbu(f, 1)
                    dbu(f, 2)
                if at(c, -1):
                    pool.wait_ge(W.arrived, 16 * W.LOADS)
                if scan:
                    pool.wait_ge(norm2.done, TJ * c + TJ)
                    nc.gpsimd.tensor_tensor(xr[:, par], xr[:, par],
                                            W.bo[:, None, :].broadcast_to([P, TJ, D]),
                                            ALU.add).then_inc(bo_added, 1)

            schedule(pool, step)

        @block.scalar
        def _(act):
            load_weights(act)
            load_pair(act, 0)
            load_pair(act, 1)
            act.wait_ge(eps_ready, 1)

            def context_turned():
                for k in range(KD):
                    act.wait_ge(gu_full, k + 1)
                    nc.scalar.activation(ctxT[:, k], pair_a[:, k * 512:k * 512 + BM], ACT.Copy).then_inc(gu_free, 1)
                act.wait_ge(diag_zero, 1)

            def make_gu(pair):
                s = pair % 2
                act.wait_ge(gu_full, gu_use(pair) + 1)
                nc.scalar.activation(wqT[:, s], pair_b[:, 0:D], ACT.Copy).then_inc(gu_free, 1)
                for w in range(2):
                    act.wait_ge(gu_full, gu_use(pair, 1 + w) + 1)
                    src = kv_bank[w].rearrange("p (b m) -> p b m", b=B)
                    nc.scalar.activation(diag[0:DH, s, w, :, 0:M], src[0:DH], ACT.Copy)
                    nc.scalar.activation(diag[DH:P, s, w, :, M:P], src[DH:P], ACT.Copy).then_inc(gu_free, 1)
                act.wait_ge(gu_full, gu_use(pair, 3) + 1)
                wait(act, g_stored[s], 16 * KD * (pair // 2))
                nc.scalar.activation(g_out[:, s], pair_a[:], ACT.Copy).then_inc(gu_free, 1)
                act.wait_ge(gu_full, gu_use(pair, 4) + 1)
                wait(act, u_stored[s], 16 * (pair // 2))
                nc.scalar.activation(u_out[s], pair_b[:], ACT.Copy).then_inc(gu_free, 1)

            def load_tables():
                nc.scalar.preload_act_table_set("natural_log_exp_and_others")

            def rstd_start(n, base):
                act.wait_ge(n.dve, LN_DVE * base + 2 * TJ)
                nc.scalar.activation(n.ln[:], n.mv[:, :, 1], ACT.Ln, bias=eps_col[:, 0:1]).then_inc(n.act, 1)
                act.wait_ge(n.act, 2 * base + 1)
                nc.scalar.activation(n.r0[:], n.ln[:], ACT.Exp, scale=-0.5).then_inc(n.act, 1)

            def normalise(n, base, src, dst):
                act.wait_ge(n.dve, LN_DVE * base + LN_DVE)
                for j in range(TJ):
                    nc.scalar.activation(dst[:, j], src[:, j], ACT.Identity, scale=n.rstd[:, j:j + 1],
                                         bias=n.shift[:, j:j + 1]).then_inc(n.done, 1)

            def step(c, half, starts, scan, att, conv_part, proj):
                a, f, g, par, other = c - 1, c + 1, c + 2, 0 if starts else 1, 1 if starts else 0

                def decay(c, n, parity):
                    wait(act, h_ready, MB * (NS * c + n - 1))
                    for m in range(MB):
                        nc.scalar.activation(dA[:, n % 2, m], delta[:, parity, m], ACT.Exp,
                                             scale=a_neg[:, m, n:n + 1]).then_inc(da_ready, 1)

                def decays(n):
                    if scan:
                        decay(c, n, par)

                def z_out():
                    wait(act, y_ready, f)
                    for m in range(MB):
                        act.wait_ge(mm_full, mm_z(f) + m + 1)
                        nc.scalar.activation(zg[:, m], mm[m % 2][:], ACT.Copy).then_inc(mm_free, 1)

                def ln2_turned(a, j):
                    act.wait_ge(tb_full, tb_ln2(a, j) + 1)
                    nc.scalar.activation(xn2T[:, j % 2].rearrange("p k t -> p (k t)"), tb[:, 0:KD * P],
                                         ACT.Copy).then_inc(tb_free, 1)

                def exponentials(j):
                    if not att:
                        return
                    act.wait_ge(sc_free, pa_scores(a, j) + 2)
                    nc.scalar.activation(probs[:, j % 2], probs[:, j % 2], ACT.Exp, scale=SCALE).then_inc(exp_ready, 1)

                def probs_turned(j):
                    if not att:
                        return
                    act.wait_ge(et_full, TJ * a + j + 3)
                    wait(act, ao_full, TJ * a + j)
                    nc.scalar.activation(probsT[:].rearrange("p c t -> p (c t)"), pair_b[:],
                                         ACT.Copy).then_inc(et_free, 1)

                def ln1_turned():
                    for k in range(KD):
                        act.wait_ge(mm_full, mm_tr(g) + k + 1)
                        nc.scalar.activation(xnT[:, par, k], mm[k % 2][:], ACT.Copy).then_inc(mm_free, 1)

                def x_in_out(blocks):
                    if 0 in blocks:
                        wait(act, halo, g)
                    for m in blocks:
                        act.wait_ge(mm_full, mm_x(g) + m + 1)
                        nc.scalar.activation(xp[:, m, KC - 1:], mm[m % 2][:], ACT.Copy).then_inc(mm_free, 1)

                def pointwise_out(blocks):
                    if 0 in blocks:
                        wait(act, u_ready, f)
                        wait(act, yd_init, MB * f)
                    for m in blocks:
                        act.wait_ge(mm_full, mm_pw(f) + m + 1)
                        nc.scalar.activation(xc[:, m], mm[m % 2][:], ACT.Identity,
                                             bias=W.conv_bias[:, m:m + 1]).then_inc(mm_free, 1)

                def silu_z():
                    act.wait_ge(mm_free, mm_z(c) + MB + 2)
                    nc.scalar.activation(zg, zg, ACT.Silu).then_inc(zg_ready, 1)

                def silu_x():
                    act.wait_ge(mm_free, mm_pw(f) + MB + 2)
                    nc.scalar.activation(xc, xc, ACT.Silu).then_inc(xc_ready, 1)

                def low_rank_out():
                    wait(act, bc_stored, 16 * f)
                    act.wait_ge(tb_full, tb_bc(f) + 1)
                    nc.scalar.activation(xd[:], tb[0:R + 2 * NS, :], ACT.Copy).then_inc(tb_free, 1)

                def softplus_in():
                    wait(act, da_ready, MB * NS * c)
                    for m in range(MB):
                        act.wait_ge(mm_full, mm_dt(f) + m + 1)
                        src = mm[m % 2]
                        nc.scalar.activation(cv[:, m], src[:], ACT.Abs,
                                             bias=W.dt_bias[:, m:m + 1]).then_inc(softplus_act, 1)
                        nc.scalar.activation(delta[:, other, m], src[:], ACT.Relu,
                                             bias=W.dt_bias[:, m:m + 1]).then_inc(mm_free, 1)

                def softplus_out():
                    act.wait_ge(softplus_act, SOFTPLUS * f + MB)
                    nc.scalar.activation(cv, cv, ACT.Exp, scale=-1.0).then_inc(softplus_act, 1)
                    act.wait_ge(softplus_act, SOFTPLUS * f + MB + 1)
                    nc.scalar.activation(cv, cv, ACT.Ln, bias=1.0).then_inc(softplus_act, 1)

                if at(c, -2):
                    load_tables()
                if at(c, -1):
                    act.wait_ge(W.arrived, 16 * W.LOADS)
                    nc.scalar.activation(a_exp[:], W.a_log[:], ACT.Exp).then_inc(a_steps, 1)
                    act.wait_ge(a_steps, 1)
                    nc.scalar.mul(a_neg[:], a_exp[:], -1.0).then_inc(a_steps, 1)
                    act.wait_ge(a_steps, 2)
                    context_turned()
                    make_gu(0)
                if att and not scan:
                    act.wait_ge(out_full, 2 * NC)
                    load_experts(act)
                decays(2)
                if att:
                    ln2_turned(a, 1)
                if at(c, 0):
                    make_gu(2)
                exponentials(0)
                decays(3)
                if at(c, 0):
                    make_gu(3)
                probs_turned(0)
                if att:
                    ln2_turned(a, 2)
                decays(4)
                exponentials(1)
                if conv_part:
                    pointwise_out((0,))
                decays(5)
                if conv_part:
                    pointwise_out((1,))
                if proj:
                    rstd_start(norm1, g)
                if scan:
                    silu_z()
                probs_turned(1)
                if att:
                    ln2_turned(a, 3)
                if conv_part:
                    pointwise_out((2, 3))
                    silu_x()
                load_tables()
                decays(6)
                exponentials(2)
                if conv_part:
                    low_rank_out()
                decays(7)
                if conv_part:
                    softplus_in()
                exponentials(3)
                if at(c, -1) or at(c, 0):
                    softplus_out()
                    for pair in ((1,) if at(c, -1) else (4, 5)):
                        make_gu(pair)
                if proj:
                    ln1_turned()
                if conv_part and not (at(c, -1) or at(c, 0)):
                    softplus_out()
                probs_turned(2)
                if proj:
                    x_in_out((0, 1))
                probs_turned(3)
                if proj:
                    x_in_out((2, 3))
                if at(c, 0):
                    make_gu(6)
                    make_gu(7)
                if conv_part:
                    act.wait_ge(delta_ready, f + 1)
                    decay(f, 0, other)
                    decay(f, 1, other)
                if att:
                    rstd_start(norm3, a)
                    act.wait_ge(xn3_stored, 16 * a + 16)
                    normalise(norm3, a, xr[:, other], xn3)
                if conv_part:
                    wait(act, out_full, 2 * f)
                    for m in range(MB):
                        nc.scalar.activation(y_d[:, m], xc[:, m], ACT.Copy,
                                             scale=W.d_skip[:, m:m + 1]).then_inc(yd_init, 1)
                if att:
                    for k in range(KD):
                        act.wait_ge(tb_full, tb_ln3(a, k) + 1)
                        nc.scalar.activation(xn3T[:, k], tb[:], ACT.Copy).then_inc(tb_free, 1)
                if scan:
                    rstd_start(norm2, c)
                    if at(c, 0):
                        for s in range(2):
                            act.wait_ge(g_stored[s], 16 * KD * (HC // 2))
                            act.wait_ge(u_stored[s], 16 * (HC // 2))
                    normalise(norm2, c, xr[:, par], xn2)
                    ln2_turned(c, 0)
                if conv_part:
                    z_out()

            schedule(act, step)

        @block.vector
        def _(dve):
            nc.vector.memset(eps_col[:], EPS).then_inc(eps_ready, 1)
            nc.vector.memset(diag, 0.0).then_inc(diag_zero, 1)

            def statistics(n, base, src):
                for j in range(TJ):
                    nc.vector.bn_stats(n.stats[:, j], src[:, j]).then_inc(n.dve, 1)
                wait_apart(dve, n.dve, LN_DVE * base + TJ, passed[2])
                for j in range(TJ):
                    nc.vector.bn_aggr(n.mv[:, j], n.stats[:, j]).then_inc(n.dve, 1)

            def refine(n, base):
                at = LN_DVE * base + 2 * TJ
                dve.wait_ge(n.dve, at)
                dve.wait_ge(n.act, 2 * base + 2)
                nc.vector.scalar_tensor_tensor(out=n.tmp[:, 0], in0=n.mv[:, :, 1], scalar=EPS, in1=n.r0[:],
                                               op0=ALU.add, op1=ALU.mult).then_inc(n.dve, 1)
                dve.wait_ge(n.dve, at + 1)
                nc.vector.tensor_tensor(n.tmp[:, 1], n.tmp[:, 0], n.r0[:], ALU.mult).then_inc(n.dve, 1)
                dve.wait_ge(n.dve, at + 2)
                nc.vector.tensor_scalar(n.tmp[:, 2], n.tmp[:, 1], -0.5, 1.5, ALU.mult, ALU.add).then_inc(n.dve, 1)
                dve.wait_ge(n.dve, at + 3)
                nc.vector.tensor_tensor(n.rstd[:], n.tmp[:, 2], n.r0[:], ALU.mult).then_inc(n.dve, 1)
                dve.wait_ge(n.dve, at + 4)
                nc.vector.scalar_tensor_tensor(out=n.shift[:], in0=n.mv[:, :, 0], scalar=-1.0, in1=n.rstd[:],
                                               op0=ALU.mult, op1=ALU.mult).then_inc(n.dve, 1)

            def step(c, half, starts, scan, att, conv_part, proj):
                a, f, g, par, other = c - 1, c + 1, c + 2, 0 if starts else 1, 1 if starts else 0

                def scan_state(c, n, starts):
                    if n == 0:
                        wait(dve, carry_ready, NS * c)
                    dve.wait_ge(dbu_ready, NS * c + n + 1)
                    for m in range(MB):
                        dve.wait_ge(da_ready, MB * (NS * c + n) + m + 1)
                        nc.vector.tensor_tensor_scan(
                            hb[:, n % 2, m], dA[:, n % 2, m], hb[:, n % 2, m],
                            0.0 if starts else carry[:, n, m:m + 1], ALU.mult, ALU.add).then_inc(h_ready, 1)
                    dve.wait_ge(h_ready, MB * (NS * c + n) + MB)
                    nc.vector.tensor_copy(carry[:, n], hb[:, n % 2, :, T - 1]).then_inc(carry_ready, 1)
                    dst = y_g if n == 0 else hb[:, n % 2]
                    dve.wait_ge(carry_ready, NS * c + n + 1)
                    nc.vector.tensor_tensor(dst, hb[:, n % 2], ring[:, n % RING, 1:2, :].broadcast_to([P, MB, T]),
                                            ALU.mult).then_inc(ch_ready, 1)
                    if n in dve_adds:
                        i = dve_adds.index(n)
                        if i == 0:
                            dve.wait_ge(yd_init, MB * (c + 1))
                        wait(dve, yd_added, YD * c + i)
                        dve.wait_ge(ch_ready, NS * c + n + 1)
                        nc.vector.tensor_tensor(y_d, y_d, hb[:, n % 2], ALU.add).then_inc(yd_added, 1)

                def less_max(j):
                    if not att:
                        return
                    dve.wait_ge(sc_full, TJ * a + j + 1)
                    s3 = pair_a[:].rearrange("p (h m) -> p h m", m=M)
                    nc.vector.tensor_reduce(row_max[:], s3, AX.X, ALU.max).then_inc(max_ready, 1)
                    dve.wait_ge(max_ready, TJ * a + j + 1)
                    dve.wait_ge(et_full, TJ * a + j + 1)
                    nc.vector.tensor_tensor(probs[:, j % 2].rearrange("p (h m) -> p h m", m=M), s3,
                                            row_max[:, :, None].broadcast_to([P, H, M]),
                                            ALU.subtract).then_inc(sc_free, 1)

                def row_sums(j):
                    if not att:
                        return
                    dve.wait_ge(exp_ready, TJ * a + j + 1)
                    nc.vector.tensor_reduce(row_sum[:], probs[:, j % 2].rearrange("p (h m) -> p h m", m=M),
                                            AX.X, ALU.add).then_inc(sum_ready, 1)
                    dve.wait_ge(sum_ready, TJ * a + j + 1)
                    nc.vector.reciprocal(row_inv[:, j % 2], row_sum[:]).then_inc(inv_ready, 1)

                def residual(j):
                    if not att:
                        return
                    if j == 0:
                        dve.wait_ge(bo_added, a + 1)
                    dve.wait_ge(ao_full, TJ * a + j + 1)
                    nc.vector.tensor_tensor(xr[:, other, j], ao[:, 0:D], xr[:, other, j], ALU.add).then_inc(ao_free, 1)

                def convolve(blocks, base):
                    for k in range(KC):
                        for i, m in enumerate(blocks):
                            src = xp[:, m, k:k + T]
                            if k == 0:
                                dve.wait_ge(mm_free, mm_x(f) + m + 3)
                                op = nc.vector.tensor_scalar(cv[:, m], src, W.taps[:, m, 0:1], None, ALU.mult)
                            else:
                                dve.wait_ge(conv, CONV * f + base + len(blocks) * (k - 1) + i + 1)
                                op = nc.vector.scalar_tensor_tensor(
                                    out=cv[:, m], in0=src, scalar=W.taps[:, m, k:k + 1], in1=cv[:, m],
                                    op0=ALU.mult, op1=ALU.add)
                            op.then_inc(conv, 1)

                def state(n):
                    if scan:
                        scan_state(c, n, starts)

                if at(c, -1):
                    dve.wait_ge(W.arrived, 16 * W.LOADS)
                if conv_part:
                    wait(dve, halo, f)
                    if starts:
                        nc.vector.tensor_copy(xp[:, :, 0:KC - 1], halo_cols[:]).then_inc(conv, 1)
                    else:
                        nc.vector.memset(xp[:, :, 0:KC - 1], 0.0).then_inc(conv, 1)
                    dve.wait_ge(conv, CONV * f + 1)
                    wait(dve, delta_ready, f)
                    convolve((0, 1), 1)
                less_max(0)
                if conv_part:
                    convolve((2, 3), 1 + 2 * KC)
                    nc.vector.tensor_copy(halo_cols[:], xp[:, :, T:T + KC - 1]).then_inc(halo, 1)
                row_sums(0)
                state(2)
                less_max(1)
                state(3)
                row_sums(1)
                residual(0)
                if proj:
                    dve.wait_ge(xa_in, 16 * g + 16)
                    wait(dve, norm1.done, TJ * g)
                    statistics(norm1, g, xa)
                state(4)
                less_max(2)
                if proj:
                    refine(norm1, g)
                state(5)
                row_sums(2)
                less_max(3)
                state(6)
                residual(1)
                row_sums(3)
                state(7)
                if conv_part:
                    dve.wait_ge(softplus_act, SOFTPLUS * (f + 1))
                    dve.wait_ge(mm_free, mm_dt(f) + MB + 2)
                    nc.vector.tensor_tensor(delta[:, other], delta[:, other], cv, ALU.add).then_inc(delta_ready, 1)
                residual(2)
                if scan:
                    dve.wait_ge(yg_added, YG * (c + 1))
                    dve.wait_ge(yd_added, YD * (c + 1))
                    nc.vector.tensor_tensor(y_d, y_d, y_g, ALU.add).then_inc(y_sum, 1)
                    dve.wait_ge(y_sum, c + 1)
                    dve.wait_ge(zg_ready, c + 1)
                    nc.vector.tensor_tensor(y_d, y_d, zg, ALU.mult).then_inc(y_ready, 1)
                residual(3)
                if att:
                    dve.wait_ge(ao_free, TJ * a + TJ + 1)
                    statistics(norm3, a, xr[:, other])
                    refine(norm3, a)
                if conv_part:
                    scan_state(f, 0, not starts)
                if scan:
                    dve.wait_ge(xr_in[par], 16 * half + 16)
                    for i in range(2):
                        two = xr[:, par, 2 * i:2 * i + 2]
                        dve.wait_ge(out_full, 2 * c + i + 1)
                        op = nc.vector.tensor_tensor(two, pair_a[:, 512 * i:512 * (i + 1)].rearrange(
                            "p (j d) -> p j d", d=D), two, ALU.add)
                        op.then_inc(sc_free if i else x1_added, 1)
                    dve.wait_ge(x1_added, c + 1)
                    dve.wait_ge(sc_free, pa_out(c) + 2)
                    statistics(norm2, c, xr[:, par])
                    refine(norm2, c)
                if att:
                    dve.wait_ge(tb_full, tb_ln3(a, KD) + 1)
                    nc.vector.tensor_tensor(scores_all[:, bass.ds(TJ * a, TJ), :],
                                            tb[:, 0:TJ * E].rearrange("p (j e) -> p j e", e=E),
                                            W.br[:, None, :].broadcast_to([P, TJ, E]),
                                            ALU.add).then_inc(tb_free, 1)
                if conv_part:
                    scan_state(f, 1, not starts)

            schedule(dve, step)

        @block.tensor
        def _(pe):
            pe.wait_ge(ident_ready, 1)
            pe.wait_ge(W.first_arrived, 16)

            def turn_context():
                pe.wait_ge(ctx_arrived, 16)
                for k in range(KD):
                    for t in range(BM // P):
                        last = nc.tensor.transpose(pair_a[:, k * 512 + t * P:k * 512 + (t + 1) * P],
                                                   ctx_sb[:, t, k * P:(k + 1) * P], ident[:])
                    last.then_inc(gu_full, 1)

            def make_gu(pair):
                s = pair % 2
                wq, wk, wv = (pair_w[:, s, w].rearrange("p (k n) -> p k n", k=KD) for w in range(3))
                pe.wait_ge(pair_w_in[s], 64 * (pair // 2 + 1))
                pe.wait_ge(gu_free, gu_use(pair))
                for k in range(KD):
                    last = nc.tensor.transpose(pair_b[:, k * P:(k + 1) * P], wq[:, k], ident[:])
                last.then_inc(gu_full, 1)
                for w, weight in enumerate((wk, wv)):
                    for k in range(KD):
                        last = nc.tensor.matmul(kv_bank[w], weight[:, k], ctxT[:, k],
                                                start=(k == 0), stop=(k == KD - 1))
                    last.then_inc(gu_full, 1)
                pe.wait_ge(gu_free, gu_use(pair, 2))
                for b in range(B):
                    for k in range(KD):
                        last = nc.tensor.matmul(pair_a[:, (b * KD + k) * P:(b * KD + k + 1) * P],
                                                wqT[:, s, k * P:(k + 1) * P], diag[:, s, 0, b], start=True, stop=True)
                last.then_inc(gu_full, 1)
                pe.wait_ge(gu_free, gu_use(pair, 3))
                for b in range(B):
                    last = nc.tensor.matmul(pair_b[:, b * D:(b + 1) * D], diag[:, s, 1, b], pair_w[:, s, 3],
                                            start=True, stop=True)
                last.then_inc(gu_full, 1)

            def step(c, half, starts, scan, att, conv_part, proj):
                a, f, g, par, other = c - 1, c + 1, c + 2, 0 if starts else 1, 1 if starts else 0

                def mm_take(first, m):
                    pe.wait_ge(mm_free, first + m + 1)
                    return mm[m % 2]

                def ln2_turn(a, j):
                    pe.wait_ge(norm2.done, TJ * a + j + 1)
                    pe.wait_ge(tb_free, tb_ln2(a, j) + 1)
                    for k in range(KD):
                        last = nc.tensor.transpose(tb[:, k * P:(k + 1) * P], xn2[:, j, k * P:(k + 1) * P], ident[:])
                    last.then_inc(tb_full, 1)

                def scores(a, j):
                    pe.wait_ge(tb_free, tb_ln2(a, j) + 2)
                    pe.wait_ge(sc_free, pa_scores(a, j) + 1)
                    for half_n in range(2):
                        for k in range(KD):
                            last = nc.tensor.matmul(pair_a[:, half_n * 512:(half_n + 1) * 512],
                                                    xn2T[:, j % 2, k], g_sb[:, k, half_n * 512:(half_n + 1) * 512],
                                                    start=(k == 0), stop=(k == KD - 1))
                    last.then_inc(sc_full, 1)

                def x_in(blocks):
                    if 0 in blocks:
                        pe.wait_ge(mm_free, mm_tr(g) + KD + 2)
                    for m in blocks:
                        dst = mm_take(mm_x(g), m)
                        for k in range(KD):
                            last = nc.tensor.matmul(dst[:], W.w_in[:, k, m * P:(m + 1) * P], xnT[:, par, k],
                                                    start=(k == 0), stop=(k == KD - 1))
                        last.then_inc(mm_full, 1)

                def z_in(blocks):
                    for m in blocks:
                        dst = mm_take(mm_z(f), m)
                        for k in range(KD):
                            last = nc.tensor.matmul(dst[:], W.w_in[:, k, DI + m * P:DI + (m + 1) * P],
                                                    xnT[:, other, k], start=(k == 0), stop=(k == KD - 1))
                        last.then_inc(mm_full, 1)

                def turn_probs(j):
                    if not att:
                        return
                    pe.wait_ge(probs_ready, TJ * a + j + 1)
                    pe.wait_ge(et_free, TJ * a + j + 1)
                    for hc in range(HC):
                        last = nc.tensor.transpose(pair_b[:, hc * P:(hc + 1) * P],
                                                   probs[:, j % 2, hc * P:(hc + 1) * P], ident[:])
                    last.then_inc(et_full, 1)

                def attend(j):
                    if not att:
                        return
                    pe.wait_ge(et_free, TJ * a + j + 2)
                    pe.wait_ge(ao_free, TJ * a + j + 1)
                    for hc in range(HC):
                        last = nc.tensor.matmul(ao[:, 0:D], probsT[:, hc], u_sb[:, hc],
                                                start=(hc == 0), stop=(hc == HC - 1))
                    last.then_inc(ao_full, 1)

                if att:
                    ln2_turn(a, 1)
                    scores(a, 1)
                    if not starts:
                        pe.wait_ge(u_in, 16 * half + 16)
                turn_probs(0)
                if att:
                    ln2_turn(a, 2)
                attend(0)
                if conv_part:
                    if at(c, -1):
                        pe.wait_ge(W.arrived, 16 * W.LOADS)
                        turn_context()
                        make_gu(0)
                    if at(c, 0):
                        make_gu(2)
                        make_gu(3)
                    pe.wait_ge(conv, CONV * (f + 1))
                for m in range(MB):
                    if att and m == 2:
                        scores(a, 2)
                        turn_probs(1)
                        ln2_turn(a, 3)
                    if conv_part:
                        dst = mm_take(mm_pw(f), m)
                        for k in range(MB):
                            last = nc.tensor.matmul(dst[:], W.pw[:, k, m * P:(m + 1) * P], cv[:, k],
                                                    start=(k == 0), stop=(k == MB - 1))
                        last.then_inc(mm_full, 1)
                attend(1)
                if conv_part:
                    pe.wait_ge(xc_ready, f + 1)
                    pe.wait_ge(tb_free, tb_bc(f) + 1)
                    for k in range(MB):
                        last = nc.tensor.matmul(tb[0:R + 2 * NS, :], W.w_x[:, k], xc[:, k],
                                                start=(k == 0), stop=(k == MB - 1))
                    last.then_inc(tb_full, 1)
                if att:
                    scores(a, 3)
                if conv_part:
                    pe.wait_ge(tb_free, tb_bc(f) + 2)
                    for m in range(MB):
                        nc.tensor.matmul(mm_take(mm_dt(f), m)[:], W.w_dt[:, m * P:(m + 1) * P], xd[0:R, :],
                                         start=True, stop=True).then_inc(mm_full, 1)
                if at(c, -1) or at(c, 0):
                    for pair in ((1,) if at(c, -1) else (4, 5)):
                        make_gu(pair)
                if proj:
                    pe.wait_ge(norm1.done, TJ * g + TJ)
                    for k in range(KD):
                        dst = mm_take(mm_tr(g), k)
                        for j in range(TJ):
                            last = nc.tensor.transpose(dst[:, j * P:(j + 1) * P], xa[:, j, k * P:(k + 1) * P],
                                                       ident[:])
                        last.then_inc(mm_full, 1)
                turn_probs(2)
                if proj:
                    x_in((0, 1))
                attend(2)
                turn_probs(3)
                if proj:
                    x_in((2, 3))
                if at(c, 0):
                    make_gu(6)
                    make_gu(7)
                    pe.wait_ge(gu_free, gu_use(HC))
                attend(3)
                if scan:
                    pe.wait_ge(y_ready, c + 1)
                    pe.wait_ge(sc_free, pa_out(c) + 1)
                    for j in range(TJ):
                        for k in range(MB):
                            last = nc.tensor.matmul(pair_a[:, j * D:(j + 1) * D], y_d[:, k, j * P:(j + 1) * P],
                                                    W.w_out[:, k], start=(k == 0), stop=(k == MB - 1))
                        if j % 2:
                            last.then_inc(out_full, 1)
                if conv_part:
                    z_in((0,))
                if att:
                    pe.wait_ge(norm3.done, TJ * a + 3 * TJ)
                    for k in range(KD):
                        pe.wait_ge(tb_free, tb_ln3(a, k) + 1)
                        for j in range(TJ):
                            last = nc.tensor.transpose(tb[:, j * P:(j + 1) * P], xn3[:, j, k * P:(k + 1) * P],
                                                       ident[:])
                        last.then_inc(tb_full, 1)
                    pe.wait_ge(tb_free, tb_ln3(a, KD) + 1)
                    for j in range(TJ):
                        for k in range(KD):
                            last = nc.tensor.matmul(tb[:, j * E:(j + 1) * E], xn3T[:, k, j * P:(j + 1) * P],
                                                    W.wr[:, k], start=(k == 0), stop=(k == KD - 1))
                    last.then_inc(tb_full, 1)
                if scan:
                    ln2_turn(c, 0)
                if conv_part:
                    z_in((1,))
                if scan:
                    if starts:
                        pe.wait_ge(g_in, 16 * half + 16)
                    scores(c, 0)
                if conv_part:
                    z_in((2, 3))

            schedule(pe, step)


def expert_part(nc, sem, sb_in, passed, ident, scores_all, bank, pair_a, pair_b, w1_sb, w2_sb, w1_in, w2_in,
                b1, b2, x2_dram, xn3_dram, out_rows):
    x2_rows = x2_dram.rearrange("p t d -> (p t) d")
    xn3_rows = xn3_dram.rearrange("p t d -> (p t) d")
    with ExitStack() as st:
        def sb(name, shape, dt=F32):
            return sb_in(st, name, shape, dt)

        tile_expert = sb("tile_expert", [P, NT], I32)
        get_row = sb("get_row", [P, NT], U32)
        put_row = sb("put_row", [P, NT], U32)
        b1_sb = sb("b1_sb", [P, E, KF])
        b2_sb = sb("b2_sb", [P, E, D])
        bias_in = sem("bias_in")
        consts, const_steps, route = sem("route_consts"), sem("const_steps"), sem("route_steps")
        counts_ready, cols_ready, rows_ready = sem("counts_ready"), sem("cols_ready"), sem("rows_ready")

        with ExitStack() as rt:
            def rb(name, shape, dt=F32):
                return sb_in(rt, name, shape, dt)

            e_less = rb("e_less", [P, TT, E])
            tri = rb("tri", [P, P])
            ones = rb("ones", [P, P])
            k128 = rb("k128", [P, E, TT])
            tile_no = rb("tile_no", [P, NT, E])
            edges = rb("edges", [P, NT + 1])
            col_no = rb("col_no", [P, P])
            part_no = rb("part_no", [P, 1])
            tt_no = rb("tt_no", [P, TT])
            best = rb("best", [P, TT])
            is_best = rb("is_best", [P, TT, E])
            pick = rb("pick", [P, TT, E])
            first = rb("first", [P, TT])
            onehot = rb("onehot", [P, TT, E])
            within = rb("within", [P, TT, E])
            total = rb("total", [P, E, TT])
            upto = rb("upto", [P, E, TT])
            more = rb("more", [P, E, TT])
            tiles = rb("tiles", [P, E])
            tiles_end = rb("tiles_end", [P, E])
            base = rb("base", [P, E])
            offs = rb("offs", [P, TT, E])
            slot = rb("slot", [P, TT])
            past = rb("past", [P, NT, E])
            expert_f = rb("expert_f", [P, NT])
            expert_c = rb("expert_c", [P, NT])
            reached = rb("reached", [P, TT, NT + 1])
            tiles_to = rb("tiles_to", [P, TT])
            start = rb("start", [P, TT])
            place = rb("place", [P, TT])
            at_place = rb("at_place", [P, TT, P], BF16)
            at_tile = rb("at_tile", [P, TT, 3, NT], BF16)
            found = rb("found", [P, 3, NT])
            get_f = rb("get_f", [P, NT])
            put_f = rb("put_f", [P, NT])
            skip_f = rb("skip_f", [P, NT])

            STEPS_TILE = 19 + E

            with nc.Block() as block:
                @block.sync
                def _(sp):
                    sp.dma_start(b1_sb[:], b1.rearrange("e (k p) -> p e k", p=P),
                                 allow_slow_non_contiguous=True).then_inc(bias_in, 16)
                    sp.dma_start(b2_sb[:], b2.partition_broadcast(P)).then_inc(bias_in, 16)
                    sp.wait_ge(bias_in, 32)

                @block.gpsimd
                def _(pool):
                    kw = dict(allow_small_or_imprecise_dtypes=True)
                    nc.gpsimd.iota(e_less[:], [[0, TT], [1, E]], base=-E, channel_multiplier=0, **kw).then_inc(consts, 1)
                    nc.gpsimd.memset(ones[:], 1.0).then_inc(consts, 1)
                    nc.gpsimd.memset(tri[:], 1.0).then_inc(const_steps, 1)
                    pool.wait_ge(const_steps, 1)
                    nc.gpsimd.affine_select(out=tri[:], in_=tri[:], compare_op=ALU.is_gt, fill=0.0, base=0,
                                            pattern=[[1, P]], channel_multiplier=-1).then_inc(consts, 1)
                    nc.gpsimd.iota(k128[:], [[0, E], [P, TT]], base=0, channel_multiplier=0, **kw).then_inc(consts, 1)
                    nc.gpsimd.iota(tile_no[:], [[1, NT], [0, E]], base=0, channel_multiplier=0, **kw).then_inc(consts, 1)
                    nc.gpsimd.iota(edges[:], [[P, NT + 1]], base=0, channel_multiplier=0, **kw).then_inc(consts, 1)
                    nc.gpsimd.iota(col_no[:], [[1, P]], base=0, channel_multiplier=0, **kw).then_inc(consts, 1)
                    nc.gpsimd.iota(part_no[:], [[0, 1]], base=0, channel_multiplier=1, **kw).then_inc(consts, 1)
                    nc.gpsimd.iota(tt_no[:], [[1, TT]], base=0, channel_multiplier=0, **kw).then_inc(consts, 1)
                    pool.wait_ge(consts, 9)
                    pool.wait_ge(route, STEPS_TILE)
                    nc.gpsimd.tensor_tensor(at_tile[:, :, 1], at_tile[:, :, 0],
                                            part_no[:, :, None].broadcast_to([P, TT, NT]), ALU.mult).then_inc(cols_ready, 1)
                    nc.gpsimd.tensor_tensor(at_tile[:, :, 2], at_tile[:, :, 0],
                                            tt_no[:, :, None].broadcast_to([P, TT, NT]), ALU.mult).then_inc(cols_ready, 1)

                @block.vector
                def _(dve):
                    count = [0]

                    def then(op):
                        op.then_inc(route, 1)
                        count[0] += 1
                        dve.wait_ge(route, count[0])

                    V = nc.vector
                    dve.wait_ge(consts, 9)
                    then(V.tensor_reduce(best[:], scores_all[:], AX.X, ALU.max))
                    then(V.tensor_tensor(is_best[:], scores_all[:], best[:, :, None].broadcast_to([P, TT, E]), ALU.is_ge))
                    then(V.tensor_tensor(pick[:], is_best[:], e_less[:], ALU.mult))
                    then(V.tensor_reduce(first[:], pick[:], AX.X, ALU.min))
                    then(V.tensor_tensor(onehot[:], e_less[:], first[:, :, None].broadcast_to([P, TT, E]), ALU.is_equal))
                    dve.wait_ge(counts_ready, 2)
                    then(V.tensor_copy(within[:], bank[0][:, 0:TT * E].rearrange("p (t e) -> p t e", e=E)))
                    then(V.tensor_copy(total[:].rearrange("p e t -> p t e"),
                                       bank[1][:, 0:TT * E].rearrange("p (t e) -> p t e", e=E)))
                    for e in range(E):
                        then(V.tensor_tensor_scan(upto[:, e], ones[:, 0:TT], total[:, e], 0.0, ALU.mult, ALU.add))
                    then(V.tensor_tensor(more[:], upto[:, :, TT - 1:TT].broadcast_to([P, E, TT]), k128[:], ALU.is_gt))
                    then(V.tensor_reduce(tiles[:], more[:], AX.X, ALU.add))
                    then(V.tensor_tensor_scan(tiles_end[:], ones[:, 0:E], tiles[:], 0.0, ALU.mult, ALU.add))
                    then(V.tensor_tensor(base[:], tiles_end[:], tiles[:], ALU.subtract))
                    then(V.tensor_scalar(base[:], base[:], float(P), None, ALU.mult))
                    then(V.tensor_tensor(upto[:], upto[:], total[:], ALU.subtract))
                    then(V.tensor_tensor(offs[:], upto[:].rearrange("p e t -> p t e"), within[:], ALU.add))
                    then(V.tensor_tensor(offs[:], offs[:], base[:, None, :].broadcast_to([P, TT, E]), ALU.add))
                    then(V.tensor_tensor(offs[:], offs[:], onehot[:], ALU.mult))
                    then(V.tensor_reduce(slot[:], offs[:], AX.X, ALU.add))
                    then(V.tensor_tensor(reached[:], slot[:, :, None].broadcast_to([P, TT, NT + 1]),
                                         edges[:, None, :].broadcast_to([P, TT, NT + 1]), ALU.is_ge))
                    then(V.tensor_tensor(at_tile[:, :, 0], reached[:, :, 0:NT], reached[:, :, 1:NT + 1], ALU.subtract))
                    then(V.tensor_reduce(tiles_to[:], reached[:], AX.X, ALU.add))
                    then(V.tensor_scalar(start[:], tiles_to[:], -float(P), float(P), ALU.mult, ALU.add))
                    then(V.tensor_tensor(place[:], slot[:], start[:], ALU.add))
                    for t in range(0, TT, TT // 4):
                        q = slice(t, t + TT // 4)
                        V.tensor_tensor(at_place[:, q], place[:, q, None].broadcast_to([P, TT // 4, P]),
                                        col_no[:, None, :].broadcast_to([P, TT // 4, P]),
                                        ALU.is_equal).then_inc(rows_ready, 1)
                    then(V.tensor_tensor(past[:], tile_no[:], tiles_end[:, None, :].broadcast_to([P, NT, E]), ALU.is_ge))
                    then(V.tensor_reduce(expert_f[:], past[:], AX.X, ALU.add))
                    then(V.tensor_scalar(expert_c[:], expert_f[:], float(E - 1), None, ALU.min))
                    then(V.tensor_copy(tile_expert[:], expert_c[:]))
                    dve.wait_ge(counts_ready, 3)
                    then(V.tensor_copy(found[:], bank[0][:, 0:3 * NT].rearrange("p (k n) -> p k n", k=3)))
                    then(V.scalar_tensor_tensor(out=get_f[:], in0=found[:, 1], scalar=float(TT), in1=found[:, 2],
                                                op0=ALU.mult, op1=ALU.add))
                    then(V.tensor_copy(get_row[:], get_f[:]))
                    then(V.scalar_tensor_tensor(out=put_f[:], in0=found[:, 2], scalar=float(P), in1=found[:, 1],
                                                op0=ALU.mult, op1=ALU.add))
                    then(V.tensor_scalar(skip_f[:], found[:, 0], -float(2 * TT * P), float(2 * TT * P), ALU.mult, ALU.add))
                    then(V.tensor_tensor(put_f[:], put_f[:], skip_f[:], ALU.add))
                    then(V.tensor_copy(put_row[:], put_f[:]))

                @block.tensor
                def _(pe):
                    pe.wait_ge(route, 5)
                    oh = onehot[:].rearrange("p t e -> p (t e)")
                    nc.tensor.matmul(bank[0][:, 0:TT * E], tri[:], oh, start=True, stop=True).then_inc(counts_ready, 1)
                    nc.tensor.matmul(bank[1][:, 0:TT * E], ones[:], oh, start=True, stop=True).then_inc(counts_ready, 1)
                    pe.wait_ge(cols_ready, 2)
                    for t in range(TT):
                        if t % (TT // 4) == 0:
                            pe.wait_ge(rows_ready, t // (TT // 4) + 1)
                        last = nc.tensor.matmul(bank[0][:, 0:3 * NT], at_place[:, t],
                                                at_tile[:, t].rearrange("p k n -> p (k n)"),
                                                start=(t == 0), stop=(t == TT - 1))
                    last.then_inc(counts_ready, 1)

        with ExitStack() as ft:
            def fb(name, shape, dt=F32):
                return sb_in(ft, name, shape, dt)

            xs = fb("xs", [P, 2, D])
            xsT = fb("xsT", [P, 2, KD, P])
            hid = fb("hid", [P, 2, F])
            hidT = fb("hidT", [P, 2, KF, P])
            x2s = fb("x2s", [P, 2, D])
            ys = fb("ys", [P, 2, D])
            x_now, x2_now, put_now = (fb(n, [P, 2, 1], U32) for n in ("x_now", "x2_now", "put_now"))

            xs_in = [sem("xs_in0"), sem("xs_in1")]
            x2s_in = [sem("x2s_in0"), sem("x2s_in1")]
            x_turned, xsT_ready = sem("x_turned"), sem("xsT_ready")
            up_full, up_free = sem("up_full"), sem("up_free")
            hid_turned, act_done = sem("hid_turned"), sem("act_done")
            down_full, down_free, y_done = sem("down_full"), sem("down_free"), sem("y_done")
            x_copied, x2_copied, put_copied = sem("x_copied"), sem("x2_copied"), sem("put_copied")
            out_stored = [sem("out_stored0"), sem("out_stored1")]
            x_bank, y_bank = bank[0], bank[1]

            def tiles_loop(eng, step):
                step(0, 0, 0, True)
                step(1, 0, 1, True)
                with eng.Fori(1, (NT - 3) // 2) as k:
                    step(2 * k, k, 0, True)
                    step(2 * k + 1, k, 1, True)
                k = (NT - 3) // 2
                step(NT - 3, k, 0, True)
                step(NT - 2, k, 1, False)

            with nc.Block() as block:
                @block.gpsimd
                def _(pool):
                    pool.sem_inc(y_done, 1)

                    def indices(table, i, now, p, copied, count):
                        nc.gpsimd.tensor_copy(now[:, p], table[:, bass.ds(i, 1)]).then_inc(copied, 1)
                        wait_apart(pool, copied, count, passed[1])

                    def get_x(i, p):
                        indices(get_row, i, x_now, p, x_copied, i + 1)
                        nc.gpsimd.indirect_dma_start(
                            xs[:, p], None, xn3_rows,
                            bass.IndirectOffsetOnAxis(ap=x_now[:, p], axis=0)).then_inc(xs_in[p], 16)

                    def get_x2(i, p):
                        indices(get_row, i, x2_now, p, x2_copied, i + 1)
                        nc.gpsimd.indirect_dma_start(
                            x2s[:, p], None, x2_rows,
                            bass.IndirectOffsetOnAxis(ap=x2_now[:, p], axis=0)).then_inc(x2s_in[p], 16)

                    def put(i, k, p):
                        wait_apart(pool, out_stored[p], 16 * k, passed[1])
                        indices(put_row, i, put_now, p, put_copied, i + 1)
                        wait_apart(pool, y_done, i + 2, passed[1])
                        nc.gpsimd.indirect_dma_start(
                            out_rows, bass.IndirectOffsetOnAxis(ap=put_now[:, p], axis=0),
                            ys[:, p], None, bounds_check=B * S - 1, oob_is_err=False).then_inc(out_stored[p], 16)

                    get_x(0, 0)
                    get_x(1, 1)
                    get_x2(0, 0)
                    pool.wait_ge(x_turned, 1)
                    get_x(2, 0)

                    def step(i, k, p, more):
                        if more and not (isinstance(i, int) and i == NT - 3):
                            wait_apart(pool, x_turned, i + 2, passed[1])
                            get_x(i + 3, 1 - p)
                        wait_apart(pool, y_done, i + 1, passed[1])
                        get_x2(i + 1, 1 - p)
                        put(i, k, p)

                    tiles_loop(pool, step)
                    put(NT - 1, (NT - 1) // 2, 0)
                    pool.wait_ge(out_stored[0], 16 * (NT // 2 + 1))
                    pool.wait_ge(out_stored[1], 16 * (NT // 2))

                @block.tensor
                def _(pe):
                    def turn_x(i, k, p):
                        pe.wait_ge(xs_in[p], 16 * k + 16)
                        wait(pe, xsT_ready, i)
                        for c in range(KD):
                            last = nc.tensor.transpose(x_bank[:, c * P:(c + 1) * P], xs[:, p, c * P:(c + 1) * P], ident[:])
                        last.then_inc(x_turned, 1)

                    def up(i, p):
                        e = pe.value_load(tile_expert[0:1, bass.ds(i, 1)], min_val=0, max_val=E - 1)
                        pe.wait_ge(xsT_ready, i + 1)
                        wait(pe, up_free, i)
                        for half in range(F // 512):
                            for c in range(KD):
                                last = nc.tensor.matmul(
                                    pair_a[:, half * 512:(half + 1) * 512], xsT[:, p, c],
                                    w1_sb[:, bass.ds(e, 1), c, half * 512:(half + 1) * 512].rearrange("p o f -> p (o f)"),
                                    start=(c == 0), stop=(c == KD - 1))
                        last.then_inc(up_full, 1)

                    def turn_hidden(i, p):
                        pe.wait_ge(up_free, i + 1)
                        wait(pe, act_done, KF * i)
                        for c in range(KF):
                            last = nc.tensor.transpose(pair_b[:, c * P:(c + 1) * P], hid[:, p, c * P:(c + 1) * P], ident[:])
                        last.then_inc(hid_turned, 1)

                    def down(i, p):
                        e = pe.value_load(tile_expert[0:1, bass.ds(i, 1)], min_val=0, max_val=E - 1)
                        pe.wait_ge(act_done, KF * i + KF)
                        wait(pe, down_free, i)
                        for c in range(KF):
                            last = nc.tensor.matmul(y_bank[:, 0:D], hidT[:, p, c],
                                                    w2_sb[:, bass.ds(e, 1), c, :].rearrange("p o d -> p (o d)"),
                                                    start=(c == 0), stop=(c == KF - 1))
                        last.then_inc(down_full, 1)

                    turn_x(0, 0, 0)
                    turn_x(1, 0, 1)
                    pe.wait_ge(w1_in, 16 * E)
                    up(0, 0)
                    turn_hidden(0, 0)
                    pe.wait_ge(w2_in, 16 * E)

                    def step(i, k, p, more):
                        up(i + 1, 1 - p)
                        if more:
                            turn_x(i + 2, k + 1, p)
                        down(i, p)
                        turn_hidden(i + 1, 1 - p)

                    tiles_loop(pe, step)
                    down(NT - 1, 0)

                @block.vector
                def _(dve):
                    dve.wait_ge(bias_in, 32)

                    def x_out(i, p):
                        dve.wait_ge(x_turned, i + 1)
                        if not (isinstance(i, int) and i < 2):
                            dve.wait_ge(up_full, i - 1)
                        nc.vector.tensor_copy(xsT[:, p].rearrange("p c t -> p (c t)"),
                                              x_bank[:, 0:KD * P]).then_inc(xsT_ready, 1)

                    def hid_out(i, p):
                        dve.wait_ge(up_full, i + 1)
                        nc.vector.tensor_copy(hid[:, p], pair_a[:]).then_inc(up_free, 1)

                    def y_out(i, k, p):
                        e = dve.value_load(tile_expert[0:1, bass.ds(i, 1)], min_val=0, max_val=E - 1)
                        dve.wait_ge(down_full, i + 1)
                        wait(dve, out_stored[p], 16 * k)
                        nc.vector.tensor_tensor(ys[:, p], y_bank[:, 0:D],
                                                b2_sb[:, bass.ds(e, 1), :].rearrange("p o d -> p (o d)"),
                                                ALU.add).then_inc(down_free, 1)
                        dve.wait_ge(down_free, i + 1)
                        dve.wait_ge(x2s_in[p], 16 * k + 16)
                        nc.vector.tensor_tensor(ys[:, p], ys[:, p], x2s[:, p], ALU.add).then_inc(y_done, 1)

                    x_out(0, 0)
                    x_out(1, 1)
                    hid_out(0, 0)

                    def step(i, k, p, more):
                        hid_out(i + 1, 1 - p)
                        if more:
                            x_out(i + 2, p)
                        y_out(i, k, p)

                    tiles_loop(dve, step)
                    y_out(NT - 1, (NT - 1) // 2, 0)

                @block.scalar
                def _(act):
                    act.wait_ge(bias_in, 32)

                    def gelu(i, p):
                        e = act.value_load(tile_expert[0:1, bass.ds(i, 1)], min_val=0, max_val=E - 1)
                        act.wait_ge(hid_turned, i + 1)
                        for c in range(KF):
                            nc.scalar.activation(hidT[:, p, c], pair_b[:, c * P:(c + 1) * P], ACT.Gelu,
                                                 bias=b1_sb[:, bass.ds(e, 1), c]).then_inc(act_done, 1)

                    gelu(0, 0)

                    def step(i, k, p, more):
                        gelu(i + 1, 1 - p)

                    tiles_loop(act, step)


_INS = ["x", "ctx_1024", "L0_attn_W_in", "L0_attn_dw_kernel", "L0_attn_pw_kernel", "L0_attn_conv_bias",
        "L0_attn_W_x", "L0_attn_W_dt", "L0_attn_b_dt", "L0_attn_A_log", "L0_attn_D", "L0_attn_W_out",
        "L0_xattn_Wq", "L0_xattn_Wk", "L0_xattn_Wv", "L0_xattn_Wo", "L0_xattn_bo",
        "L0_ffn_wr", "L0_ffn_br", "L0_ffn_w1", "L0_ffn_b1", "L0_ffn_w2", "L0_ffn_b2"]


def kernel(**inputs):
    import numpy as _np
    import concourse.bacc as _bacc
    from concourse import mybir as _mybir
    from concourse.bass_utils import run_bass_kernel_spmd as _run

    nc = _bacc.Bacc("TRN2", target_bir_lowering=False, num_devices=1)
    arrays, args = {}, []
    for name in _INS:
        a = _np.ascontiguousarray(inputs[name])
        arrays[f"in_{name}"] = a
        args.append(nc.dram_tensor(f"in_{name}", a.shape, _mybir.dt.from_np(a.dtype), kind="ExternalInput").ap())
    out = nc.dram_tensor("out_0", (B, S, D), _mybir.dt.float32, kind="ExternalOutput").ap()
    decoder_layer(nc, *args, out)
    r = _run(nc, [arrays], core_ids=[0])
    return r.results[0]["out_0"]
```
